# Optimizing a Trainium2 kernel written in Bass

```python
import numpy as np
import jax
import jax.numpy as jnp

def _softmax(x, axis=-1):
    return jax.nn.softmax(x, axis=axis)

def _gelu(x):
    return jax.nn.gelu(x, approximate=True)

def _silu(x):
    return jax.nn.silu(x)

def _sigmoid(x):
    return jax.nn.sigmoid(x)

def _layernorm(x, axis=-1, eps=1e-05):
    m = jnp.mean(x, axis=axis, keepdims=True)
    v = jnp.var(x, axis=axis, keepdims=True)
    return (x - m) / jnp.sqrt(v + eps)

def _scatter_add(tgt, idx, src, axis=0):
    return tgt.at[idx].add(src)

def _segment_sum(src, seg, n):
    return jax.ops.segment_sum(src, seg, n)
kernel_name = 'mk_early_fusion_d1_tok_img768_r4_259458'

def setup_inputs(seed: int=0):
    np.random.seed(seed)
    _w = jnp.asarray

    def _rec_inputs():
        import jax
        import jax.numpy as jnp
        _rk = jax.random.key(seed)
        x = 7.57192e-06 + 1.00007 * jax.random.normal(jax.random.fold_in(_rk, 1), (8, 3, 224, 224), jnp.float32)
        txt = 0.00277252 + 1.14258 * jax.random.normal(jax.random.fold_in(_rk, 2), (8, 128, 192), jnp.float32)
        return (x, txt)
    x, txt = _rec_inputs()

    def _L0_tok_setup():
        import jax, jax.numpy as jnp
        import numpy as np
        from jax import lax
        P = 16
        S = 8
        key = jax.random.key(seed)
        k1, k2, k3, k4, k5 = jax.random.split(key, 5)
        B, C, H, W = (64, 3, 224, 224)
        D = 192
        patch_dim = C * P * P
        out = (H - P) // S + 1
        n_tok = out * out + 1
        return {'x': jax.random.normal(k1, (B, C, H, W), dtype=jnp.float32), 'w': jax.random.normal(k2, (D, patch_dim), dtype=jnp.float32) * 0.02, 'b': jax.random.normal(k3, (D,), dtype=jnp.float32) * 0.02, 'cls_token': jax.random.normal(k4, (1, 1, D), dtype=jnp.float32), 'pos_embedding': jax.random.normal(k5, (1, n_tok, D), dtype=jnp.float32)}
    _L0_tok_all = _L0_tok_setup()
    _L0_tok_in = {k: v for k, v in _L0_tok_all.items() if k in ('w', 'b', 'cls_token', 'pos_embedding')}
    del _L0_tok_all

    def _L0_attn_setup():
        import jax, jax.numpy as jnp
        import numpy as np
        B_SZ, L, DIM, H_DIM, D_STATE, K = (2, 512, 192, 384, 16, 4)

        def _forward(x, W1, b1, W2, b2, conv_w, conv_b, Wf, bf, A, WB, bB, WC, bC, WD, bD, Dvec):
            b, l, _ = x.shape
            k = conv_w.shape[-1]
            a = x @ W1 + b1
            g = jax.nn.silu(x @ W2 + b2)
            xc = jnp.swapaxes(a, 1, 2)
            ac = jax.lax.conv_general_dilated(xc, conv_w, window_strides=(1,), padding=[(k - 1, 0)], feature_group_count=xc.shape[1], dimension_numbers=('NCH', 'OIH', 'NCH')) + conv_b[None, :, None]
            a = jax.nn.silu(jnp.swapaxes(ac, 1, 2))
            delta = jax.nn.softplus(Dvec + a @ WD + bD)
            Bm = a @ WB + bB
            A_ = jnp.exp(-A)[None, None] * delta[..., None]
            X_ = Bm[:, :, None, :] * delta[..., None] * a[..., None]
            A_t = jnp.moveaxis(A_, 1, 0)
            X_t = jnp.moveaxis(X_, 1, 0)

            def step(h, AX):
                At, Xt = AX
                h = At * h + Xt
                return (h, h)
            h0 = jnp.zeros(A_t.shape[1:], dtype=x.dtype)
            _, hs = jax.lax.scan(step, h0, (A_t, X_t))
            hid = jnp.moveaxis(hs, 0, 1)
            output = a * g @ Wf + bf
            return (output, hid, a[..., 1:])

        def _reference_tuple_inner(x, W1, b1, W2, b2, conv_w, conv_b, Wf, bf, A, WB, bB, WC, bC, WD, bD, Dvec):
            return _forward(x, W1, b1, W2, b2, conv_w, conv_b, Wf, bf, A, WB, bB, WC, bC, WD, bD, Dvec)
        key = jax.random.key(seed)
        ks = jax.random.split(key, 16)
        sc = 0.02
        inp = {'x': jax.random.normal(ks[0], (B_SZ, L, DIM), dtype=jnp.float32), 'W1': jax.random.normal(ks[1], (DIM, H_DIM), dtype=jnp.float32) * sc, 'b1': jnp.zeros((H_DIM,), dtype=jnp.float32), 'W2': jax.random.normal(ks[2], (DIM, H_DIM), dtype=jnp.float32) * sc, 'b2': jnp.zeros((H_DIM,), dtype=jnp.float32), 'conv_w': jax.random.normal(ks[3], (H_DIM, 1, K), dtype=jnp.float32) * sc, 'conv_b': jnp.zeros((H_DIM,), dtype=jnp.float32), 'Wf': jax.random.normal(ks[4], (H_DIM, DIM), dtype=jnp.float32) * sc, 'bf': jnp.zeros((DIM,), dtype=jnp.float32), 'A': jnp.tile(jnp.arange(1, D_STATE + 1, dtype=jnp.float32), (H_DIM, 1)), 'WB': jax.random.normal(ks[5], (H_DIM, D_STATE), dtype=jnp.float32) * sc, 'bB': jnp.zeros((D_STATE,), dtype=jnp.float32), 'WC': jax.random.normal(ks[6], (H_DIM, D_STATE), dtype=jnp.float32) * sc, 'bC': jnp.zeros((D_STATE,), dtype=jnp.float32), 'WD': jax.random.normal(ks[7], (H_DIM, H_DIM), dtype=jnp.float32) * sc, 'bD': jnp.zeros((H_DIM,), dtype=jnp.float32), 'Dvec': jnp.ones((H_DIM,), dtype=jnp.float32)}
        return inp
    _L0_attn_all = _L0_attn_setup()
    _L0_attn_in = {k: v for k, v in _L0_attn_all.items() if k in ('W1', 'b1', 'W2', 'b2', 'conv_w', 'conv_b', 'Wf', 'bf', 'A', 'WB', 'bB', 'WC', 'bC', 'WD', 'bD', 'Dvec')}
    del _L0_attn_all

    def _L0_ffn_setup():
        import jax, jax.numpy as jnp
        import numpy as np
        B, M, D = (32, 196, 192)
        N, P, H = (64, 1, 768)
        EPS = 1e-12

        def _l2norm(v, axis):
            n = jnp.sqrt(jnp.sum(v * v, axis=axis, keepdims=True))
            return v / jnp.maximum(n, EPS)
        key = jax.random.key(seed)
        ks = jax.random.split(key, 7)
        x = jax.random.normal(ks[0], (B, M, D), dtype=jnp.float32)
        phi = jax.random.normal(ks[1], (D, N, P), dtype=jnp.float32) * (1.0 / D ** 0.5)
        scale = jnp.ones((1,), dtype=jnp.float32)
        w1 = jax.random.normal(ks[2], (N, D, H), dtype=jnp.float32) * (1.0 / D ** 0.5)
        b1 = jnp.zeros((N, H), dtype=jnp.float32)
        w2 = jax.random.normal(ks[3], (N, H, D), dtype=jnp.float32) * (1.0 / H ** 0.5)
        b2 = jnp.zeros((N, D), dtype=jnp.float32)
        return {'x': x, 'phi': phi, 'scale': scale, 'w1': w1, 'b1': b1, 'w2': w2, 'b2': b2}
    _L0_ffn_all = _L0_ffn_setup()
    _L0_ffn_in = {k: v for k, v in _L0_ffn_all.items() if k in ('phi', 'scale', 'w1', 'b1', 'w2', 'b2')}
    del _L0_ffn_all
    return {'x': x, 'txt': txt, 'L0_tok_w': _L0_tok_in['w'], 'L0_tok_b': _L0_tok_in['b'], 'L0_tok_cls_token': _L0_tok_in['cls_token'], 'L0_tok_pos_embedding': _L0_tok_in['pos_embedding'], 'L0_attn_W1': _L0_attn_in['W1'], 'L0_attn_b1': _L0_attn_in['b1'], 'L0_attn_W2': _L0_attn_in['W2'], 'L0_attn_b2': _L0_attn_in['b2'], 'L0_attn_conv_w': _L0_attn_in['conv_w'], 'L0_attn_conv_b': _L0_attn_in['conv_b'], 'L0_attn_Wf': _L0_attn_in['Wf'], 'L0_attn_bf': _L0_attn_in['bf'], 'L0_attn_A': _L0_attn_in['A'], 'L0_attn_WB': _L0_attn_in['WB'], 'L0_attn_bB': _L0_attn_in['bB'], 'L0_attn_WC': _L0_attn_in['WC'], 'L0_attn_bC': _L0_attn_in['bC'], 'L0_attn_WD': _L0_attn_in['WD'], 'L0_attn_bD': _L0_attn_in['bD'], 'L0_attn_Dvec': _L0_attn_in['Dvec'], 'L0_ffn_phi': _L0_ffn_in['phi'], 'L0_ffn_scale': _L0_ffn_in['scale'], 'L0_ffn_w1': _L0_ffn_in['w1'], 'L0_ffn_b1': _L0_ffn_in['b1'], 'L0_ffn_w2': _L0_ffn_in['w2'], 'L0_ffn_b2': _L0_ffn_in['b2']}

def reference(x, txt, L0_tok_w, L0_tok_b, L0_tok_cls_token, L0_tok_pos_embedding, L0_attn_W1, L0_attn_b1, L0_attn_W2, L0_attn_b2, L0_attn_conv_w, L0_attn_conv_b, L0_attn_Wf, L0_attn_bf, L0_attn_A, L0_attn_WB, L0_attn_bB, L0_attn_WC, L0_attn_bC, L0_attn_WD, L0_attn_bD, L0_attn_Dvec, L0_ffn_phi, L0_ffn_scale, L0_ffn_w1, L0_ffn_b1, L0_ffn_w2, L0_ffn_b2):
    import jax
    import jax.numpy as jnp

    def _L0_tok_ref(x, w, b, cls_token, pos_embedding):
        import jax, jax.numpy as jnp
        import numpy as np
        from jax import lax
        P = 16
        S = 8
        B = x.shape[0]
        patches = lax.conv_general_dilated_patches(x, filter_shape=(P, P), window_strides=(S, S), padding='VALID', dimension_numbers=('NCHW', 'OIHW', 'NCHW'))
        pd = patches.shape[1]
        patches = patches.reshape(B, pd, -1).transpose(0, 2, 1)
        tok = jnp.einsum('bnp,dp->bnd', patches, w) + b
        cls = jnp.broadcast_to(cls_token, (B, 1, tok.shape[-1]))
        out = jnp.concatenate([cls, tok], axis=1) + pos_embedding
        return out

    def _L0_attn_ref(x, W1, b1, W2, b2, conv_w, conv_b, Wf, bf, A, WB, bB, WC, bC, WD, bD, Dvec):
        import jax, jax.numpy as jnp
        import numpy as np
        B_SZ, L, DIM, H_DIM, D_STATE, K = (2, 512, 192, 384, 16, 4)

        def _forward(x, W1, b1, W2, b2, conv_w, conv_b, Wf, bf, A, WB, bB, WC, bC, WD, bD, Dvec):
            b, l, _ = x.shape
            k = conv_w.shape[-1]
            a = x @ W1 + b1
            g = jax.nn.silu(x @ W2 + b2)
            xc = jnp.swapaxes(a, 1, 2)
            ac = jax.lax.conv_general_dilated(xc, conv_w, window_strides=(1,), padding=[(k - 1, 0)], feature_group_count=xc.shape[1], dimension_numbers=('NCH', 'OIH', 'NCH')) + conv_b[None, :, None]
            a = jax.nn.silu(jnp.swapaxes(ac, 1, 2))
            delta = jax.nn.softplus(Dvec + a @ WD + bD)
            Bm = a @ WB + bB
            A_ = jnp.exp(-A)[None, None] * delta[..., None]
            X_ = Bm[:, :, None, :] * delta[..., None] * a[..., None]
            A_t = jnp.moveaxis(A_, 1, 0)
            X_t = jnp.moveaxis(X_, 1, 0)

            def step(h, AX):
                At, Xt = AX
                h = At * h + Xt
                return (h, h)
            h0 = jnp.zeros(A_t.shape[1:], dtype=x.dtype)
            _, hs = jax.lax.scan(step, h0, (A_t, X_t))
            hid = jnp.moveaxis(hs, 0, 1)
            output = a * g @ Wf + bf
            return (output, hid, a[..., 1:])

        def _reference_tuple_inner(x, W1, b1, W2, b2, conv_w, conv_b, Wf, bf, A, WB, bB, WC, bC, WD, bD, Dvec):
            return _forward(x, W1, b1, W2, b2, conv_w, conv_b, Wf, bf, A, WB, bB, WC, bC, WD, bD, Dvec)
        return _reference_tuple_inner(x, W1, b1, W2, b2, conv_w, conv_b, Wf, bf, A, WB, bB, WC, bC, WD, bD, Dvec)[0]

    def _L0_ffn_ref(x, phi, scale, w1, b1, w2, b2):
        import jax, jax.numpy as jnp
        import numpy as np
        B, M, D = (32, 196, 192)
        N, P, H = (64, 1, 768)
        EPS = 1e-12

        def _l2norm(v, axis):
            n = jnp.sqrt(jnp.sum(v * v, axis=axis, keepdims=True))
            return v / jnp.maximum(n, EPS)
        xn = _l2norm(x, axis=2)
        phin = scale * _l2norm(phi, axis=0)
        logits = jnp.einsum('bmd,dnp->bmnp', xn, phin)
        d = jax.nn.softmax(logits, axis=1)
        b_, m_, n_, p_ = logits.shape
        c = jax.nn.softmax(logits.reshape(b_, m_, n_ * p_), axis=-1).reshape(b_, m_, n_, p_)
        xs = jnp.einsum('bmd,bmnp->bnpd', xn, d)
        h = jax.nn.gelu(jnp.einsum('bnpd,ndh->bnph', xs, w1) + b1[None, :, None, :], approximate=False)
        ys = jnp.einsum('bnph,nhd->bnpd', h, w2) + b2[None, :, None, :]
        y = jnp.einsum('bnpd,bmnp->bmd', ys, c)
        return y
    h = _L0_tok_ref(x, L0_tok_w, L0_tok_b, L0_tok_cls_token, L0_tok_pos_embedding)
    h = jnp.concatenate([h, txt], axis=1)
    h = h + _L0_attn_ref(_layernorm(h, axis=-1), L0_attn_W1, L0_attn_b1, L0_attn_W2, L0_attn_b2, L0_attn_conv_w, L0_attn_conv_b, L0_attn_Wf, L0_attn_bf, L0_attn_A, L0_attn_WB, L0_attn_bB, L0_attn_WC, L0_attn_bC, L0_attn_WD, L0_attn_bD, L0_attn_Dvec)
    h = h + _L0_ffn_ref(_layernorm(h, axis=-1), L0_ffn_phi, L0_ffn_scale, L0_ffn_w1, L0_ffn_b1, L0_ffn_w2, L0_ffn_b2)
    return h

_drawn_inputs = setup_inputs


def setup_inputs(seed=0):
    import zlib

    import numpy as np

    out = dict(_drawn_inputs(seed))
    spreads = {'L0_attn_b1': (0.0, 0.8),
     'L0_attn_b2': (0.0, 0.8),
     'L0_attn_conv_b': (0.0, 0.8),
     'L0_attn_bf': (0.0, 0.269),
     'L0_attn_bB': (0.0, 0.1),
     'L0_attn_bC': (0.0, 0.1),
     'L0_attn_bD': (0.0, 0.1),
     'L0_attn_Dvec': (1.0, 0.2),
     'L0_ffn_b1': (0.0, 0.8),
     'L0_ffn_b2': (0.0, 2.0)}
    factors = {'L0_tok_b': 3.474,
     'L0_attn_W1': 8.0,
     'L0_attn_W2': 8.0,
     'L0_attn_conv_w': 8.0,
     'L0_attn_Wf': 8.0,
     'L0_ffn_phi': 38.459,
     'L0_ffn_w1': 8.0,
     'L0_ffn_w2': 8.0}
    for name, (base, spread) in spreads.items():
        noise = np.random.default_rng([zlib.crc32(name.encode()), seed]).standard_normal(out[name].shape)
        drawn = base * np.exp(spread * noise) if base else spread * noise
        out[name] = jnp.asarray(drawn.astype(out[name].dtype))
    for name, factor in factors.items():
        out[name] = (out[name] * factor).astype(out[name].dtype)
    return out
```

```python
from contextlib import ExitStack

import concourse.bass as bass
from concourse import mybir

F32 = mybir.dt.float32
F32R = mybir.dt.float32r
ALU = mybir.AluOpType
ACT = mybir.ActivationFunctionType
AX = mybir.AxisListType

B = 8
P = 128
D = 192
HALF = D // 2
HID = 384
CT = HID // P
TAPS = 4
GRID = 27
NPATCH = GRID * GRID
NIMG = NPATCH + 1
NTXT = 128
SEQ = NIMG + NTXT
BLOCKS = (GRID + 1) * GRID
CH = 3
TILES = 7
TOK = TILES * P
LASTP = NPATCH - 5 * P
CLS = 5 * P + LASTP
TXT0 = 6 * P
SPLIT = 430
LSPLIT = TOK // 2
EXP = 64
FF = 768
KJ = FF // P
GROUP = 8
NG = EXP // GROUP
PAIRS = GROUP // 2
UNIT = 3 * FF
CHUNK = UNIT // 3
SLOTS = 8
HIS = 6
EPS_LN = 1e-5
EPS_L2 = 1e-12
SEG = ((0, NIMG), (TXT0, TOK))


def now(x):
    return x() if callable(x) else x


def build(nc, xp, txt, wt, tb, cls, pos, w1, w2, chan, wf, bf, phi, scale, ew1, eb1, ew2, eb2, out):
    with ExitStack() as ctx:
        def sb(name, shape, dt=F32):
            return ctx.enter_context(nc.sbuf_tensor(name, shape, dt))

        def sem(name):
            return ctx.enter_context(nc.semaphore(name))

        H = sb("H", [P, B, TILES, D])
        CTt = sb("CTt", [P, B, TOK])
        XT = sb("XT", [P, 2, B, EXP])
        RC = sb("RC", [P, B, TILES])
        ident = sb("ident", [P, P])
        b1T = sb("b1T", [P, EXP, KJ])
        b2e = sb("b2e", [EXP, D])
        stage_lo_at = (now(nc.sbuf_base) + 31) // 32 * 32
        stage_lo = nc.alloc_sbuf_tensor_at("stage_lo", [P, 4, UNIT], F32, offset=stage_lo_at)

        base = stage_lo_at + 4 * UNIT * 4
        end = now(nc.sbuf_usable_end)

        def arena():
            at = [base]

            def take(name, shape, dt=F32):
                size = 4
                for n in shape[1:]:
                    size *= n
                t = nc.alloc_sbuf_tensor_at(name, shape, dt, offset=at[0])
                at[0] += (size + 31) // 32 * 32
                assert at[0] <= end, (name, at[0], end)
                return t
            return take

        one = arena()
        X = one("X", [P, CH, BLOCKS])
        Wt = one("Wt", [P, CH, 2, D])
        PB = one("PB", [P, 6, D])
        W12 = one("W12", [HALF, 2, 2 * HID])
        CHAN = one("CHAN", [P, CT, TAPS + 3])
        Wf = one("Wf", [P, CT, D])
        BF = one("BF", [P, D])
        PHI = one("PHI", [HALF, 2, EXP])
        PHN = one("PHN", [HALF, 2, 2 * EXP])
        SC = one("SC", [HALF, 1])
        pn = one("pn", [HALF, EXP])
        pr = one("pr", [HALF, EXP])
        XN = one("XN", [P, TILES, D])
        XN2 = one("XN2", [P, TILES, D])
        XNT = one("XNT", [HALF, 2, SEQ])
        CB, TBb = XN[:, 0, :], XN[:, 1, :]
        ones = XNT[:, 0, 0:HALF]
        X2T = one("X2T", [HALF, 2, TOK])
        PSQ = X2T[:, :, 0:EXP]
        A = one("A", [P, CT, TAPS - 1 + SEQ])
        CV = one("CV", [P, 2, SEQ])
        AG = one("AG", [P, CT, TOK])
        LE = one("LE", [P, TOK])
        DT = one("DT", [P, TILES, EXP])
        CS = one("CS", [P, TILES, EXP])
        CE = one("CE", [P, TILES, 2 * EXP])
        XS = one("XS", [EXP, 4 * EXP])
        st1 = one("st1", [P, TILES, 6])
        mv1 = one("mv1", [P, TILES, 2])
        ve1 = one("ve1", [P, TILES])
        sd1 = one("sd1", [P, TILES])
        rs1 = one("rs1", [P, TILES])
        st2 = one("st2", [P, TILES, 6])
        mv2 = one("mv2", [P, TILES, 2])
        ve2 = one("ve2", [P, 2, TILES])
        sd2 = one("sd2", [P, 2, TILES])
        rs2 = one("rs2", [P, TILES])
        nr2 = one("nr2", [P, TILES])
        nq2 = one("nq2", [P, TILES])
        ri2 = one("ri2", [P, TILES])
        sc2 = one("sc2", [P, TILES])
        mx2 = one("mx2", [P, 2])
        mxa = one("mxa", [P, 1])
        nmx = one("nmx", [P, 1])
        es = one("es", [P, 2])
        esum = one("esum", [P, 1])
        erec = one("erec", [P, 1])
        rmx = one("rmx", [P, TILES])
        rsm = one("rsm", [P, TILES])

        two = arena()
        stage_hi = two("stage_hi", [P, 4, UNIT])
        WH = two("WH", [P, HIS, CHUNK], F32R)
        XPD = two("XPD", [P, 12 * P + 416], F32R)
        HS = two("HS", [P, FF])
        HB = two("HB", [P, KJ * EXP])
        HG = two("HG", [P, KJ * EXP])
        HH = two("HH", [P, KJ, GROUP, 2, B], F32R)
        SEL = two("SEL", [P, 96])
        YS = two("YS", [P, PAIRS, 2 * D])
        YB = two("YB", [P, B, D])
        low_lo = nc.alloc_sbuf_tensor_at("low_lo", [P, 4, UNIT], F32R, offset=stage_lo_at)
        low_hi = nc.alloc_sbuf_tensor_at("low_hi", [P, 4, UNIT], F32R, offset=base)

        def stage(s):
            return stage_lo[:, s, :] if s < 4 else stage_hi[:, s - 4, :]

        def low(s):
            return low_lo[:, s, :] if s < 4 else low_hi[:, s - 4, :]

        PS = ctx.enter_context(nc.psum_tensor("PS", [P, 8, 512], F32))

        def bank(i):
            return PS[:, i, :]

        W_BANK, E_BANK, F_BANK, X_BANK = 0, 2, 4, 6
        H_BANK, T_BANK, Y_BANK, O_BANK = 0, 2, 4, 6

        in_const, in_pos, in_cls = sem("in_const"), sem("in_pos"), sem("in_cls")
        in_x = sem("in_x")
        pos_ready, cls_ready, zeroed, id_ready, a_pad = (sem(n) for n in ("pos_ready", "cls_ready", "zeroed", "id_ready", "a_pad"))
        phi_sq, phi_sum, phi_root, phi_clip, phi_rec, phi_sc, phi_ready = (sem("phi" + n) for n in "abcdefg")
        emb_done, emb_used = sem("emb_done"), sem("emb_used")
        stats1, mean1, var1, root1, rstd1, norm1 = (sem(n) for n in ("stats1", "mean1", "var1", "root1", "rstd1", "norm1"))
        stats2, mean2, var2, root2, len2, norm2 = (sem(n) for n in ("stats2", "mean2", "var2", "root2", "len2", "norm2"))
        xnt_ready, x2t_ready = sem("xnt_ready"), sem("x2t_ready")
        w_done, w_used, a_ready, g_ready = sem("w_done"), sem("w_used"), sem("a_ready"), sem("g_ready")
        tap_done, conv_done, silu_done, ag_ready = sem("tap_done"), sem("conv_done"), sem("silu_done"), sem("ag_ready")
        bf_added, wf_done, wf_used = sem("bf_added"), sem("wf_done"), sem("wf_used")
        xb_done = [sem("xb_done0"), sem("xb_done1")]
        xb_used = [sem("xb_used0"), sem("xb_used1")]
        le_ready, max_ready, exp_done, pad_done, rec_done, d_ready = (sem(n) for n in ("le_ready", "max_ready", "exp_done", "pad_done", "rec_done", "d_ready"))
        rmax_done, dt_ready, cs_ready, ce_ready, rsum_done, xs_ready = (sem(n) for n in ("rmax_done", "dt_ready", "cs_ready", "ce_ready", "rsum_done", "xs_ready"))
        staged = [sem(f"staged{s}") for s in range(SLOTS)]
        held_pe, held_dve, held_pool = sem("held_pe"), sem("held_dve"), sem("held_pool")

        def uses_c(b):
            return 0 if isinstance(b, int) and b == 0 else b * 8 - 6

        def uses_e1(b):
            return b * 8 + (2 if isinstance(b, int) and b == B - 1 else 4)

        def uses_e2(b):
            return b * 8 + (5 if isinstance(b, int) and b == B - 1 else 7)

        def wait(eng, s, n):
            if not isinstance(n, int) or n > 0:
                eng.wait_ge(s, n)

        def hold(eng, held):
            eng.sem_inc(held, 1)

        def load_w1(sp, s, e0):
            dst = stage(s).rearrange("p (k h) -> p k h", k=3)
            sp.dma_start(dst[:, 0:2, :], ew1[bass.ds(e0, 2), 0:P, :].rearrange("e d h -> d e h")).then_inc(staged[s], 16)
            sp.dma_start(dst[0:64, 2, :], ew1[bass.ds(e0, 1), P:D, :].rearrange("e d h -> (e d) h")).then_inc(staged[s], 16)
            sp.dma_start(dst[64:P, 2, :], ew1[bass.ds(e0 + 1, 1), P:D, :].rearrange("e d h -> (e d) h")).then_inc(staged[s], 16)

        def load_w2(sp, s, e0):
            dst = stage(s).rearrange("p (c e n) -> p c e n", c=3, e=2)
            src = ew2[bass.ds(e0, 2), :, :].rearrange("e (p c j) d -> p c e (j d)", c=3, j=2)
            for c in range(3):
                sp.dma_start(dst[:, c, :, :], src[:, c, :, :]).then_inc(staged[s], 16)

        with nc.Block() as block:
            @block.sync
            def _(sp):
                n_const = [0]

                def const(dst, src):
                    sp.dma_start(dst, src).then_inc(in_const, 16)
                    n_const[0] += 1

                def load_x(b):
                    if not (isinstance(b, int) and b == 0):
                        sp.wait_ge(emb_done, b * 6)
                    sp.dma_start(X[:, :, :], xp[bass.ds(b, 1), :, :, :].rearrange("o p c n -> (o p) c n")).then_inc(in_x, 16)

                load_x(0)
                const(Wt[:, :, :, :], wt)
                sp.dma_start(PB[:, 0:5, :], pos[1:1 + 5 * P, :].rearrange("(t p) d -> p t d", p=P)).then_inc(in_pos, 16)
                sp.dma_start(PB[0:LASTP, 5, :], pos[1 + 5 * P:NIMG, :]).then_inc(in_pos, 16)
                sp.dma_start(PB[LASTP:LASTP + 1, 5, :], pos[0:1, :]).then_inc(in_pos, 16)
                sp.dma_start(TBb[:, :], tb.unsqueeze(0).broadcast_to([P, D])).then_inc(in_pos, 16)
                sp.dma_start(CB[0:LASTP, :], tb.unsqueeze(0).broadcast_to([LASTP, D])).then_inc(in_pos, 16)
                sp.dma_start(CB[LASTP:LASTP + 1, :], cls).then_inc(in_pos, 16)
                const(H[:, :, 6, :], txt.rearrange("b p d -> p b d"))
                const(W12[:, :, 0:HID], w1.rearrange("(s q) h -> q s h", s=2))
                const(W12[:, :, HID:2 * HID], w2.rearrange("(s q) h -> q s h", s=2))
                const(CHAN[:, :, :], chan)
                const(Wf[:, :, :], wf.rearrange("(c p) d -> p c d", p=P))
                const(BF[:, :], bf.unsqueeze(0).broadcast_to([P, D]))
                const(PHI[:, :, :], phi.rearrange("(s q) n o -> q s (n o)", s=2))
                const(SC[:, :], scale.unsqueeze(0).broadcast_to([HALF, 1]))
                const(b1T[:, :, :], eb1)
                const(b2e[:, :], eb2)
                sp.wait_ge(pos_ready, 2)
                sp.wait_ge(zeroed, 1)
                sp.dma_start(H[LASTP:LASTP + 1, :, 5, :], PB[LASTP:LASTP + 1, 5, :].unsqueeze(1).broadcast_to([1, B, D])).then_inc(in_cls, 16)
                for p in range(PAIRS):
                    load_w1(sp, p, 2 * p)
                with sp.Fori(1, B) as b:
                    load_x(b)

            N_CONST = 11 * 16

            @block.gpsimd
            def _(pool):
                nc.gpsimd.memset(H[:, :, 5, :], 0.0).then_inc(zeroed, 1)
                nc.gpsimd.memset(ident[:, :], 0.0).then_inc(id_ready, 1)
                nc.gpsimd.memset(A[:, :, 0:TAPS - 1], 0.0).then_inc(a_pad, 1)
                nc.gpsimd.memset(AG[:, :, CLS + 1:TXT0], 0.0).then_inc(a_pad, 1)
                pool.wait_ge(id_ready, 1)
                nc.gpsimd.affine_select(out=ident[:, :], in_=ident[:, :], compare_op=ALU.not_equal, fill=1.0,
                                        base=0, pattern=[[-1, P]], channel_multiplier=1).then_inc(id_ready, 1)
                nc.gpsimd.memset(ones[:, :], 1.0).then_inc(id_ready, 1)
                pool.wait_ge(in_const, N_CONST)

                def add_bf(b):
                    pool.wait_ge(norm1, b * TILES + TILES)
                    h = H[:, bass.ds(b, 1), :, :].rearrange("p o t d -> p (o t) d")
                    nc.gpsimd.tensor_tensor(h, h, BF[:, :].unsqueeze(1).broadcast_to([P, TILES, D]), ALU.add).then_inc(bf_added, 1)

                def gate(b):
                    wait(pool, pad_done, b * 1)
                    for c in range(CT):
                        pool.wait_ge(silu_done, b * CT + c + 1)
                        pool.wait_ge(g_ready, b * CT + c + 1)
                        for dst, src in ((slice(0, NPATCH), slice(1, NIMG)), (slice(CLS, CLS + 1), slice(0, 1)), (slice(TXT0, TOK), slice(NIMG, SEQ))):
                            nc.gpsimd.tensor_tensor(AG[:, c, dst], AG[:, c, dst], CV[:, c % 2, src], ALU.mult).then_inc(ag_ready, 1)

                def zero_pad(b, after):
                    if after:
                        pool.wait_ge(bf_added, b + 2)
                    else:
                        pool.wait_ge(ag_ready, b * 9 + 9)
                    pool.wait_ge(le_ready, b * 2 + 2)
                    hold(pool, held_pool)
                    nc.gpsimd.memset(LE[EXP:P, CLS + 1:TXT0], 0.0).then_inc(pad_done, 1)

                add_bf(0)
                with pool.Fori(0, B - 1) as b:
                    gate(b)
                    add_bf(b + 1)
                    zero_pad(b, True)
                gate(B - 1)
                zero_pad(B - 1, False)

            @block.tensor
            def _(pe):
                def embed(b):
                    pe.wait_ge(in_x, b * 16 + 16)
                    for t in range(6):
                        m = P if t < 5 else LASTP
                        wait(pe, emb_used, b * 6 + (t - 1))
                        for c in range(CH):
                            for r in range(2):
                                at = r * GRID + t * P
                                mm = nc.tensor.matmul(bank(E_BANK + t % 2)[0:m, 0:D], X[:, c, at:at + m], Wt[:, c, r, :],
                                                      start=(c + r == 0), stop=(c == CH - 1 and r == 1))
                        mm.then_inc(emb_done, 1)

                def transposes(src, normed, count, n0):
                    for q in range(4):
                        j = q % 2
                        wait(pe, xb_used[j], n0 + q // 2)
                        for t in range(2 * q, min(2 * q + 2, TILES)):
                            pe.wait_ge(normed, count + t + 1)
                            for s in range(2):
                                at = s * 256 + (t % 2) * P
                                mm = nc.tensor.transpose(bank(X_BANK + j)[0:HALF, at:at + P], src[:, t, s * HALF:(s + 1) * HALF], ident[:, :])
                        mm.then_inc(xb_done[j], 1)

                def mixer_in(b, first, last):
                    pe.wait_ge(xnt_ready, b * 5 + 5)
                    for i in range(first, last):
                        c, half = i // 2, i % 2
                        lo, hi = (0, SPLIT) if half == 0 else (SPLIT, SEQ)
                        wait(pe, w_used, b * 12 + (i - 1))
                        for s in range(2):
                            mm = nc.tensor.matmul(bank(W_BANK + i % 2)[:, 0:hi - lo], W12[:, s, c * P:(c + 1) * P], XNT[:, s, lo:hi],
                                                  start=(s == 0), stop=(s == 1))
                        mm.then_inc(w_done, 1)

                def mixer_out(b):
                    pe.wait_ge(ag_ready, b * 9 + 9)
                    for t in range(TILES):
                        wait(pe, wf_used, b * TILES + (t if t == 0 else t - 1))
                        for c in range(CT):
                            mm = nc.tensor.matmul(bank(F_BANK + t % 2)[:, 0:D], AG[:, c, t * P:(t + 1) * P], Wf[:, c, :],
                                                  start=(c == 0), stop=(c == CT - 1))
                        mm.then_inc(wf_done, 1)

                def logits(b):
                    n0 = uses_e1(b)
                    transposes(XN2, norm2, b * TILES, n0)
                    pe.wait_ge(x2t_ready, b * 4 + 4)
                    for j in range(2):
                        pe.wait_ge(xb_used[j], n0 + 2)
                        for s in range(2):
                            mm = nc.tensor.matmul(bank(X_BANK + j)[:, 0:LSPLIT], PHN[:, s, :], X2T[:, s, j * LSPLIT:(j + 1) * LSPLIT],
                                                  start=(s == 0), stop=(s == 1))
                        mm.then_inc(xb_done[j], 1)

                def softmax_rows(b):
                    n0 = uses_e2(b)
                    pe.wait_ge(d_ready, b + 1)
                    for j in range(2):
                        pe.wait_ge(xb_used[j], n0)
                        for t in range(4 * j, min(4 * j + 4, TILES)):
                            mm = nc.tensor.transpose(bank(X_BANK + j)[:, (t % 4) * P:(t % 4 + 1) * P], LE[:, t * P:(t + 1) * P], ident[:, :])
                        mm.then_inc(xb_done[j], 1)

                def dispatch(b):
                    n0 = uses_e2(b)
                    pe.wait_ge(dt_ready, b * 2 + 2)
                    pe.wait_ge(xb_used[0], n0 + 1)
                    for t in range(TILES):
                        mm = nc.tensor.matmul(bank(X_BANK)[0:EXP, 0:D], DT[:, t, :], XN2[:, t, :], start=(t == 0), stop=(t == TILES - 1))
                    mm.then_inc(xb_done[0], 1)
                    pe.wait_ge(ce_ready, b + 1)
                    for j, tiles, n in ((1, range(0, 4), n0 + 1), (0, range(4, TILES), n0 + 2)):
                        pe.wait_ge(xb_used[j], n)
                        for t in tiles:
                            mm = nc.tensor.transpose(bank(X_BANK + j)[:, (t % 4) * P:(t % 4 + 1) * P], CE[:, t, :], ident[:, :])
                        mm.then_inc(xb_done[j], 1)
                    pe.wait_ge(xs_ready, b * 2 + 2)
                    pe.wait_ge(xb_used[1], n0 + 2)
                    hold(pe, held_pe)
                    for s in range(2):
                        mm = nc.tensor.transpose(bank(X_BANK + 1)[:, s * EXP:(s + 1) * EXP], XS[:, s * P:(s + 1) * P], ident[0:EXP, 0:EXP])
                    mm.then_inc(xb_done[1], 1)

                pe.wait_ge(in_const, N_CONST)
                pe.wait_ge(id_ready, 3)
                pe.wait_ge(phi_sq, 1)
                for s in range(2):
                    mm = nc.tensor.matmul(bank(W_BANK)[0:HALF, 0:EXP], ones[:, :], PSQ[:, s, :], start=(s == 0), stop=(s == 1))
                mm.then_inc(phi_sum, 1)
                embed(0)
                transposes(XN, norm1, 0, 0)
                pe.wait_ge(phi_root, 1)
                pe.wait_ge(phi_ready, 2)

                def step(b, before, after):
                    mixer_in(b, 0, 6)
                    if before:
                        softmax_rows(b - 1)
                    mixer_in(b, 6, 12)
                    if before:
                        dispatch(b - 1)
                    if after:
                        embed(b + 1)
                    mixer_out(b)
                    if after:
                        transposes(XN, norm1, b * TILES + TILES, uses_c(b + 1))
                    logits(b)

                step(0, False, True)
                with pe.Fori(1, B - 1) as b:
                    step(b, True, True)
                step(B - 1, True, False)
                softmax_rows(B - 1)
                dispatch(B - 1)

            @block.scalar
            def _(act):
                def root1_(b):
                    act.wait_ge(var1, b + 1)
                    nc.scalar.activation(sd1[:, :], ve1[:, :], ACT.Sqrt).then_inc(root1, 1)

                def keep_xnt(b):
                    n0 = uses_c(b)
                    for q in range(4):
                        j = q % 2
                        act.wait_ge(xb_done[j], n0 + (q // 2 + 1))
                        src = bank(X_BANK + j)[0:HALF, :].rearrange("p (s n) -> p s n", s=2)
                        if q < 2:
                            nc.scalar.activation(XNT[:, :, 1 + q * 256:1 + (q + 1) * 256], src, ACT.Identity).then_inc(xnt_ready, 1)
                        elif q == 2:
                            nc.scalar.activation(XNT[:, :, 513:NIMG], src[:, :, 0:P + LASTP], ACT.Identity).then_inc(xnt_ready, 1)
                            nc.scalar.activation(XNT[:, :, 0:1], src[:, :, P + LASTP:P + LASTP + 1], ACT.Identity).then_inc(xnt_ready, 1)
                        else:
                            nc.scalar.activation(XNT[:, :, NIMG:SEQ], src[:, :, 0:P], ACT.Identity).then_inc(xnt_ready, 1)
                        act.wait_ge(xnt_ready, b * 5 + (q + 1 if q < 2 else q + 2))
                        act.sem_inc(xb_used[j], 1)

                def keep_a(b):
                    act.wait_ge(a_pad, 2)
                    wait(act, conv_done, b * CT)
                    for i in range(6):
                        c, half = i // 2, i % 2
                        lo, hi = (0, SPLIT) if half == 0 else (SPLIT, SEQ)
                        act.wait_ge(w_done, b * 12 + (i + 1))
                        nc.scalar.activation(A[:, c, TAPS - 1 + lo:TAPS - 1 + hi], bank(W_BANK + i % 2)[:, 0:hi - lo], ACT.Identity,
                                             bias=CHAN[:, c, TAPS + 1:TAPS + 2]).then_inc(a_ready, 1)
                        act.wait_ge(a_ready, b * 6 + (i + 1))
                        act.sem_inc(w_used, 1)

                def combine_exp(b):
                    act.wait_ge(cs_ready, b * 2 + 2)
                    nc.scalar.activation(CE[:, :, :].rearrange("p t (r n) -> p t r n", r=2),
                                         CS[:, :, :].unsqueeze(2).broadcast_to([P, TILES, 2, EXP]), ACT.Exp).then_inc(ce_ready, 1)

                def keep_g(b):
                    for c in range(CT):
                        bias = CHAN[:, c, TAPS + 2:TAPS + 3]
                        act.wait_ge(w_done, b * 12 + (6 + 2 * c + 1))
                        src = bank(W_BANK)
                        nc.scalar.activation(AG[:, c, CLS:CLS + 1], src[:, 0:1], ACT.Silu, bias=bias)
                        nc.scalar.activation(AG[:, c, 0:SPLIT - 1], src[:, 1:SPLIT], ACT.Silu, bias=bias).then_inc(w_used, 1)
                        act.wait_ge(w_done, b * 12 + (6 + 2 * c + 2))
                        src = bank(W_BANK + 1)
                        nc.scalar.activation(AG[:, c, SPLIT - 1:NPATCH], src[:, 0:NIMG - SPLIT], ACT.Silu, bias=bias)
                        nc.scalar.activation(AG[:, c, TXT0:TOK], src[:, NIMG - SPLIT:SEQ - SPLIT], ACT.Silu, bias=bias).then_inc(w_used, 1)
                        act.wait_ge(w_used, b * 12 + (6 + 2 * c + 2))
                        act.sem_inc(g_ready, 1)
                    for c in range(CT):
                        act.wait_ge(conv_done, b * CT + (c + 1))
                        nc.scalar.activation(CV[:, c % 2, :], CV[:, c % 2, :], ACT.Silu, bias=CHAN[:, c, TAPS:TAPS + 1]).then_inc(silu_done, 1)

                def keep_dispatch(b):
                    n0 = uses_e2(b)
                    act.wait_ge(xb_done[0], n0 + 2)
                    nc.scalar.activation(XS[:, 0:D], bank(X_BANK)[0:EXP, 0:D], ACT.Identity).then_inc(xs_ready, 1)
                    nc.scalar.activation(XS[:, D:4 * EXP], bank(X_BANK)[0:EXP, P:D], ACT.Identity).then_inc(xs_ready, 1)
                    act.wait_ge(xs_ready, b * 2 + 2)
                    act.sem_inc(xb_used[0], 1)
                    for j, lo, hi, n in ((1, 0, 4 * P, n0 + 2), (0, 4 * P, TOK, n0 + 3)):
                        act.wait_ge(xb_done[j], n)
                        nc.scalar.activation(CTt[:, bass.ds(b, 1), lo:hi].rearrange("p o n -> p (o n)"), bank(X_BANK + j)[:, 0:hi - lo],
                                             ACT.Identity).then_inc(xb_used[j], 1)

                def root2_(b):
                    act.wait_ge(var2, b * 2 + 2)
                    nc.scalar.activation(sd2[:, :, :], ve2[:, :, :], ACT.Sqrt).then_inc(root2, 1)

                def keep_x2t(b):
                    n0 = uses_e1(b)
                    for q in range(4):
                        j = q % 2
                        cols = 256 if q < 3 else P
                        act.wait_ge(xb_done[j], n0 + (q // 2 + 1))
                        src = bank(X_BANK + j)[0:HALF, :].rearrange("p (s n) -> p s n", s=2)[:, :, 0:cols]
                        nc.scalar.activation(X2T[:, :, q * 256:q * 256 + cols], src, ACT.Identity).then_inc(x2t_ready, 1)
                        act.wait_ge(x2t_ready, b * 4 + (q + 1))
                        act.sem_inc(xb_used[j], 1)

                def dispatch_exp(b):
                    n0 = uses_e1(b)
                    for j in range(2):
                        act.wait_ge(xb_done[j], n0 + 3)
                        nc.scalar.activation(LE[:, j * LSPLIT:(j + 1) * LSPLIT], bank(X_BANK + j)[:, 0:LSPLIT], ACT.Identity).then_inc(le_ready, 1)
                        act.wait_ge(le_ready, b * 2 + (j + 1))
                        act.sem_inc(xb_used[j], 1)
                    act.wait_ge(max_ready, b * 4 + 4)
                    for i, (lo, hi) in enumerate(SEG):
                        nc.scalar.activation(LE[EXP:P, lo:hi], LE[EXP:P, lo:hi], ACT.Exp, bias=nmx[EXP:P, :],
                                             accum_out=es[EXP:P, i:i + 1]).then_inc(exp_done, 1)

                act.wait_ge(in_const, N_CONST)
                act.wait_ge(phi_sum, 1)
                nc.scalar.activation(pn[:, :], bank(W_BANK)[0:HALF, 0:EXP], ACT.Sqrt).then_inc(phi_root, 1)
                root1_(0)
                keep_xnt(0)

                def step(b, before, after):
                    keep_a(b)
                    if before:
                        combine_exp(b - 1)
                    keep_g(b)
                    if before:
                        keep_dispatch(b - 1)
                    if after:
                        root1_(b + 1)
                        keep_xnt(b + 1)
                    root2_(b)
                    keep_x2t(b)
                    dispatch_exp(b)

                step(0, False, True)
                with act.Fori(1, B - 1) as b:
                    step(b, True, True)
                step(B - 1, True, False)
                combine_exp(B - 1)
                keep_dispatch(B - 1)

            @block.vector
            def _(dve):
                def row(b, t):
                    return H[:, bass.ds(b, 1), t, :].rearrange("p o d -> p (o d)")

                def norm_in(b):
                    for t in range(6):
                        m = P if t < 5 else LASTP
                        dve.wait_ge(emb_done, b * 6 + (t + 1))
                        nc.vector.tensor_tensor(row(b, t)[0:m], bank(E_BANK + t % 2)[0:m, 0:D], PB[0:m, t, :], ALU.add).then_inc(emb_used, 1)
                    dve.wait_ge(emb_used, b * 6 + 6)
                    hold(dve, held_dve)
                    for t in range(TILES):
                        nc.vector.bn_stats(st1[:, t, :], row(b, t)).then_inc(stats1, 1)
                    dve.wait_ge(stats1, b * TILES + TILES)
                    hold(dve, held_dve)
                    for t in range(TILES):
                        nc.vector.bn_aggr(mv1[:, t, :], st1[:, t, :]).then_inc(mean1, 1)
                    dve.wait_ge(mean1, b * TILES + TILES)
                    nc.vector.tensor_scalar(ve1[:, :], mv1[:, :, 1], EPS_LN, None, ALU.add).then_inc(var1, 1)
                    dve.wait_ge(root1, b + 1)
                    nc.vector.reciprocal(rs1[:, :], sd1[:, :]).then_inc(rstd1, 1)
                    dve.wait_ge(rstd1, b + 1)
                    for t in range(TILES):
                        nc.vector.tensor_scalar(XN[:, t, :], row(b, t), mv1[:, t, 0:1], rs1[:, t:t + 1], ALU.subtract, ALU.mult).then_inc(norm1, 1)

                def conv(b, channels):
                    for c in channels:
                        dve.wait_ge(a_ready, b * 6 + (2 * c + 2))
                        wait(dve, ag_ready, b * 9 + (3 if c == 2 else 0))
                        cv = CV[:, c % 2, :]
                        nc.vector.tensor_scalar(cv, A[:, c, 0:SEQ], CHAN[:, c, 0:1], None, ALU.mult).then_inc(tap_done, 1)
                        for k in range(1, TAPS):
                            dve.wait_ge(tap_done, b * 9 + (3 * c + k))
                            mm = nc.vector.scalar_tensor_tensor(out=cv, in0=A[:, c, k:k + SEQ], scalar=CHAN[:, c, k:k + 1], in1=cv, op0=ALU.mult, op1=ALU.add)
                            mm.then_inc(tap_done if k < TAPS - 1 else conv_done, 1)

                def norm_mid(b):
                    dve.wait_ge(bf_added, b + 1)
                    for t in range(TILES):
                        if t > 0:
                            dve.wait_ge(wf_used, b * TILES + t)
                        dve.wait_ge(wf_done, b * TILES + (t + 1))
                        nc.vector.tensor_tensor(row(b, t), bank(F_BANK + t % 2)[:, 0:D], row(b, t), ALU.add).then_inc(wf_used, 1)
                        if t > 0:
                            nc.vector.bn_stats(st2[:, t - 1, :], row(b, t - 1)).then_inc(stats2, 1)
                    dve.wait_ge(wf_used, b * TILES + TILES)
                    hold(dve, held_dve)
                    nc.vector.bn_stats(st2[:, TILES - 1, :], row(b, TILES - 1)).then_inc(stats2, 1)
                    dve.wait_ge(stats2, b * TILES + TILES)
                    hold(dve, held_dve)
                    for t in range(TILES):
                        nc.vector.bn_aggr(mv2[:, t, :], st2[:, t, :]).then_inc(mean2, 1)
                    dve.wait_ge(mean2, b * TILES + TILES)
                    nc.vector.tensor_scalar(ve2[:, 0, :], mv2[:, :, 1], EPS_LN, None, ALU.add).then_inc(var2, 1)
                    nc.vector.tensor_scalar(ve2[:, 1, :], mv2[:, :, 1], float(D), None, ALU.mult).then_inc(var2, 1)
                    dve.wait_ge(root2, b + 1)
                    nc.vector.reciprocal(rs2[:, :], sd2[:, 0, :]).then_inc(len2, 1)
                    dve.wait_ge(len2, b * 5 + 1)
                    nc.vector.tensor_tensor(nr2[:, :], sd2[:, 1, :], rs2[:, :], ALU.mult).then_inc(len2, 1)
                    dve.wait_ge(len2, b * 5 + 2)
                    nc.vector.tensor_scalar(nq2[:, :], nr2[:, :], EPS_L2, None, ALU.max).then_inc(len2, 1)
                    dve.wait_ge(len2, b * 5 + 3)
                    nc.vector.reciprocal(ri2[:, :], nq2[:, :]).then_inc(len2, 1)
                    dve.wait_ge(len2, b * 5 + 4)
                    nc.vector.tensor_tensor(sc2[:, :], rs2[:, :], ri2[:, :], ALU.mult).then_inc(len2, 1)
                    dve.wait_ge(len2, b * 5 + 5)
                    for t in range(TILES):
                        nc.vector.tensor_scalar(XN2[:, t, :], row(b, t), mv2[:, t, 0:1], sc2[:, t:t + 1], ALU.subtract, ALU.mult).then_inc(norm2, 1)

                def dispatch_max(b):
                    dve.wait_ge(le_ready, b * 2 + 2)
                    for i, (lo, hi) in enumerate(SEG):
                        nc.vector.reduce_max(mx2[EXP:P, i:i + 1], LE[EXP:P, lo:hi], AX.X).then_inc(max_ready, 1)
                    dve.wait_ge(max_ready, b * 4 + 2)
                    nc.vector.tensor_tensor(mxa[EXP:P, :], mx2[EXP:P, 0:1], mx2[EXP:P, 1:2], ALU.max).then_inc(max_ready, 1)
                    dve.wait_ge(max_ready, b * 4 + 3)
                    nc.vector.tensor_scalar(nmx[EXP:P, :], mxa[EXP:P, :], -1.0, None, ALU.mult).then_inc(max_ready, 1)
                    dve.wait_ge(exp_done, b * 2 + 2)
                    nc.vector.tensor_tensor(esum[EXP:P, :], es[EXP:P, 0:1], es[EXP:P, 1:2], ALU.add).then_inc(rec_done, 1)
                    dve.wait_ge(rec_done, b * 2 + 1)
                    nc.vector.reciprocal(erec[EXP:P, :], esum[EXP:P, :]).then_inc(rec_done, 1)
                    dve.wait_ge(rec_done, b * 2 + 2)
                    dve.wait_ge(pad_done, b + 1)
                    nc.vector.tensor_scalar(LE[EXP:P, :], LE[EXP:P, :], erec[EXP:P, :], None, ALU.mult).then_inc(d_ready, 1)

                def combine_max(b):
                    n0 = uses_e2(b)
                    for j, (lo, hi) in enumerate(((0, 4), (4, TILES))):
                        dve.wait_ge(xb_done[j], n0 + 1)
                        src = bank(X_BANK + j)[:, 0:(hi - lo) * P].rearrange("p (t n) -> p t n", n=P)
                        nc.vector.reduce_max(rmx[:, lo:hi], src[:, :, 0:EXP], AX.X).then_inc(rmax_done, 1)
                        nc.vector.tensor_copy(DT[:, lo:hi, :], src[:, :, EXP:P]).then_inc(dt_ready, 1)
                        dve.wait_ge(rmax_done, b * 2 + (j + 1))
                        nc.vector.tensor_tensor(CS[:, lo:hi, :], src[:, :, 0:EXP], rmx[:, lo:hi].unsqueeze(2).broadcast_to([P, hi - lo, EXP]),
                                                ALU.subtract).then_inc(cs_ready, 1)
                        dve.wait_ge(cs_ready, b * 2 + (j + 1))
                        dve.sem_inc(xb_used[j], 1)

                def combine_sum(b):
                    dve.wait_ge(ce_ready, b + 1)
                    nc.vector.reduce_sum(rsm[:, :], CE[:, :, 0:EXP], AX.X).then_inc(rsum_done, 1)
                    dve.wait_ge(rsum_done, b * 2 + 1)
                    nc.vector.reciprocal(RC[:, bass.ds(b, 1), :].rearrange("p o t -> p (o t)"), rsm[:, :]).then_inc(rsum_done, 1)

                def keep_xt(b):
                    n0 = uses_e2(b)
                    dve.wait_ge(xb_done[1], n0 + 3)
                    nc.vector.tensor_copy(XT[:, :, bass.ds(b, 1), :].rearrange("p s o n -> p s (o n)"),
                                          bank(X_BANK + 1)[:, 0:2 * EXP].rearrange("p (s n) -> p s n", s=2)).then_inc(xb_used[1], 1)

                dve.wait_ge(in_pos, 6 * 16)
                nc.vector.tensor_tensor(PB[:, 0:5, :], PB[:, 0:5, :], TBb[:, :].unsqueeze(1).broadcast_to([P, 5, D]), ALU.add).then_inc(pos_ready, 1)
                nc.vector.tensor_tensor(PB[0:LASTP + 1, 5, :], PB[0:LASTP + 1, 5, :], CB[0:LASTP + 1, :], ALU.add).then_inc(pos_ready, 1)
                dve.wait_ge(in_const, N_CONST)
                nc.vector.tensor_tensor(PSQ[:, :, :], PHI[:, :, :], PHI[:, :, :], ALU.mult).then_inc(phi_sq, 1)
                dve.wait_ge(phi_root, 1)
                nc.vector.tensor_scalar(pr[:, :], pn[:, :], EPS_L2, None, ALU.max).then_inc(phi_clip, 1)
                dve.wait_ge(phi_clip, 1)
                nc.vector.reciprocal(pn[:, :], pr[:, :]).then_inc(phi_rec, 1)
                dve.wait_ge(phi_rec, 1)
                nc.vector.tensor_scalar(pr[:, :], pn[:, :], SC[:, 0:1], None, ALU.mult).then_inc(phi_sc, 1)
                dve.wait_ge(phi_sc, 1)
                for s in range(2):
                    nc.vector.tensor_tensor(PHN[:, s, :].rearrange("p (r n) -> p r n", r=2), PHI[:, s, :].unsqueeze(1).broadcast_to([HALF, 2, EXP]),
                                            pr[:, :].unsqueeze(1).broadcast_to([HALF, 2, EXP]), ALU.mult).then_inc(phi_ready, 1)
                dve.wait_ge(pos_ready, 2)
                dve.wait_ge(in_cls, 16)
                norm_in(0)

                def step(b, before, after):
                    conv(b, (0, 1))
                    if before:
                        combine_max(b - 1)
                    conv(b, (2,))
                    if before:
                        combine_sum(b - 1)
                        keep_xt(b - 1)
                    if after:
                        norm_in(b + 1)
                    norm_mid(b)
                    dispatch_max(b)

                step(0, False, True)
                with dve.Fori(1, B - 1) as b:
                    step(b, True, True)
                step(B - 1, True, False)
                combine_max(B - 1)
                combine_sum(B - 1)
                keep_xt(B - 1)

        hi_done, lo_done, w_spent = sem("hi_done"), sem("lo_done"), sem("w_spent")
        xpd_zero, xp_hi, xp_ready = sem("xpd_zero"), sem("xp_hi"), sem("xp_ready")
        hs_ready, t_done, hb_ready, hg_ready, hh_hi, hh_ready = (sem(n) for n in ("hs_ready", "t_done", "hb_ready", "hg_ready", "hh_hi", "hh_ready"))
        ys_ready, sel_ready = sem("ys_ready"), sem("sel_ready")
        ys_sent = [sem(f"ys_sent{p}") for p in range(PAIRS)]
        yb_ready, o_done, o_ready, stored = sem("yb_ready"), sem("o_done"), sem("o_ready"), sem("stored")

        def unit_w1(g, p):
            return p if isinstance(g, int) and g == 0 else g * 8 + (2 * p - 4)

        def unit_w2(g, p):
            return 60 + p if isinstance(g, int) and g == NG else g * 8 + (2 * p - 3)

        def slot_w1(g, p):
            return p if isinstance(g, int) and g == 0 else (2 * p + 4) % 8

        def slot_w2(g, p):
            return 4 + p if isinstance(g, int) and g == NG else (2 * p + 5) % 8

        def loads(g, k, s, second):
            if isinstance(g, int) and g in (0, NG):
                return 1 if g == 0 else 8
            return g + (1 if (2 * k + (5 if second else 4)) >= 8 else 0)

        with nc.Block() as block:
            @block.sync
            def _(sp):
                def load(g, p, second):
                    k = unit_w2(g, p) if second else unit_w1(g, p)
                    wait(sp, w_spent, k * 3 - 21)
                    if second:
                        load_w2(sp, slot_w2(g, p), g * GROUP + (2 * p - GROUP))
                    else:
                        load_w1(sp, slot_w1(g, p), g * GROUP + 2 * p)

                for p in range(PAIRS):
                    load(1, p, False)
                    load(1, p, True)
                with sp.Fori(2, NG) as g:
                    for p in range(PAIRS):
                        load(g, p, False)
                        load(g, p, True)
                for p in range(PAIRS):
                    load(NG, p, True)

            @block.gpsimd
            def _(pool):
                nc.gpsimd.memset(XPD[:, :].bitcast(F32), 0.0).then_inc(xpd_zero, 1)
                nc.gpsimd.memset(SEL[:, :], 0.0).then_inc(sel_ready, 1)
                pool.wait_ge(sel_ready, 1)
                for part in range(2):
                    sel = SEL[:, 0:EXP].rearrange("p (e b) -> p e b", e=GROUP)
                    nc.gpsimd.affine_select(out=sel, in_=sel, compare_op=ALU.not_equal, fill=1.0, base=-8 * part,
                                            pattern=[[-16, GROUP], [-1, B]], channel_multiplier=1).then_inc(sel_ready, 1)
                    pool.wait_ge(sel_ready, part + 2)

                def send(g):
                    for p in range(PAIRS):
                        pool.wait_ge(ys_ready, g * PAIRS + (p + 1))
                        for k in range(2):
                            e = 2 * p + k
                            for r in range(2):
                                n = g * GROUP + e + EXP * r
                                dst = YB[n:n + 1, :, :]
                                pool.dma_start(dst, YS[16 * e + B * r:16 * e + B * r + B, p, k * D:(k + 1) * D]).then_inc(ys_sent[p], 16)

                for g in range(NG):
                    send(g)
                for p in range(PAIRS):
                    pool.wait_ge(ys_sent[p], NG * 64)

            @block.tensor
            def _(pe):
                def first(g, p):
                    k, s = unit_w1(g, p), slot_w1(g, p)
                    if p == 0:
                        pe.wait_ge(xp_ready, g * 4 + 4)
                        wait(pe, hs_ready, g * 2)
                    for c in range(3):
                        pe.wait_ge(lo_done, k * 3 + (c + 1))
                        x = XPD[:, (3 * p + c) * P:(3 * p + c + 1) * P]
                        ring = (3 * s + c) % HIS
                        for n in range(2):
                            cols = slice(n * HID, (n + 1) * HID)
                            for i, w in enumerate((WH[:, ring, cols], low(s)[:, c * CHUNK + n * HID:c * CHUNK + (n + 1) * HID])):
                                mm = nc.tensor.matmul(bank(H_BANK + n)[:, 0:HID], x, w,
                                                      start=(p == 0 and c == 0 and i == 0), stop=(p == PAIRS - 1 and c == 2 and i == 1))
                        mm.then_inc(w_spent, 1)

                def turn(g):
                    pe.wait_ge(hs_ready, g * 2 + 2)
                    wait(pe, hb_ready, g * 2)
                    hs = HS[:, :].rearrange("p (n j) -> p n j", j=KJ)
                    for j in range(KJ):
                        at = (j % 3) * 96
                        mm = nc.tensor.matmul(bank(T_BANK + j // 3)[:, at:at + 96], hs[:, :, j], SEL[:, :], start=True, stop=True)
                        if j % 3 == 2:
                            mm.then_inc(t_done, 1)

                def second(g, p):
                    k, s = unit_w2(g, p), slot_w2(g, p)
                    n = g * PAIRS + (p - PAIRS)
                    if p == 0:
                        pe.wait_ge(hh_ready, g * 1)
                    wait(pe, ys_ready, n - (0 if p == 0 else 1))
                    for c in range(3):
                        pe.wait_ge(lo_done, k * 3 + (c + 1))
                        ring = (3 * s + c) % HIS
                        for j in range(2):
                            x = HH[:, 2 * c + j, :, :, :].rearrange("p e r b -> p (e r b)")
                            for i, w in enumerate((WH[:, ring, :], low(s)[:, c * CHUNK:(c + 1) * CHUNK])):
                                w = w.rearrange("p (e j d) -> p e j d", e=2, j=2)[:, :, j, :]
                                mm = nc.tensor.matmul(bank(Y_BANK + p % 2)[:, 0:2 * D], x, w,
                                                      start=(c + j + i == 0), stop=(c == 2 and j == 1 and i == 1))
                        mm.then_inc(w_spent, 1)

                pe.wait_ge(sel_ready, 3)
                for p in range(PAIRS):
                    first(0, p)
                turn(0)
                with pe.Fori(1, NG) as g:
                    for p in range(PAIRS):
                        first(g, p)
                        second(g, p)
                    turn(g)
                for p in range(PAIRS):
                    second(NG, p)

            @block.scalar
            def _(act):
                def high(g, p, second):
                    k, s = (unit_w2(g, p), slot_w2(g, p)) if second else (unit_w1(g, p), slot_w1(g, p))
                    act.wait_ge(staged[s], loads(g, p, s, second) * 48)
                    for c in range(3):
                        wait(act, w_spent, k * 3 + (c - 5))
                        nc.scalar.activation(WH[:, (3 * s + c) % HIS, :], stage(s)[:, c * CHUNK:(c + 1) * CHUNK], ACT.Identity).then_inc(hi_done, 1)

                def keep_h(g):
                    act.wait_ge(w_spent, unit_w1(g, PAIRS - 1) * 3 + 3)
                    wait(act, t_done, g * 2)
                    for n in range(2):
                        nc.scalar.activation(HS[:, n * HID:(n + 1) * HID], bank(H_BANK + n)[:, 0:HID], ACT.Identity).then_inc(hs_ready, 1)

                def keep_y(g, p):
                    act.wait_ge(w_spent, unit_w2(g, p) * 3 + 3)
                    wait(act, ys_sent[p], g * 64 - 64 if not (isinstance(g, int)) or g > 1 else 0)
                    nc.scalar.activation(YS[:, p, :], bank(Y_BANK + p % 2)[:, 0:2 * D], ACT.Identity).then_inc(ys_ready, 1)

                def gelu(g):
                    act.wait_ge(hb_ready, g * 2 + 2)
                    nc.scalar.activation(HG[:, :], HB[:, :], ACT.Gelu).then_inc(hg_ready, 1)
                    act.wait_ge(hg_ready, g + 1)
                    hg = HG[:, :].rearrange("p (n b) -> p n b", b=B)
                    nc.scalar.activation(HH[:, :, :, 0, :].rearrange("p j e b -> p (j e) b"), hg, ACT.Identity).then_inc(hh_hi, 1)

                for p in range(PAIRS):
                    high(0, p, False)
                keep_h(0)
                with act.Fori(1, NG) as g:
                    for p in range(PAIRS):
                        high(g, p, False)
                        if p == 0:
                            gelu(g - 1)
                        high(g, p, True)
                        if p > 0:
                            keep_y(g, p - 1)
                    keep_y(g, PAIRS - 1)
                    keep_h(g)
                gelu(NG - 1)
                for p in range(PAIRS):
                    high(NG, p, True)
                    if p > 0:
                        keep_y(NG, p - 1)
                keep_y(NG, PAIRS - 1)

            @block.vector
            def _(dve):
                def diagonal(g):
                    if not (isinstance(g, int) and g == 0):
                        dve.wait_ge(w_spent, (unit_w1(g - 1, PAIRS - 1) if not (isinstance(g, int) and g == 1) else PAIRS - 1) * 3 + 3)
                    x = XT[:, :, :, bass.ds(g * GROUP, GROUP)]
                    for part in range(2):
                        for n, (r, s, k, at) in enumerate(((slice(0, P), 0, 0, 0), (slice(0, P), 0, 1, P + 16), (slice(0, 64), 1, 0, 2 * P), (slice(64, P), 1, 1, 2 * P + 16))):
                            src = x[r, s, :, :].rearrange("p b (q k) -> p q b k", k=2)[:, :, :, k]
                            hi = diag(r, at)
                            if part == 0:
                                nc.vector.tensor_copy(hi, src).then_inc(xp_hi, 1)
                            else:
                                dve.wait_ge(xp_hi, g * 4 + (n + 1))
                                nc.vector.tensor_tensor(diag(r, at + B), src, hi.bitcast(F32), ALU.subtract).then_inc(xp_ready, 1)

                def diag(r, at):
                    step = 3 * P + 32
                    return XPD[r, at:at + 4 * step].rearrange("p (q c) -> p q c", c=step)[:, :, 0:B]

                def low_part(g, p, second):
                    k, s = (unit_w2(g, p), slot_w2(g, p)) if second else (unit_w1(g, p), slot_w1(g, p))
                    for c in range(3):
                        dve.wait_ge(hi_done, k * 3 + (c + 1))
                        cols = slice(c * CHUNK, (c + 1) * CHUNK)
                        nc.vector.tensor_tensor(low(s)[:, cols], stage(s)[:, cols], WH[:, (3 * s + c) % HIS, :].bitcast(F32), ALU.subtract).then_inc(lo_done, 1)

                def bias(g):
                    for i in range(2):
                        dve.wait_ge(t_done, g * 2 + (i + 1))
                        if i == 0:
                            wait(dve, hg_ready, g * 1)
                        src = bank(T_BANK + i)[:, 0:3 * 96].rearrange("p (j n) -> p j n", j=3)[:, :, 0:EXP]
                        for j in range(3):
                            jj = 3 * i + j
                            last = nc.vector.tensor_tensor(HB[:, jj * EXP:(jj + 1) * EXP].rearrange("p (e b) -> p e b", b=B),
                                                           src[:, j, :].rearrange("p (e b) -> p e b", b=B),
                                                           b1T[:, bass.ds(g * GROUP, GROUP), jj:jj + 1].broadcast_to([P, GROUP, B]), ALU.add)
                        last.then_inc(hb_ready, 1)

                def hidden_low(g):
                    dve.wait_ge(hh_hi, g + 1)
                    nc.vector.tensor_tensor(HH[:, :, :, 1, :].rearrange("p j e b -> p (j e) b"), HG[:, :].rearrange("p (n b) -> p n b", b=B),
                                            HH[:, :, :, 0, :].rearrange("p j e b -> p (j e) b").bitcast(F32), ALU.subtract).then_inc(hh_ready, 1)

                dve.wait_ge(xpd_zero, 1)
                diagonal(0)
                for p in range(PAIRS):
                    low_part(0, p, False)
                diagonal(1)
                bias(0)
                with dve.Fori(1, NG - 1) as g:
                    for p in range(PAIRS):
                        low_part(g, p, False)
                        if p == 0:
                            hidden_low(g - 1)
                        low_part(g, p, True)
                    diagonal(g + 1)
                    bias(g)
                for p in range(PAIRS):
                    low_part(NG - 1, p, False)
                    if p == 0:
                        hidden_low(NG - 2)
                    low_part(NG - 1, p, True)
                bias(NG - 1)
                hidden_low(NG - 1)
                for p in range(PAIRS):
                    low_part(NG, p, True)

        with nc.Block() as block:
            @block.vector
            def _(dve):
                for b in range(B):
                    nc.vector.tensor_tensor(YB[0:EXP, b, :], YB[0:EXP, b, :], b2e[:, :], ALU.add).then_inc(yb_ready, 1)
                for b in range(B):
                    for t in range(TILES):
                        n = b * TILES + t
                        dve.wait_ge(o_done, n + 1)
                        nc.vector.scalar_tensor_tensor(out=H[:, b, t, :], in0=bank(n % 8)[:, 0:D], scalar=RC[:, b, t:t + 1], in1=H[:, b, t, :],
                                                       op0=ALU.mult, op1=ALU.add).then_inc(o_ready, 1)

            @block.tensor
            def _(pe):
                for b in range(B):
                    pe.wait_ge(yb_ready, b + 1)
                    for t in range(TILES):
                        n = b * TILES + t
                        wait(pe, o_ready, n - 7)
                        nc.tensor.matmul(bank(n % 8)[:, 0:D], CTt[:, b, t * P:(t + 1) * P], YB[:, b, :], start=True, stop=True).then_inc(o_done, 1)

            @block.sync
            def _(sp):
                for b in range(B):
                    sp.wait_ge(o_ready, b * TILES + TILES)
                    sp.dma_start(out[b, 1:1 + 5 * P, :].rearrange("(t p) d -> p t d", p=P), H[:, b, 0:5, :]).then_inc(stored, 16)
                    sp.dma_start(out[b, 1 + 5 * P:NIMG, :], H[0:LASTP, b, 5, :]).then_inc(stored, 16)
                    sp.dma_start(out[b, 0:1, :], H[LASTP:LASTP + 1, b, 5, :]).then_inc(stored, 16)
                    sp.dma_start(out[b, NIMG:SEQ, :], H[:, b, 6, :]).then_inc(stored, 16)
                sp.wait_ge(stored, B * 4 * 16)


def kernel(**inputs):
    import numpy as np
    import concourse.bacc as bacc
    from concourse.bass_utils import run_bass_kernel_spmd

    def arr(name):
        return np.ascontiguousarray(inputs[name])

    x = arr("x").reshape(B, CH, GRID + 1, 8, 28, 8)
    left, right = x[..., :GRID, :], x[..., 1:, :]
    strips = np.concatenate([left, right], axis=-1)
    strips = np.ascontiguousarray(strips.transpose(0, 3, 5, 1, 2, 4)).reshape(B, P, CH, BLOCKS)
    filt = arr("L0_tok_w").reshape(D, CH, 2, 8, 16).transpose(3, 4, 1, 2, 0)
    filt = np.ascontiguousarray(filt).reshape(P, CH, 2, D)
    columns = [arr("L0_attn_conv_w").reshape(CT, P, TAPS)] + [arr(n).reshape(CT, P, 1) for n in ("L0_attn_conv_b", "L0_attn_b1", "L0_attn_b2")]
    chan = np.ascontiguousarray(np.concatenate(columns, axis=2).transpose(1, 0, 2))
    eb1 = np.ascontiguousarray(arr("L0_ffn_b1").reshape(EXP, P, KJ).transpose(1, 0, 2))
    arrays = {
        "xp": strips, "txt": arr("txt"), "wt": filt, "tb": arr("L0_tok_b"),
        "cls": arr("L0_tok_cls_token").reshape(1, D), "pos": arr("L0_tok_pos_embedding").reshape(NIMG, D),
        "w1": arr("L0_attn_W1"), "w2": arr("L0_attn_W2"), "chan": chan, "wf": arr("L0_attn_Wf"), "bf": arr("L0_attn_bf"),
        "phi": arr("L0_ffn_phi"), "scale": arr("L0_ffn_scale"), "ew1": arr("L0_ffn_w1"), "eb1": eb1,
        "ew2": arr("L0_ffn_w2"), "eb2": arr("L0_ffn_b2"),
    }
    nc = bacc.Bacc("TRN2", target_bir_lowering=False, num_devices=1)
    args = [nc.dram_tensor(f"in_{n}", a.shape, mybir.dt.from_np(a.dtype), kind="ExternalInput").ap() for n, a in arrays.items()]
    o = nc.dram_tensor("out_0", (B, SEQ, D), F32, kind="ExternalOutput").ap()
    build(nc, *args, o)
    r = run_bass_kernel_spmd(nc, [{f"in_{n}": a for n, a in arrays.items()}], core_ids=[0])
    return r.results[0]["out_0"]
```

```python
from contextlib import ExitStack

import concourse.bass as bass
from concourse import mybir

F32 = mybir.dt.float32
F32R = mybir.dt.float32r
ALU = mybir.AluOpType
ACT = mybir.ActivationFunctionType
AX = mybir.AxisListType

B = 8
P = 128
D = 192
HALF = D // 2
HID = 384
CT = HID // P
TAPS = 4
GRID = 27
NPATCH = GRID * GRID
NIMG = NPATCH + 1
NTXT = 128
SEQ = NIMG + NTXT
BLOCKS = (GRID + 1) * GRID
CH = 3
TILES = 7
TOK = TILES * P
LASTP = NPATCH - 5 * P
CLS = 5 * P + LASTP
TXT0 = 6 * P
SPLIT = 430
LSPLIT = TOK // 2
EXP = 64
FF = 768
KJ = FF // P
GROUP = 8
NG = EXP // GROUP
PAIRS = GROUP // 2
UNIT = 3 * FF
CHUNK = UNIT // 3
SLOTS = 8
EARLY = 1
SLOT_AFTER_EMBED = 2
SLOT_AFTER_MIXER = 4
SLOT_AFTER_CONV = 5
HIS = 6
EPS_LN = 1e-5
EPS_L2 = 1e-12
SEG = ((0, NIMG), (TXT0, TOK))


def now(x):
    return x() if callable(x) else x


def build(nc, xp, txt, wt, tb, cls, pos, w1, w2, chan, wf, bf, phi, scale, ew1, eb1, ew2, eb2, out):
    with ExitStack() as ctx:
        def sb(name, shape, dt=F32):
            return ctx.enter_context(nc.sbuf_tensor(name, shape, dt))

        def sem(name):
            return ctx.enter_context(nc.semaphore(name))

        H = sb("H", [P, B, TILES, D])
        CTt = sb("CTt", [P, B, TOK])
        XT = sb("XT", [P, 2, B, EXP])
        RC = sb("RC", [P, B, TILES])
        ident = sb("ident", [P, P])
        b1T = sb("b1T", [P, EXP, KJ])
        b2e = sb("b2e", [EXP, D])
        stage_lo_at = (now(nc.sbuf_base) + 31) // 32 * 32
        stage_lo = nc.alloc_sbuf_tensor_at("stage_lo", [P, EARLY, UNIT], F32, offset=stage_lo_at)

        base = stage_lo_at + EARLY * UNIT * 4
        end = now(nc.sbuf_usable_end)

        def arena():
            at = [base]

            def take(name, shape, dt=F32):
                size = 4
                for n in shape[1:]:
                    size *= n
                t = nc.alloc_sbuf_tensor_at(name, shape, dt, offset=at[0])
                at[0] += (size + 31) // 32 * 32
                assert at[0] <= end, (name, at[0], end)
                return t
            take.at = at
            return take

        one = arena()
        X = one("X", [P, CH, BLOCKS])
        Wt = one("Wt", [P, CH, 2, D])
        PB = one("PB", [P, 6, D])
        PHI = one("PHI", [HALF, 2, EXP])
        assert one.at[0] >= base + SLOT_AFTER_EMBED * UNIT * 4
        XNH = one("XNH", [HALF, 2, SEQ], F32R)
        XNL = one("XNL", [HALF, 2, SEQ], F32R)
        WLa = one.at[0]
        W12 = one("W12", [HALF, 2, 2 * HID])
        W12L = nc.alloc_sbuf_tensor_at("W12L", [HALF, 2, 2 * HID], F32R, offset=WLa)
        W12H = one("W12H", [HALF, 2, 2 * HID], F32R)
        assert one.at[0] >= base + SLOT_AFTER_MIXER * UNIT * 4
        A = one("A", [P, CT, TAPS - 1 + SEQ])
        assert one.at[0] >= base + SLOT_AFTER_CONV * UNIT * 4
        CV = one("CV", [P, CT, SEQ])
        assert one.at[0] >= base + (SLOTS - EARLY) * UNIT * 4
        CHAN = one("CHAN", [P, CT, TAPS + 3])
        Wf = one("Wf", [P, CT, D])
        BF = one("BF", [P, D])
        PHN = one("PHN", [HALF, 2, 2 * EXP])
        SC = one("SC", [HALF, 1])
        pn = one("pn", [HALF, EXP])
        pr = one("pr", [HALF, EXP])
        XN = one("XN", [P, TILES, D])
        XN2 = one("XN2", [P, TILES, D])
        X2T = one("X2T", [HALF, 2, TOK])
        CB, TBb = XN[:, 0, :], XN[:, 1, :]
        ones = CV[0:HALF, 0, 0:HALF]
        PSQ = X2T[:, :, 0:EXP]
        AG = one("AG", [P, CT, TOK])
        LE = one("LE", [P, TOK])
        DT = one("DT", [P, TILES, EXP])
        CS = one("CS", [P, TILES, EXP])
        CE = one("CE", [P, TILES, 2 * EXP])
        XS = one("XS", [EXP, 4 * EXP])
        nm1 = one("nm1", [P, TILES])
        st1 = one("st1", [P, TILES, 6])
        mv1 = one("mv1", [P, TILES, 2])
        ve1 = one("ve1", [P, TILES])
        sd1 = one("sd1", [P, TILES])
        rs1 = one("rs1", [P, TILES])
        st2 = one("st2", [P, TILES, 6])
        mv2 = one("mv2", [P, TILES, 2])
        ve2 = one("ve2", [P, 2, TILES])
        sd2 = one("sd2", [P, 2, TILES])
        rs2 = one("rs2", [P, TILES])
        nr2 = one("nr2", [P, TILES])
        nq2 = one("nq2", [P, TILES])
        ri2 = one("ri2", [P, TILES])
        sc2 = one("sc2", [P, TILES])
        mx2 = one("mx2", [P, 2])
        mxa = one("mxa", [P, 1])
        nmx = one("nmx", [P, 1])
        es = one("es", [P, 2])
        esum = one("esum", [P, 1])
        erec = one("erec", [P, 1])
        rmx = one("rmx", [P, TILES])
        rsm = one("rsm", [P, TILES])

        two = arena()
        stage_hi = two("stage_hi", [P, SLOTS - EARLY, UNIT])
        WH = two("WH", [P, HIS, CHUNK], F32R)
        XPD = two("XPD", [P, 12 * P + 416], F32R)
        HS = two("HS", [P, FF])
        HB = two("HB", [P, KJ * EXP])
        HG = two("HG", [P, KJ * EXP])
        HH = two("HH", [P, KJ, GROUP, 2, B], F32R)
        SEL = two("SEL", [P, 96])
        YS = two("YS", [P, PAIRS, 2 * D])
        YB = two("YB", [P, B, D])
        low_lo = nc.alloc_sbuf_tensor_at("low_lo", [P, EARLY, UNIT], F32R, offset=stage_lo_at)
        low_hi = nc.alloc_sbuf_tensor_at("low_hi", [P, SLOTS - EARLY, UNIT], F32R, offset=base)

        def stage(s):
            return stage_lo[:, s, :] if s < EARLY else stage_hi[:, s - EARLY, :]

        def low(s):
            return low_lo[:, s, :] if s < EARLY else low_hi[:, s - EARLY, :]

        PS = ctx.enter_context(nc.psum_tensor("PS", [P, 8, 512], F32))

        def bank(i):
            return PS[:, i, :]

        def slot(first, t):
            return PS[:, first + t // 2 % 2, (t % 2) * 256:(t % 2) * 256 + D]

        def both(first, q):
            return PS[:, first + q % 2, :].rearrange("p (t n) -> p t n", t=2)[:, :, 0:D]

        W_BANK, E_BANK, F_BANK, X_BANK = 0, 2, 4, 6
        TURN1 = (E_BANK, E_BANK + 1, X_BANK, X_BANK + 1)
        TURN2 = (F_BANK, F_BANK + 1, X_BANK, X_BANK + 1)
        H_BANK, T_BANK, Y_BANK, O_BANK = 0, 2, 4, 6

        in_const, in_pos, in_cls = sem("in_const"), sem("in_pos"), sem("in_cls")
        in_x, in_wt, w12_hi, w12_lo = sem("in_x"), sem("in_wt"), sem("w12_hi"), sem("w12_lo")
        pos_ready, cls_ready, zeroed, id_ready, a_pad = (sem(n) for n in ("pos_ready", "cls_ready", "zeroed", "id_ready", "a_pad"))
        phi_sq, phi_sum, phi_root, phi_clip, phi_rec, phi_sc, phi_ready = (sem("phi" + n) for n in "abcdefg")
        emb_done, emb_used = sem("emb_done"), sem("emb_used")
        stats1, mean1, var1, root1, rstd1, norm1 = (sem(n) for n in ("stats1", "mean1", "var1", "root1", "rstd1", "norm1"))
        stats2, mean2, var2, root2, len2, norm2 = (sem(n) for n in ("stats2", "mean2", "var2", "root2", "len2", "norm2"))
        turned, xnt_high, xnt_ready, x2t_ready = sem("turned"), sem("xnt_high"), sem("xnt_ready"), sem("x2t_ready")
        w_done, w_used, a_ready, g_ready = sem("w_done"), sem("w_used"), sem("a_ready"), sem("g_ready")
        tap_done, conv_done, silu_done, ag_ready = sem("tap_done"), sem("conv_done"), sem("silu_done"), sem("ag_ready")
        bf_added, wf_done, wf_used = sem("bf_added"), sem("wf_done"), sem("wf_used")
        xb_done = [sem("xb_done0"), sem("xb_done1")]
        xb_used = [sem("xb_used0"), sem("xb_used1")]
        le_ready, max_ready, exp_done, pad_done, rec_done, d_ready = (sem(n) for n in ("le_ready", "max_ready", "exp_done", "pad_done", "rec_done", "d_ready"))
        rmax_done, dt_ready, cs_ready, ce_ready, rsum_done, xs_ready = (sem(n) for n in ("rmax_done", "dt_ready", "cs_ready", "ce_ready", "rsum_done", "xs_ready"))
        staged = [sem(f"staged{s}") for s in range(SLOTS)]
        held_pe, held_dve, held_pool = sem("held_pe"), sem("held_dve"), sem("held_pool")

        PER_STEP = (7, 5)

        def uses(s, j):
            if isinstance(s, int) and s == B:
                return 2 + PER_STEP[j] * (B - 1) - 1
            return s * PER_STEP[j] + (2 - PER_STEP[j])

        def uses_norm1(b, j):
            if isinstance(b, int) and b < 2:
                return b
            return uses(b - 1, j) + (5 if j == 0 else 4)

        def turns(b, norm):
            if norm == 1:
                return 2 * b if isinstance(b, int) and b < 2 else b * 4 - 2
            return b * 4 + (4 if not isinstance(b, int) or b < B - 1 else 2)

        def uses_inputs(s):
            return uses(s, 0) + (6 if not isinstance(s, int) or s < B - 1 else 5)

        def wait(eng, s, n):
            if not isinstance(n, int) or n > 0:
                eng.wait_ge(s, n)

        def hold(eng, held):
            eng.sem_inc(held, 1)

        def load_w1(sp, s, e0):
            dst = stage(s).rearrange("p (k h) -> p k h", k=3)
            sp.dma_start(dst[:, 0:2, :], ew1[bass.ds(e0, 2), 0:P, :].rearrange("e d h -> d e h")).then_inc(staged[s], 16)
            sp.dma_start(dst[0:64, 2, :], ew1[bass.ds(e0, 1), P:D, :].rearrange("e d h -> (e d) h")).then_inc(staged[s], 16)
            sp.dma_start(dst[64:P, 2, :], ew1[bass.ds(e0 + 1, 1), P:D, :].rearrange("e d h -> (e d) h")).then_inc(staged[s], 16)

        def load_w2(sp, s, e0):
            dst = stage(s).rearrange("p (c e n) -> p c e n", c=3, e=2)
            src = ew2[bass.ds(e0, 2), :, :].rearrange("e (p c j) d -> p c e (j d)", c=3, j=2)
            for c in range(3):
                sp.dma_start(dst[:, c, :, :], src[:, c, :, :]).then_inc(staged[s], 16)

        def turned_columns(q):
            if q < 2:
                return ((slice(1 + q * 256, 257 + q * 256), slice(0, 256)),)
            if q == 2:
                return ((slice(513, NIMG), slice(0, P + LASTP)), (slice(0, 1), slice(P + LASTP, P + LASTP + 1)))
            return ((slice(NIMG, SEQ), slice(0, P)),)

        def load_unit(sp, k):
            if k < PAIRS or k % 2 == 0:
                load_w1(sp, k, 2 * k if k < PAIRS else GROUP + k - PAIRS)
            else:
                load_w2(sp, k, k - PAIRS - 1)

        with nc.Block() as block:
            @block.sync
            def _(sp):
                n_const = [0]

                def const(dst, src):
                    sp.dma_start(dst, src).then_inc(in_const, 16)
                    n_const[0] += 1

                def load_x(b):
                    if not (isinstance(b, int) and b == 0):
                        sp.wait_ge(emb_done, b * 3)
                    sp.dma_start(X[:, :, :], xp[bass.ds(b, 1), :, :, :].rearrange("o p c n -> (o p) c n")).then_inc(in_x, 16)

                sp.dma_start(Wt[:, :, :, :], wt).then_inc(in_wt, 16)
                load_x(0)
                sp.dma_start(PB[:, 0:5, :], pos[1:1 + 5 * P, :].rearrange("(t p) d -> p t d", p=P)).then_inc(in_pos, 16)
                sp.dma_start(PB[0:LASTP, 5, :], pos[1 + 5 * P:NIMG, :]).then_inc(in_pos, 16)
                sp.dma_start(PB[LASTP:LASTP + 1, 5, :], pos[0:1, :]).then_inc(in_pos, 16)
                sp.dma_start(TBb[:, :], tb.unsqueeze(0).broadcast_to([P, D])).then_inc(in_pos, 16)
                sp.dma_start(CB[0:LASTP, :], tb.unsqueeze(0).broadcast_to([LASTP, D])).then_inc(in_pos, 16)
                sp.dma_start(CB[LASTP:LASTP + 1, :], cls).then_inc(in_pos, 16)
                const(H[:, :, 6, :], txt.rearrange("b p d -> p b d"))
                const(W12[:, :, 0:HID], w1.rearrange("(s q) h -> q s h", s=2))
                const(W12[:, :, HID:2 * HID], w2.rearrange("(s q) h -> q s h", s=2))
                const(CHAN[:, :, :], chan)
                const(Wf[:, :, :], wf.rearrange("(c p) d -> p c d", p=P))
                const(BF[:, :], bf.unsqueeze(0).broadcast_to([P, D]))
                const(PHI[:, :, :], phi.rearrange("(s q) n o -> q s (n o)", s=2))
                const(SC[:, :], scale.unsqueeze(0).broadcast_to([HALF, 1]))
                const(b1T[:, :, :], eb1)
                const(b2e[:, :], eb2)
                sp.wait_ge(pos_ready, 2)
                sp.wait_ge(zeroed, 1)
                sp.dma_start(H[LASTP:LASTP + 1, :, 5, :], PB[LASTP:LASTP + 1, 5, :].unsqueeze(1).broadcast_to([1, B, D])).then_inc(in_cls, 16)
                for k in range(EARLY):
                    load_unit(sp, k)
                with sp.Fori(1, B) as b:
                    load_x(b)
                sp.wait_ge(emb_used, B * 3)
                for k in range(EARLY, EARLY + SLOT_AFTER_EMBED):
                    load_unit(sp, k)
                sp.wait_ge(w_done, B * 12)
                for k in range(EARLY + SLOT_AFTER_EMBED, EARLY + SLOT_AFTER_MIXER):
                    load_unit(sp, k)
                sp.wait_ge(conv_done, B * CT)
                for k in range(EARLY + SLOT_AFTER_MIXER, EARLY + SLOT_AFTER_CONV):
                    load_unit(sp, k)
                sp.wait_ge(ag_ready, B * CT * 3)
                for k in range(EARLY + SLOT_AFTER_CONV, SLOTS):
                    load_unit(sp, k)

            N_CONST = 10 * 16

            @block.gpsimd
            def _(pool):
                nc.gpsimd.memset(H[:, :, 5, :], 0.0).then_inc(zeroed, 1)
                nc.gpsimd.memset(ident[:, :], 0.0).then_inc(id_ready, 1)
                nc.gpsimd.memset(A[:, :, 0:TAPS - 1], 0.0).then_inc(a_pad, 1)
                nc.gpsimd.memset(AG[:, :, CLS + 1:TXT0], 0.0).then_inc(a_pad, 1)
                pool.wait_ge(id_ready, 1)
                nc.gpsimd.affine_select(out=ident[:, :], in_=ident[:, :], compare_op=ALU.not_equal, fill=1.0,
                                        base=0, pattern=[[-1, P]], channel_multiplier=1).then_inc(id_ready, 1)
                nc.gpsimd.memset(ones[:, :], 1.0).then_inc(id_ready, 1)
                pool.wait_ge(in_const, N_CONST)

                def add_bf(b):
                    pool.wait_ge(norm1, b * TILES + TILES)
                    h = H[:, bass.ds(b, 1), :, :].rearrange("p o t d -> p (o t) d")
                    nc.gpsimd.tensor_tensor(h, h, BF[:, :].unsqueeze(1).broadcast_to([P, TILES, D]), ALU.add).then_inc(bf_added, 1)

                def gate(b):
                    wait(pool, pad_done, b * 1)
                    for c in range(CT):
                        pool.wait_ge(silu_done, b * CT + c + 1)
                        pool.wait_ge(g_ready, b * CT + c + 1)
                        for dst, src in ((slice(0, NPATCH), slice(1, NIMG)), (slice(CLS, CLS + 1), slice(0, 1)), (slice(TXT0, TOK), slice(NIMG, SEQ))):
                            nc.gpsimd.tensor_tensor(AG[:, c, dst], AG[:, c, dst], CV[:, c, src], ALU.mult).then_inc(ag_ready, 1)

                def zero_pad(s):
                    pool.wait_ge(ag_ready, s * 9)
                    wait(pool, bf_added, B if isinstance(s, int) and s >= B - 1 else s + 1)
                    pool.wait_ge(le_ready, s * 2)
                    hold(pool, held_pool)
                    nc.gpsimd.memset(LE[EXP:P, CLS + 1:TXT0], 0.0).then_inc(pad_done, 1)

                add_bf(0)
                gate(0)
                add_bf(1)
                with pool.Fori(1, B - 1) as b:
                    zero_pad(b)
                    gate(b)
                    add_bf(b + 1)
                zero_pad(B - 1)
                gate(B - 1)
                zero_pad(B)

            @block.tensor
            def _(pe):
                def embed(b):
                    pe.wait_ge(in_x, b * 16 + 16)
                    for t in range(6):
                        m = P if t < 5 else LASTP
                        if t % 2 == 0:
                            wait(pe, emb_used, b * 3 + t // 4)
                        for c in range(CH):
                            for r in range(2):
                                at = r * GRID + t * P
                                mm = nc.tensor.matmul(slot(E_BANK, t)[0:m], X[:, c, at:at + m], Wt[:, c, r, :],
                                                      start=(c + r == 0), stop=(c == CH - 1 and r == 1))
                        if t % 2:
                            mm.then_inc(emb_done, 1)

                def transposes(src, normed, count, banks, n0):
                    for q in range(4):
                        if q >= 2:
                            wait(pe, xb_used[q - 2], n0[q - 2])
                        for t in range(2 * q, min(2 * q + 2, TILES)):
                            pe.wait_ge(normed, count + t + 1)
                            for s in range(2):
                                at = s * 256 + (t % 2) * P
                                mm = nc.tensor.transpose(bank(banks[q])[0:HALF, at:at + P], src[:, t, s * HALF:(s + 1) * HALF], ident[:, :])
                        mm.then_inc(turned if q < 2 else xb_done[q - 2], 1)

                def mixer_in(b, first, last):
                    pe.wait_ge(xnt_ready, b * 5 + 5)
                    for i in range(first, last):
                        c, half = i // 2, i % 2
                        lo, hi = (0, SPLIT) if half == 0 else (SPLIT, SEQ)
                        wait(pe, w_used, b * 12 + (i - 1))
                        for s in range(2):
                            for k, (w, x) in enumerate(((W12H, XNH), (W12H, XNL), (W12L, XNH))):
                                mm = nc.tensor.matmul(bank(W_BANK + i % 2)[:, 0:hi - lo], w[:, s, c * P:(c + 1) * P], x[:, s, lo:hi],
                                                      start=(s + k == 0), stop=(s == 1 and k == 2))
                        mm.then_inc(w_done, 1)

                def mixer_out(b):
                    pe.wait_ge(ag_ready, b * 9 + 9)
                    for t in range(TILES):
                        if t % 2 == 0:
                            wait(pe, wf_used, b * 4 + (t // 2 - 1))
                        for c in range(CT):
                            mm = nc.tensor.matmul(slot(F_BANK, t), AG[:, c, t * P:(t + 1) * P], Wf[:, c, :],
                                                  start=(c == 0), stop=(c == CT - 1))
                        if t % 2 or t == TILES - 1:
                            mm.then_inc(wf_done, 1)

                def norm2_rows(s):
                    transposes(XN2, norm2, s * TILES - TILES, TURN2, (uses(s, 0), uses(s, 1)))

                def logits(s):
                    pe.wait_ge(x2t_ready, s * 4)
                    for j in range(2):
                        pe.wait_ge(xb_used[j], uses(s, j) + 1)
                        for h in range(2):
                            mm = nc.tensor.matmul(bank(X_BANK + j)[:, 0:LSPLIT], PHN[:, h, :], X2T[:, h, j * LSPLIT:(j + 1) * LSPLIT],
                                                  start=(h == 0), stop=(h == 1))
                        mm.then_inc(xb_done[j], 1)

                def logit_rows(s):
                    pe.wait_ge(le_ready, s * 2)
                    pe.wait_ge(xb_used[0], uses(s, 0) + 2)
                    hold(pe, held_pe)
                    for t in range(TILES):
                        mm = nc.tensor.transpose(bank(X_BANK)[:, t * EXP:(t + 1) * EXP], LE[0:EXP, t * P:(t + 1) * P], ident[0:EXP, 0:EXP])
                    mm.then_inc(xb_done[0], 1)

                def softmax_turns(s):
                    pe.wait_ge(d_ready, s * 1)
                    pe.wait_ge(xb_used[1], uses(s, 1) + 2)
                    hold(pe, held_pe)
                    for t in range(TILES):
                        mm = nc.tensor.transpose(bank(X_BANK + 1)[:, t * EXP:(t + 1) * EXP], LE[EXP:P, t * P:(t + 1) * P], ident[EXP:P, EXP:P])
                    mm.then_inc(xb_done[1], 1)
                    pe.wait_ge(ce_ready, s * 1)
                    for j, tiles in ((0, range(0, 4)), (1, range(4, TILES))):
                        pe.wait_ge(xb_used[j], uses(s, j) + 3)
                        for t in tiles:
                            mm = nc.tensor.transpose(bank(X_BANK + j)[:, (t % 4) * P:(t % 4 + 1) * P], CE[:, t, :], ident[:, :])
                        mm.then_inc(xb_done[j], 1)

                def inputs(s):
                    pe.wait_ge(dt_ready, s * 1)
                    pe.wait_ge(xb_used[0], uses(s, 0) + 4)
                    for t in range(TILES):
                        mm = nc.tensor.matmul(bank(X_BANK)[0:EXP, 0:D], DT[:, t, :], XN2[:, t, :], start=(t == 0), stop=(t == TILES - 1))
                    mm.then_inc(xb_done[0], 1)

                def inputs_turn(s):
                    pe.wait_ge(xs_ready, s * 2)
                    pe.wait_ge(xb_used[0], uses_inputs(s))
                    hold(pe, held_pe)
                    for h in range(2):
                        mm = nc.tensor.transpose(bank(X_BANK)[:, h * EXP:(h + 1) * EXP], XS[:, h * P:(h + 1) * P], ident[0:EXP, 0:EXP])
                    mm.then_inc(xb_done[0], 1)

                pe.wait_ge(in_wt, 16)
                embed(0)
                pe.wait_ge(in_const, N_CONST)
                pe.wait_ge(id_ready, 3)
                pe.wait_ge(phi_sq, 1)
                for s in range(2):
                    mm = nc.tensor.matmul(bank(W_BANK)[0:HALF, 0:EXP], ones[:, :], PSQ[:, s, :], start=(s == 0), stop=(s == 1))
                mm.then_inc(phi_sum, 1)
                transposes(XN, norm1, 0, TURN1, (0, 0))
                pe.wait_ge(phi_root, 1)
                pe.wait_ge(phi_ready, 2)
                pe.wait_ge(w12_lo, 1)

                def step(b, before, after):
                    mixer_in(b, 0, 2)
                    if before:
                        norm2_rows(b)
                    mixer_in(b, 2, 4)
                    if before:
                        logits(b)
                    mixer_in(b, 4, 6)
                    if before:
                        logit_rows(b)
                    mixer_in(b, 6, 12)
                    if after:
                        embed(b + 1)
                    if before:
                        softmax_turns(b)
                    mixer_out(b)
                    if before:
                        inputs(b)
                    if after:
                        transposes(XN, norm1, b * TILES + TILES, TURN1, (uses_norm1(b + 1, 0), uses_norm1(b + 1, 1)))
                    if before:
                        inputs_turn(b)

                step(0, False, True)
                with pe.Fori(1, B - 1) as b:
                    step(b, True, True)
                step(B - 1, True, False)
                norm2_rows(B)
                logits(B)
                logit_rows(B)
                softmax_turns(B)
                inputs(B)
                inputs_turn(B)

            @block.scalar
            def _(act):
                def root1_(b):
                    act.wait_ge(var1, b + 1)
                    nc.scalar.activation(sd1[:, :], ve1[:, :], ACT.Sqrt).then_inc(root1, 1)

                def norm1_(b):
                    act.wait_ge(rstd1, b * 2 + 2)
                    for t in range(TILES):
                        nc.scalar.activation(XN[:, t, :], H[:, bass.ds(b, 1), t, :].rearrange("p o d -> p (o d)"), ACT.Identity,
                                             bias=nm1[:, t:t + 1], scale=rs1[:, t:t + 1]).then_inc(norm1, 1)

                def keep_xnt(b):
                    for q in range(4):
                        if q < 2:
                            act.wait_ge(turned, turns(b, 1) + (q + 1))
                        else:
                            act.wait_ge(xb_done[q - 2], uses_norm1(b, q - 2) + 1)
                        for dst, src in turned_columns(q):
                            nc.scalar.activation(XNH[:, :, dst], bank(TURN1[q])[0:HALF, :].rearrange("p (s n) -> p s n", s=2)[:, :, src],
                                                 ACT.Identity).then_inc(xnt_high, 1)

                def keep_a(b, first, last):
                    if first == 0:
                        act.wait_ge(a_pad, 2)
                        wait(act, conv_done, b * CT)
                    for i in range(first, last):
                        c, half = i // 2, i % 2
                        lo, hi = (0, SPLIT) if half == 0 else (SPLIT, SEQ)
                        act.wait_ge(w_done, b * 12 + (i + 1))
                        nc.scalar.activation(A[:, c, TAPS - 1 + lo:TAPS - 1 + hi], bank(W_BANK + i % 2)[:, 0:hi - lo], ACT.Identity,
                                             bias=CHAN[:, c, TAPS + 1:TAPS + 2]).then_inc(a_ready, 1)
                        act.wait_ge(a_ready, b * 6 + (i + 1))
                        act.sem_inc(w_used, 1)

                def combine_exp(s):
                    act.wait_ge(cs_ready, s * 1)
                    nc.scalar.activation(CE[:, :, :].rearrange("p t (r n) -> p t r n", r=2),
                                         CS[:, :, :].unsqueeze(2).broadcast_to([P, TILES, 2, EXP]), ACT.Exp).then_inc(ce_ready, 1)

                def keep_g(b):
                    for c in range(CT):
                        bias = CHAN[:, c, TAPS + 2:TAPS + 3]
                        act.wait_ge(w_done, b * 12 + (6 + 2 * c + 1))
                        src = bank(W_BANK)
                        nc.scalar.activation(AG[:, c, CLS:CLS + 1], src[:, 0:1], ACT.Silu, bias=bias)
                        nc.scalar.activation(AG[:, c, 0:SPLIT - 1], src[:, 1:SPLIT], ACT.Silu, bias=bias).then_inc(w_used, 1)
                        act.wait_ge(w_done, b * 12 + (6 + 2 * c + 2))
                        src = bank(W_BANK + 1)
                        nc.scalar.activation(AG[:, c, SPLIT - 1:NPATCH], src[:, 0:NIMG - SPLIT], ACT.Silu, bias=bias)
                        nc.scalar.activation(AG[:, c, TXT0:TOK], src[:, NIMG - SPLIT:SEQ - SPLIT], ACT.Silu, bias=bias).then_inc(w_used, 1)
                        act.wait_ge(w_used, b * 12 + (6 + 2 * c + 2))
                        act.sem_inc(g_ready, 1)

                def silu_conv(b):
                    for c in range(CT):
                        act.wait_ge(conv_done, b * CT + (c + 1))
                        nc.scalar.activation(CV[:, c, :], CV[:, c, :], ACT.Silu, bias=CHAN[:, c, TAPS:TAPS + 1]).then_inc(silu_done, 1)

                def keep_combine(s):
                    for j, lo, hi in ((0, 0, 4 * P), (1, 4 * P, TOK)):
                        act.wait_ge(xb_done[j], uses(s, j) + 4)
                        nc.scalar.activation(CTt[:, bass.ds(s - 1, 1), lo:hi].rearrange("p o n -> p (o n)"), bank(X_BANK + j)[:, 0:hi - lo],
                                             ACT.Identity).then_inc(xb_used[j], 1)

                def keep_inputs(s):
                    act.wait_ge(xb_done[0], uses(s, 0) + 5)
                    nc.scalar.activation(XS[:, 0:D], bank(X_BANK)[0:EXP, 0:D], ACT.Identity).then_inc(xs_ready, 1)
                    nc.scalar.activation(XS[:, D:4 * EXP], bank(X_BANK)[0:EXP, P:D], ACT.Identity).then_inc(xs_ready, 1)
                    act.wait_ge(xs_ready, s * 2)
                    act.sem_inc(xb_used[0], 1)

                def root2_(b):
                    act.wait_ge(var2, b * 2 + 2)
                    nc.scalar.activation(sd2[:, :, :], ve2[:, :, :], ACT.Sqrt).then_inc(root2, 1)

                def keep_x2t(s):
                    for q in range(4):
                        cols = 256 if q < 3 else P
                        if q < 2:
                            act.wait_ge(turned, turns(s - 1, 2) + (q + 1))
                        else:
                            act.wait_ge(xb_done[q - 2], uses(s, q - 2) + 1)
                        src = bank(TURN2[q])[0:HALF, :].rearrange("p (s n) -> p s n", s=2)[:, :, 0:cols]
                        nc.scalar.activation(X2T[:, :, q * 256:q * 256 + cols], src, ACT.Identity).then_inc(x2t_ready, 1)
                        if q >= 2:
                            act.wait_ge(x2t_ready, s * 4 + (q - 3))
                            act.sem_inc(xb_used[q - 2], 1)

                def keep_logits(s):
                    for j in range(2):
                        act.wait_ge(xb_done[j], uses(s, j) + 2)
                        nc.scalar.activation(LE[:, j * LSPLIT:(j + 1) * LSPLIT], bank(X_BANK + j)[:, 0:LSPLIT], ACT.Identity).then_inc(le_ready, 1)
                        act.wait_ge(le_ready, s * 2 + (j - 1))
                        act.sem_inc(xb_used[j], 1)

                def dispatch_exp(s):
                    act.wait_ge(max_ready, s * 4)
                    for i, (lo, hi) in enumerate(SEG):
                        nc.scalar.activation(LE[EXP:P, lo:hi], LE[EXP:P, lo:hi], ACT.Exp, bias=nmx[EXP:P, :],
                                             accum_out=es[EXP:P, i:i + 1]).then_inc(exp_done, 1)

                act.wait_ge(in_const, N_CONST)
                nc.scalar.activation(W12H[:, :, :], W12[:, :, :], ACT.Identity).then_inc(w12_hi, 1)
                act.wait_ge(phi_sum, 1)
                nc.scalar.activation(pn[:, :], bank(W_BANK)[0:HALF, 0:EXP], ACT.Sqrt).then_inc(phi_root, 1)
                root1_(0)
                norm1_(0)
                keep_xnt(0)

                def step(b, before, after):
                    keep_a(b, 0, 2)
                    if before:
                        keep_x2t(b)
                    keep_a(b, 2, 4)
                    if before:
                        keep_logits(b)
                    keep_a(b, 4, 6)
                    keep_g(b)
                    silu_conv(b)
                    if before:
                        dispatch_exp(b)
                        combine_exp(b)
                    if after:
                        root1_(b + 1)
                    if before:
                        keep_combine(b)
                    if after:
                        norm1_(b + 1)
                    root2_(b)
                    if before:
                        keep_inputs(b)
                    if after:
                        keep_xnt(b + 1)

                step(0, False, True)
                with act.Fori(1, B - 1) as b:
                    step(b, True, True)
                step(B - 1, True, False)
                keep_x2t(B)
                keep_logits(B)
                dispatch_exp(B)
                combine_exp(B)
                keep_combine(B)
                keep_inputs(B)

            @block.vector
            def _(dve):
                def row(b, t):
                    return H[:, bass.ds(b, 1), t, :].rearrange("p o d -> p (o d)")

                def rows(b, q):
                    return H[:, bass.ds(b, 1), 2 * q:2 * q + 2, :].rearrange("p o t d -> p (o t) d")

                def norm_in(b, middle):
                    def stats(*tiles):
                        for t in tiles:
                            nc.vector.bn_stats(st1[:, t, :], row(b, t)).then_inc(stats1, 1)

                    for q in range(3):
                        wait(dve, emb_used, b * 3 + q)
                        dve.wait_ge(emb_done, b * 3 + (q + 1))
                        if q < 2:
                            nc.vector.tensor_tensor(rows(b, q), both(E_BANK, q), PB[:, 2 * q:2 * q + 2, :], ALU.add).then_inc(emb_used, 1)
                        else:
                            nc.vector.tensor_tensor(row(b, 4), slot(E_BANK, 4), PB[:, 4, :], ALU.add)
                            nc.vector.tensor_tensor(row(b, 5)[0:LASTP], slot(E_BANK, 5)[0:LASTP], PB[0:LASTP, 5, :], ALU.add).then_inc(emb_used, 1)
                        stats(*((6,), (0, 1), (2, 3))[q])
                        if q == 1 and middle:
                            middle()
                    dve.wait_ge(emb_used, b * 3 + 3)
                    hold(dve, held_dve)
                    stats(4, 5)
                    dve.wait_ge(stats1, b * TILES + TILES)
                    hold(dve, held_dve)
                    for t in range(TILES):
                        nc.vector.bn_aggr(mv1[:, t, :], st1[:, t, :]).then_inc(mean1, 1)
                    dve.wait_ge(mean1, b * TILES + TILES)
                    nc.vector.tensor_scalar(ve1[:, :], mv1[:, :, 1], EPS_LN, None, ALU.add).then_inc(var1, 1)
                    dve.wait_ge(root1, b + 1)
                    nc.vector.reciprocal(rs1[:, :], sd1[:, :]).then_inc(rstd1, 1)
                    dve.wait_ge(rstd1, b * 2 + 1)
                    nc.vector.scalar_tensor_tensor(out=nm1[:, :], in0=mv1[:, :, 0], scalar=-1.0, in1=rs1[:, :], op0=ALU.mult, op1=ALU.mult).then_inc(rstd1, 1)

                def keep_xnt(b):
                    done = 0
                    for q in range(4):
                        done += len(turned_columns(q))
                        dve.wait_ge(xnt_high, b * 5 + done)
                        for dst, src in turned_columns(q):
                            nc.vector.tensor_tensor(XNL[:, :, dst], bank(TURN1[q])[0:HALF, :].rearrange("p (s n) -> p s n", s=2)[:, :, src],
                                                    XNH[:, :, dst].bitcast(F32), ALU.subtract).then_inc(xnt_ready, 1)
                        if q >= 2:
                            dve.wait_ge(xnt_ready, b * 5 + done)
                            dve.sem_inc(xb_used[q - 2], 1)

                def conv(b, channels):
                    for c in channels:
                        dve.wait_ge(a_ready, b * 6 + (2 * c + 2))
                        wait(dve, ag_ready, b * 9 + (3 * c - 6))
                        cv = CV[:, c, :]
                        nc.vector.tensor_scalar(cv, A[:, c, 0:SEQ], CHAN[:, c, 0:1], None, ALU.mult).then_inc(tap_done, 1)
                        for k in range(1, TAPS):
                            dve.wait_ge(tap_done, b * 9 + (3 * c + k))
                            mm = nc.vector.scalar_tensor_tensor(out=cv, in0=A[:, c, k:k + SEQ], scalar=CHAN[:, c, k:k + 1], in1=cv, op0=ALU.mult, op1=ALU.add)
                            mm.then_inc(tap_done if k < TAPS - 1 else conv_done, 1)

                def norm_mid(b, before, after):
                    dve.wait_ge(bf_added, b + 1)
                    def stats(*tiles):
                        for t in tiles:
                            nc.vector.bn_stats(st2[:, t, :], row(b, t)).then_inc(stats2, 1)

                    for q in range(4):
                        wait(dve, wf_used, b * 4 + q)
                        dve.wait_ge(wf_done, b * 4 + (q + 1))
                        if q < 3:
                            nc.vector.tensor_tensor(rows(b, q), both(F_BANK, q), rows(b, q), ALU.add).then_inc(wf_used, 1)
                        else:
                            nc.vector.tensor_tensor(row(b, 6), slot(F_BANK, 6), row(b, 6), ALU.add).then_inc(wf_used, 1)
                        if q > 0:
                            stats(2 * q - 2, 2 * q - 1)
                    dve.wait_ge(wf_used, b * 4 + 4)
                    hold(dve, held_dve)
                    stats(6)
                    dve.wait_ge(stats2, b * TILES + TILES)
                    hold(dve, held_dve)
                    for t in range(TILES):
                        nc.vector.bn_aggr(mv2[:, t, :], st2[:, t, :]).then_inc(mean2, 1)
                    dve.wait_ge(mean2, b * TILES + TILES)
                    nc.vector.tensor_scalar(ve2[:, 0, :], mv2[:, :, 1], EPS_LN, None, ALU.add).then_inc(var2, 1)
                    nc.vector.tensor_scalar(ve2[:, 1, :], mv2[:, :, 1], float(D), None, ALU.mult).then_inc(var2, 1)
                    if after:
                        keep_xnt(b + 1)
                    dve.wait_ge(root2, b + 1)
                    nc.vector.reciprocal(rs2[:, :], sd2[:, 0, :]).then_inc(len2, 1)
                    dve.wait_ge(len2, b * 5 + 1)
                    nc.vector.tensor_tensor(nr2[:, :], sd2[:, 1, :], rs2[:, :], ALU.mult).then_inc(len2, 1)
                    dve.wait_ge(len2, b * 5 + 2)
                    nc.vector.tensor_scalar(nq2[:, :], nr2[:, :], EPS_L2, None, ALU.max).then_inc(len2, 1)
                    dve.wait_ge(len2, b * 5 + 3)
                    nc.vector.reciprocal(ri2[:, :], nq2[:, :]).then_inc(len2, 1)
                    dve.wait_ge(len2, b * 5 + 4)
                    nc.vector.tensor_tensor(sc2[:, :], rs2[:, :], ri2[:, :], ALU.mult).then_inc(len2, 1)
                    if before:
                        dve.wait_ge(xb_done[0], uses(b, 0) + 5)
                    dve.wait_ge(len2, b * 5 + 5)
                    for t in range(TILES):
                        nc.vector.tensor_scalar(XN2[:, t, :], row(b, t), mv2[:, t, 0:1], sc2[:, t:t + 1], ALU.subtract, ALU.mult).then_inc(norm2, 1)

                def dispatch_max(s):
                    dve.wait_ge(le_ready, s * 2)
                    for i, (lo, hi) in enumerate(SEG):
                        nc.vector.reduce_max(mx2[EXP:P, i:i + 1], LE[EXP:P, lo:hi], AX.X).then_inc(max_ready, 1)
                    dve.wait_ge(max_ready, s * 4 - 2)
                    nc.vector.tensor_tensor(mxa[EXP:P, :], mx2[EXP:P, 0:1], mx2[EXP:P, 1:2], ALU.max).then_inc(max_ready, 1)
                    dve.wait_ge(max_ready, s * 4 - 1)
                    nc.vector.tensor_scalar(nmx[EXP:P, :], mxa[EXP:P, :], -1.0, None, ALU.mult).then_inc(max_ready, 1)

                def dispatch_scale(s):
                    dve.wait_ge(exp_done, s * 2)
                    nc.vector.tensor_tensor(esum[EXP:P, :], es[EXP:P, 0:1], es[EXP:P, 1:2], ALU.add).then_inc(rec_done, 1)
                    dve.wait_ge(rec_done, s * 2 - 1)
                    nc.vector.reciprocal(erec[EXP:P, :], esum[EXP:P, :]).then_inc(rec_done, 1)
                    dve.wait_ge(rec_done, s * 2)
                    dve.wait_ge(pad_done, s * 1)
                    nc.vector.tensor_scalar(LE[EXP:P, :], LE[EXP:P, :], erec[EXP:P, :], None, ALU.mult).then_inc(d_ready, 1)

                def combine_max(s):
                    dve.wait_ge(xb_done[0], uses(s, 0) + 3)
                    src = bank(X_BANK)[:, 0:TILES * EXP].rearrange("p (t n) -> p t n", n=EXP)
                    nc.vector.reduce_max(rmx[:, :], src, AX.X).then_inc(rmax_done, 1)
                    dve.wait_ge(rmax_done, s * 1)
                    nc.vector.tensor_tensor(CS[:, :, :], src, rmx[:, :].unsqueeze(2).broadcast_to([P, TILES, EXP]), ALU.subtract).then_inc(cs_ready, 1)
                    dve.wait_ge(cs_ready, s * 1)
                    dve.sem_inc(xb_used[0], 1)

                def combine_sum(s):
                    dve.wait_ge(ce_ready, s * 1)
                    nc.vector.reduce_sum(rsm[:, :], CE[:, :, 0:EXP], AX.X).then_inc(rsum_done, 1)
                    dve.wait_ge(rsum_done, s * 2 - 1)
                    nc.vector.reciprocal(RC[:, bass.ds(s - 1, 1), :].rearrange("p o t -> p (o t)"), rsm[:, :]).then_inc(rsum_done, 1)

                def keep_dispatch(s):
                    dve.wait_ge(xb_done[1], uses(s, 1) + 3)
                    nc.vector.tensor_copy(DT[:, :, :], bank(X_BANK + 1)[:, 0:TILES * EXP].rearrange("p (t n) -> p t n", n=EXP)).then_inc(dt_ready, 1)
                    dve.wait_ge(dt_ready, s * 1)
                    dve.sem_inc(xb_used[1], 1)

                def keep_xt(s):
                    dve.wait_ge(xb_done[0], uses_inputs(s) + 1)
                    nc.vector.tensor_copy(XT[:, :, bass.ds(s - 1, 1), :].rearrange("p h o n -> p h (o n)"),
                                          bank(X_BANK)[:, 0:2 * EXP].rearrange("p (h n) -> p h n", h=2)).then_inc(xb_used[0], 1)

                dve.wait_ge(in_pos, 6 * 16)
                nc.vector.tensor_tensor(PB[:, 0:5, :], PB[:, 0:5, :], TBb[:, :].unsqueeze(1).broadcast_to([P, 5, D]), ALU.add).then_inc(pos_ready, 1)
                nc.vector.tensor_tensor(PB[0:LASTP + 1, 5, :], PB[0:LASTP + 1, 5, :], CB[0:LASTP + 1, :], ALU.add).then_inc(pos_ready, 1)
                dve.wait_ge(in_const, N_CONST)
                nc.vector.tensor_tensor(PSQ[:, :, :], PHI[:, :, :], PHI[:, :, :], ALU.mult).then_inc(phi_sq, 1)
                dve.wait_ge(pos_ready, 2)
                dve.wait_ge(in_cls, 16)
                norm_in(0, None)
                dve.wait_ge(phi_root, 1)
                nc.vector.tensor_scalar(pr[:, :], pn[:, :], EPS_L2, None, ALU.max).then_inc(phi_clip, 1)
                dve.wait_ge(phi_clip, 1)
                nc.vector.reciprocal(pn[:, :], pr[:, :]).then_inc(phi_rec, 1)
                dve.wait_ge(phi_rec, 1)
                nc.vector.tensor_scalar(pr[:, :], pn[:, :], SC[:, 0:1], None, ALU.mult).then_inc(phi_sc, 1)
                dve.wait_ge(phi_sc, 1)
                for s in range(2):
                    nc.vector.tensor_tensor(PHN[:, s, :].rearrange("p (r n) -> p r n", r=2), PHI[:, s, :].unsqueeze(1).broadcast_to([HALF, 2, EXP]),
                                            pr[:, :].unsqueeze(1).broadcast_to([HALF, 2, EXP]), ALU.mult).then_inc(phi_ready, 1)
                dve.wait_ge(w12_hi, 1)
                nc.vector.tensor_tensor(W12L[:, :, :], W12[:, :, :], W12H[:, :, :].bitcast(F32), ALU.subtract).then_inc(w12_lo, 1)
                keep_xnt(0)

                def step(b, before, after):
                    conv(b, (0, 1))
                    if before:
                        dispatch_max(b)
                        combine_max(b)
                    conv(b, (2,))

                    def scales():
                        dispatch_scale(b)
                        combine_sum(b)

                    if after:
                        norm_in(b + 1, scales if before else None)
                    elif before:
                        scales()
                    if before:
                        keep_dispatch(b)
                    norm_mid(b, before, after)
                    if before:
                        keep_xt(b)

                step(0, False, True)
                with dve.Fori(1, B - 1) as b:
                    step(b, True, True)
                step(B - 1, True, False)
                dispatch_max(B)
                combine_max(B)
                dispatch_scale(B)
                combine_sum(B)
                keep_dispatch(B)
                keep_xt(B)

        hi_done, lo_done, w_spent = sem("hi_done"), sem("lo_done"), sem("w_spent")
        xpd_zero, xp_hi, xp_ready = sem("xpd_zero"), sem("xp_hi"), sem("xp_ready")
        hs_ready, t_done, hb_ready, hg_ready, hh_hi, hh_ready = (sem(n) for n in ("hs_ready", "t_done", "hb_ready", "hg_ready", "hh_hi", "hh_ready"))
        ys_ready, sel_ready = sem("ys_ready"), sem("sel_ready")
        ys_sent = [sem(f"ys_sent{p}") for p in range(PAIRS)]
        yb_ready, o_done, o_ready, stored = sem("yb_ready"), sem("o_done"), sem("o_ready"), sem("stored")

        def unit_w1(g, p):
            return p if isinstance(g, int) and g == 0 else g * 8 + (2 * p - 4)

        def unit_w2(g, p):
            return 60 + p if isinstance(g, int) and g == NG else g * 8 + (2 * p - 3)

        def slot_w1(g, p):
            return p if isinstance(g, int) and g == 0 else (2 * p + 4) % 8

        def slot_w2(g, p):
            return 4 + p if isinstance(g, int) and g == NG else (2 * p + 5) % 8

        def loads(g, k, s, second):
            if isinstance(g, int) and g in (0, NG):
                return 1 if g == 0 else 8
            return g + (1 if (2 * k + (5 if second else 4)) >= 8 else 0)

        with nc.Block() as block:
            @block.sync
            def _(sp):
                def load(g, p, second):
                    k = unit_w2(g, p) if second else unit_w1(g, p)
                    wait(sp, w_spent, k * 3 - 21)
                    if second:
                        load_w2(sp, slot_w2(g, p), g * GROUP + (2 * p - GROUP))
                    else:
                        load_w1(sp, slot_w1(g, p), g * GROUP + 2 * p)

                for p in range(PAIRS // 2, PAIRS):
                    load(1, p, False)
                    load(1, p, True)
                with sp.Fori(2, NG) as g:
                    for p in range(PAIRS):
                        load(g, p, False)
                        load(g, p, True)
                for p in range(PAIRS):
                    load(NG, p, True)

            @block.gpsimd
            def _(pool):
                nc.gpsimd.memset(XPD[:, :].bitcast(F32), 0.0).then_inc(xpd_zero, 1)
                nc.gpsimd.memset(SEL[:, :], 0.0).then_inc(sel_ready, 1)
                pool.wait_ge(sel_ready, 1)
                for part in range(2):
                    sel = SEL[:, 0:EXP].rearrange("p (e b) -> p e b", e=GROUP)
                    nc.gpsimd.affine_select(out=sel, in_=sel, compare_op=ALU.not_equal, fill=1.0, base=-8 * part,
                                            pattern=[[-16, GROUP], [-1, B]], channel_multiplier=1).then_inc(sel_ready, 1)
                    pool.wait_ge(sel_ready, part + 2)

                def send(g):
                    for p in range(PAIRS):
                        pool.wait_ge(ys_ready, g * PAIRS + (p + 1))
                        for k in range(2):
                            e = 2 * p + k
                            for r in range(2):
                                n = g * GROUP + e + EXP * r
                                dst = YB[n:n + 1, :, :]
                                pool.dma_start(dst, YS[16 * e + B * r:16 * e + B * r + B, p, k * D:(k + 1) * D]).then_inc(ys_sent[p], 16)

                for g in range(NG):
                    send(g)
                for p in range(PAIRS):
                    pool.wait_ge(ys_sent[p], NG * 64)

            @block.tensor
            def _(pe):
                def first(g, p):
                    k, s = unit_w1(g, p), slot_w1(g, p)
                    if p == 0:
                        pe.wait_ge(xp_ready, g * 4 + 4)
                        wait(pe, hs_ready, g * 2)
                    for c in range(3):
                        pe.wait_ge(lo_done, k * 3 + (c + 1))
                        x = XPD[:, (3 * p + c) * P:(3 * p + c + 1) * P]
                        ring = (3 * s + c) % HIS
                        for n in range(2):
                            cols = slice(n * HID, (n + 1) * HID)
                            for i, w in enumerate((WH[:, ring, cols], low(s)[:, c * CHUNK + n * HID:c * CHUNK + (n + 1) * HID])):
                                mm = nc.tensor.matmul(bank(H_BANK + n)[:, 0:HID], x, w,
                                                      start=(p == 0 and c == 0 and i == 0), stop=(p == PAIRS - 1 and c == 2 and i == 1))
                        mm.then_inc(w_spent, 1)

                def turn(g):
                    pe.wait_ge(hs_ready, g * 2 + 2)
                    wait(pe, hb_ready, g * 2)
                    hs = HS[:, :].rearrange("p (n j) -> p n j", j=KJ)
                    for j in range(KJ):
                        at = (j % 3) * 96
                        mm = nc.tensor.matmul(bank(T_BANK + j // 3)[:, at:at + 96], hs[:, :, j], SEL[:, :], start=True, stop=True)
                        if j % 3 == 2:
                            mm.then_inc(t_done, 1)

                def second(g, p):
                    k, s = unit_w2(g, p), slot_w2(g, p)
                    n = g * PAIRS + (p - PAIRS)
                    if p == 0:
                        pe.wait_ge(hh_ready, g * 1)
                    wait(pe, ys_ready, n - (0 if p == 0 else 1))
                    for c in range(3):
                        pe.wait_ge(lo_done, k * 3 + (c + 1))
                        ring = (3 * s + c) % HIS
                        for j in range(2):
                            x = HH[:, 2 * c + j, :, :, :].rearrange("p e r b -> p (e r b)")
                            for i, w in enumerate((WH[:, ring, :], low(s)[:, c * CHUNK:(c + 1) * CHUNK])):
                                w = w.rearrange("p (e j d) -> p e j d", e=2, j=2)[:, :, j, :]
                                mm = nc.tensor.matmul(bank(Y_BANK + p % 2)[:, 0:2 * D], x, w,
                                                      start=(c + j + i == 0), stop=(c == 2 and j == 1 and i == 1))
                        mm.then_inc(w_spent, 1)

                pe.wait_ge(sel_ready, 3)
                for p in range(PAIRS):
                    first(0, p)
                turn(0)
                with pe.Fori(1, NG) as g:
                    for p in range(PAIRS):
                        first(g, p)
                        second(g, p)
                    turn(g)
                for p in range(PAIRS):
                    second(NG, p)

            @block.scalar
            def _(act):
                def high(g, p, second):
                    k, s = (unit_w2(g, p), slot_w2(g, p)) if second else (unit_w1(g, p), slot_w1(g, p))
                    act.wait_ge(staged[s], loads(g, p, s, second) * 48)
                    for c in range(3):
                        wait(act, w_spent, k * 3 + (c - 5))
                        nc.scalar.activation(WH[:, (3 * s + c) % HIS, :], stage(s)[:, c * CHUNK:(c + 1) * CHUNK], ACT.Identity).then_inc(hi_done, 1)

                def keep_h(g):
                    act.wait_ge(w_spent, unit_w1(g, PAIRS - 1) * 3 + 3)
                    wait(act, t_done, g * 2)
                    for n in range(2):
                        nc.scalar.activation(HS[:, n * HID:(n + 1) * HID], bank(H_BANK + n)[:, 0:HID], ACT.Identity).then_inc(hs_ready, 1)

                def keep_y(g, p):
                    act.wait_ge(w_spent, unit_w2(g, p) * 3 + 3)
                    wait(act, ys_sent[p], g * 64 - 64 if not (isinstance(g, int)) or g > 1 else 0)
                    nc.scalar.activation(YS[:, p, :], bank(Y_BANK + p % 2)[:, 0:2 * D], ACT.Identity).then_inc(ys_ready, 1)

                def gelu(g):
                    act.wait_ge(hb_ready, g * 2 + 2)
                    nc.scalar.activation(HG[:, :], HB[:, :], ACT.Gelu).then_inc(hg_ready, 1)
                    act.wait_ge(hg_ready, g + 1)
                    hg = HG[:, :].rearrange("p (n b) -> p n b", b=B)
                    nc.scalar.activation(HH[:, :, :, 0, :].rearrange("p j e b -> p (j e) b"), hg, ACT.Identity).then_inc(hh_hi, 1)

                for p in range(PAIRS):
                    high(0, p, False)
                keep_h(0)
                with act.Fori(1, NG) as g:
                    for p in range(PAIRS):
                        high(g, p, False)
                        if p == 0:
                            gelu(g - 1)
                        high(g, p, True)
                        if p > 0:
                            keep_y(g, p - 1)
                    keep_y(g, PAIRS - 1)
                    keep_h(g)
                gelu(NG - 1)
                for p in range(PAIRS):
                    high(NG, p, True)
                    if p > 0:
                        keep_y(NG, p - 1)
                keep_y(NG, PAIRS - 1)

            @block.vector
            def _(dve):
                def diagonal(g):
                    if not (isinstance(g, int) and g == 0):
                        dve.wait_ge(w_spent, (unit_w1(g - 1, PAIRS - 1) if not (isinstance(g, int) and g == 1) else PAIRS - 1) * 3 + 3)
                    x = XT[:, :, :, bass.ds(g * GROUP, GROUP)]
                    for part in range(2):
                        for n, (r, s, k, at) in enumerate(((slice(0, P), 0, 0, 0), (slice(0, P), 0, 1, P + 16), (slice(0, 64), 1, 0, 2 * P), (slice(64, P), 1, 1, 2 * P + 16))):
                            src = x[r, s, :, :].rearrange("p b (q k) -> p q b k", k=2)[:, :, :, k]
                            hi = diag(r, at)
                            if part == 0:
                                nc.vector.tensor_copy(hi, src).then_inc(xp_hi, 1)
                            else:
                                dve.wait_ge(xp_hi, g * 4 + (n + 1))
                                nc.vector.tensor_tensor(diag(r, at + B), src, hi.bitcast(F32), ALU.subtract).then_inc(xp_ready, 1)

                def diag(r, at):
                    step = 3 * P + 32
                    return XPD[r, at:at + 4 * step].rearrange("p (q c) -> p q c", c=step)[:, :, 0:B]

                def low_part(g, p, second):
                    k, s = (unit_w2(g, p), slot_w2(g, p)) if second else (unit_w1(g, p), slot_w1(g, p))
                    for c in range(3):
                        dve.wait_ge(hi_done, k * 3 + (c + 1))
                        cols = slice(c * CHUNK, (c + 1) * CHUNK)
                        nc.vector.tensor_tensor(low(s)[:, cols], stage(s)[:, cols], WH[:, (3 * s + c) % HIS, :].bitcast(F32), ALU.subtract).then_inc(lo_done, 1)

                def bias(g):
                    for i in range(2):
                        dve.wait_ge(t_done, g * 2 + (i + 1))
                        if i == 0:
                            wait(dve, hg_ready, g * 1)
                        src = bank(T_BANK + i)[:, 0:3 * 96].rearrange("p (j n) -> p j n", j=3)[:, :, 0:EXP]
                        for j in range(3):
                            jj = 3 * i + j
                            last = nc.vector.tensor_tensor(HB[:, jj * EXP:(jj + 1) * EXP].rearrange("p (e b) -> p e b", b=B),
                                                           src[:, j, :].rearrange("p (e b) -> p e b", b=B),
                                                           b1T[:, bass.ds(g * GROUP, GROUP), jj:jj + 1].broadcast_to([P, GROUP, B]), ALU.add)
                        last.then_inc(hb_ready, 1)

                def hidden_low(g):
                    dve.wait_ge(hh_hi, g + 1)
                    nc.vector.tensor_tensor(HH[:, :, :, 1, :].rearrange("p j e b -> p (j e) b"), HG[:, :].rearrange("p (n b) -> p n b", b=B),
                                            HH[:, :, :, 0, :].rearrange("p j e b -> p (j e) b").bitcast(F32), ALU.subtract).then_inc(hh_ready, 1)

                dve.wait_ge(xpd_zero, 1)
                diagonal(0)
                for p in range(PAIRS):
                    low_part(0, p, False)
                diagonal(1)
                bias(0)
                with dve.Fori(1, NG - 1) as g:
                    for p in range(PAIRS):
                        low_part(g, p, False)
                        if p == 0:
                            hidden_low(g - 1)
                        low_part(g, p, True)
                    diagonal(g + 1)
                    bias(g)
                for p in range(PAIRS):
                    low_part(NG - 1, p, False)
                    if p == 0:
                        hidden_low(NG - 2)
                    low_part(NG - 1, p, True)
                bias(NG - 1)
                hidden_low(NG - 1)
                for p in range(PAIRS):
                    low_part(NG, p, True)

        with nc.Block() as block:
            @block.vector
            def _(dve):
                for b in range(B):
                    nc.vector.tensor_tensor(YB[0:EXP, b, :], YB[0:EXP, b, :], b2e[:, :], ALU.add).then_inc(yb_ready, 1)
                for b in range(B):
                    for t in range(TILES):
                        n = b * TILES + t
                        dve.wait_ge(o_done, n + 1)
                        nc.vector.scalar_tensor_tensor(out=H[:, b, t, :], in0=bank(n % 8)[:, 0:D], scalar=RC[:, b, t:t + 1], in1=H[:, b, t, :],
                                                       op0=ALU.mult, op1=ALU.add).then_inc(o_ready, 1)

            @block.tensor
            def _(pe):
                for b in range(B):
                    pe.wait_ge(yb_ready, b + 1)
                    for t in range(TILES):
                        n = b * TILES + t
                        wait(pe, o_ready, n - 7)
                        nc.tensor.matmul(bank(n % 8)[:, 0:D], CTt[:, b, t * P:(t + 1) * P], YB[:, b, :], start=True, stop=True).then_inc(o_done, 1)

            @block.sync
            def _(sp):
                for b in range(B):
                    sp.wait_ge(o_ready, b * TILES + TILES)
                    sp.dma_start(out[b, 1:1 + 5 * P, :].rearrange("(t p) d -> p t d", p=P), H[:, b, 0:5, :]).then_inc(stored, 16)
                    sp.dma_start(out[b, 1 + 5 * P:NIMG, :], H[0:LASTP, b, 5, :]).then_inc(stored, 16)
                    sp.dma_start(out[b, 0:1, :], H[LASTP:LASTP + 1, b, 5, :]).then_inc(stored, 16)
                    sp.dma_start(out[b, NIMG:SEQ, :], H[:, b, 6, :]).then_inc(stored, 16)
                sp.wait_ge(stored, B * 4 * 16)


def kernel(**inputs):
    import numpy as np
    import concourse.bacc as bacc
    from concourse.bass_utils import run_bass_kernel_spmd

    def arr(name):
        return np.ascontiguousarray(inputs[name])

    x = arr("x").reshape(B, CH, GRID + 1, 8, 28, 8)
    left, right = x[..., :GRID, :], x[..., 1:, :]
    strips = np.concatenate([left, right], axis=-1)
    strips = np.ascontiguousarray(strips.transpose(0, 3, 5, 1, 2, 4)).reshape(B, P, CH, BLOCKS)
    filt = arr("L0_tok_w").reshape(D, CH, 2, 8, 16).transpose(3, 4, 1, 2, 0)
    filt = np.ascontiguousarray(filt).reshape(P, CH, 2, D)
    columns = [arr("L0_attn_conv_w").reshape(CT, P, TAPS)] + [arr(n).reshape(CT, P, 1) for n in ("L0_attn_conv_b", "L0_attn_b1", "L0_attn_b2")]
    chan = np.ascontiguousarray(np.concatenate(columns, axis=2).transpose(1, 0, 2))
    eb1 = np.ascontiguousarray(arr("L0_ffn_b1").reshape(EXP, P, KJ).transpose(1, 0, 2))
    arrays = {
        "xp": strips, "txt": arr("txt"), "wt": filt, "tb": arr("L0_tok_b"),
        "cls": arr("L0_tok_cls_token").reshape(1, D), "pos": arr("L0_tok_pos_embedding").reshape(NIMG, D),
        "w1": arr("L0_attn_W1"), "w2": arr("L0_attn_W2"), "chan": chan, "wf": arr("L0_attn_Wf"), "bf": arr("L0_attn_bf"),
        "phi": arr("L0_ffn_phi"), "scale": arr("L0_ffn_scale"), "ew1": arr("L0_ffn_w1"), "eb1": eb1,
        "ew2": arr("L0_ffn_w2"), "eb2": arr("L0_ffn_b2"),
    }
    nc = bacc.Bacc("TRN2", target_bir_lowering=False, num_devices=1)
    args = [nc.dram_tensor(f"in_{n}", a.shape, mybir.dt.from_np(a.dtype), kind="ExternalInput").ap() for n, a in arrays.items()]
    o = nc.dram_tensor("out_0", (B, SEQ, D), F32, kind="ExternalOutput").ap()
    build(nc, *args, o)
    r = run_bass_kernel_spmd(nc, [{f"in_{n}": a for n, a in arrays.items()}], core_ids=[0])
    return r.results[0]["out_0"]
```

```python
from contextlib import ExitStack

import concourse.bass as bass
from concourse import mybir

F32 = mybir.dt.float32
F32R = mybir.dt.float32r
ALU = mybir.AluOpType
ACT = mybir.ActivationFunctionType
AX = mybir.AxisListType

B = 8
P = 128
D = 192
HALF = D // 2
HID = 384
CT = HID // P
TAPS = 4
GRID = 27
NPATCH = GRID * GRID
NIMG = NPATCH + 1
NTXT = 128
SEQ = NIMG + NTXT
BLOCKS = (GRID + 1) * GRID
CH = 3
TILES = 7
TOK = TILES * P
LASTP = NPATCH - 5 * P
CLS = 5 * P + LASTP
TXT0 = 6 * P
SPLIT = 430
LSPLIT = TOK // 2
EXP = 64
FF = 768
KJ = FF // P
GROUP = 8
NG = EXP // GROUP
PAIRS = GROUP // 2
UNIT = 3 * FF
CHUNK = UNIT // 3
SLOTS = 8
SLOT_AFTER_EMBED = 3
SLOT_AFTER_MIXER = 6
SLOT_AFTER_CONV = 7
ORDER = ((0, 0), (0, 1), (1, 0), (0, 2), (1, 1), (0, 3), (1, 2), (1, 3))
HIS = 6
EPS_LN = 1e-5
EPS_L2 = 1e-12
SEG = ((0, NIMG), (TXT0, TOK))


def now(x):
    return x() if callable(x) else x


def build(nc, xp, txt, wt, tb, cls, pos, w1, w2, chan, wf, bf, phi, scale, ew1, eb1, ew2, eb2, out):
    with ExitStack() as ctx:
        def sb(name, shape, dt=F32):
            return ctx.enter_context(nc.sbuf_tensor(name, shape, dt))

        def sem(name):
            return ctx.enter_context(nc.semaphore(name))

        H = sb("H", [P, B, TILES, D])
        CTt = sb("CTt", [P, B, TOK])
        XT = sb("XT", [P, 2, B, EXP])
        RC = sb("RC", [P, B, TILES])
        ident = sb("ident", [P, P])
        b1T = sb("b1T", [P, EXP, KJ])
        b2e = sb("b2e", [EXP, D])
        base = (now(nc.sbuf_base) + 31) // 32 * 32
        end = now(nc.sbuf_usable_end)

        def arena():
            at = [base]

            def take(name, shape, dt=F32):
                size = 4
                for n in shape[1:]:
                    size *= n
                t = nc.alloc_sbuf_tensor_at(name, shape, dt, offset=at[0])
                at[0] += (size + 31) // 32 * 32
                assert at[0] <= end, (name, at[0], end)
                return t
            take.at = at
            return take

        one = arena()
        X = one("X", [P, CH, BLOCKS])
        XL = nc.alloc_sbuf_tensor_at("XL", [P, CH, BLOCKS], F32R, offset=base)
        XH = one("XH", [P, CH, BLOCKS], F32R)
        WtHL = one("WtHL", [P, CH, 2, 2, D], F32R)
        PB = one("PB", [P, 6, D])
        PHI = one("PHI", [HALF, 2, EXP])
        assert one.at[0] >= base + SLOT_AFTER_EMBED * UNIT * 4
        XNH = one("XNH", [P, SEQ], F32R)
        XNL = one("XNL", [P, SEQ], F32R)
        XNR = one("XNR", [P, SEQ], F32R)
        w12_at = one.at[0]
        W12 = one("W12", [P, 2, 2 * HID])
        W12L = nc.alloc_sbuf_tensor_at("W12L", [P, 2, 2 * HID], F32R, offset=w12_at)
        W12H = one("W12H", [P, 2, 2 * HID], F32R)
        pn = one("pn", [HALF, EXP])
        assert one.at[0] >= base + SLOT_AFTER_MIXER * UNIT * 4
        A = one("A", [P, CT, TAPS - 1 + SEQ])
        assert one.at[0] >= base + SLOT_AFTER_CONV * UNIT * 4
        CV = one("CV", [P, CT, SEQ])
        assert one.at[0] >= base + SLOTS * UNIT * 4
        CHAN = one("CHAN", [P, CT, TAPS + 3])
        Wf = one("Wf", [P, CT, D])
        BF = one("BF", [P, D])
        XN = one("XN", [P, TILES, 2 * P])
        AG = one("AG", [P, CT, TOK])
        wh_end = one.at[0]
        X2T = one("X2T", [HALF, 2, TOK])
        PHN = one("PHN", [HALF, 2, 2 * EXP])
        xpd_end = one.at[0]
        XN2 = one("XN2", [P, TILES, D])
        DT = one("DT", [P, TILES, EXP])
        XS = one("XS", [EXP, 4 * EXP])
        SC = one("SC", [HALF, 1])
        pr = one("pr", [HALF, EXP])
        nm1 = one("nm1", [P, TILES])
        st1 = one("st1", [P, TILES, 6])
        mv1 = one("mv1", [P, TILES, 2])
        ve1 = one("ve1", [P, TILES])
        sd1 = one("sd1", [P, TILES])
        rs1 = one("rs1", [P, TILES])
        st2 = one("st2", [P, TILES, 6])
        mv2 = one("mv2", [P, TILES, 2])
        ve2 = one("ve2", [P, 2, TILES])
        sd2 = one("sd2", [P, 2, TILES])
        rs2 = one("rs2", [P, TILES])
        nr2 = one("nr2", [P, TILES])
        nq2 = one("nq2", [P, TILES])
        ri2 = one("ri2", [P, TILES])
        sc2 = one("sc2", [P, TILES])
        mx2 = one("mx2", [P, 2])
        mxa = one("mxa", [P, 1])
        nmx = one("nmx", [P, 1])
        es = one("es", [P, 2])
        esum = one("esum", [P, 1])
        erec = one("erec", [P, 1])
        hh_end = one.at[0]
        LE = one("LE", [P, TOK])
        CS = one("CS", [P, TILES, EXP])
        CE = one("CE", [P, TILES, 2 * EXP])
        rmx = one("rmx", [P, TILES])
        unused = one("unused", [P, 1])
        rsm = one("rsm", [P, TILES])
        CB, TBb = XN[:, 0, 0:D], XN[:, 1, 0:D]
        ones = CV[0:HALF, 0, 0:HALF]
        Wt = CV[:, 1:3, :].rearrange("p c n -> p (c n)")[:, 0:CH * 2 * D].rearrange("p (c r d) -> p c r d", c=CH, r=2)
        PSQ = X2T[:, :, 0:EXP]

        two = arena()
        STAGE = two("STAGE", [P, SLOTS, UNIT])
        WH = two("WH", [P, HIS, CHUNK], F32R)
        assert two.at[0] <= wh_end
        two.at[0] = wh_end
        XPD = two("XPD", [P, 12 * P + 416], F32R)
        SEL = two("SEL", [P, 96])
        assert two.at[0] <= xpd_end
        two.at[0] = xpd_end
        HS = two("HS", [P, FF])
        HB = two("HB", [P, KJ * EXP])
        HG = two("HG", [P, KJ * EXP])
        HH = two("HH", [P, KJ, GROUP, 2, B], F32R)
        assert two.at[0] <= hh_end
        YS = two("YS", [P, PAIRS, 2 * D])
        YB = two("YB", [P, B, D])
        LOW = nc.alloc_sbuf_tensor_at("LOW", [P, SLOTS, UNIT], F32R, offset=base)

        def stage(s):
            return STAGE[:, s, :]

        def low(s):
            return LOW[:, s, :]

        PS = ctx.enter_context(nc.psum_tensor("PS", [P, 8, 512], F32))

        def bank(i):
            return PS[:, i, :]

        def slot(first, t):
            return PS[:, first + t // 2 % 2, (t % 2) * 256:(t % 2) * 256 + D]

        def both(first, q):
            return PS[:, first + q % 2, :].rearrange("p (t n) -> p t n", t=2)[:, :, 0:D]

        W_BANK, E_BANK, F_BANK, X_BANK = 0, 2, 4, 6
        TURN = (E_BANK, E_BANK + 1, F_BANK, F_BANK + 1)
        OUT = (F_BANK, F_BANK + 1, W_BANK, W_BANK + 1)
        H_BANK, T_BANK, Y_BANK = 0, 2, 4

        in_const, in_pos, in_cls = sem("in_const"), sem("in_pos"), sem("in_cls")
        in_x, in_wt, w12_hi, w12_lo = sem("in_x"), sem("in_wt"), sem("w12_hi"), sem("w12_lo")
        pos_ready, zeroed, id_ready, a_pad = (sem(n) for n in ("pos_ready", "zeroed", "id_ready", "a_pad"))
        phi_sq, phi_sum, phi_root, phi_clip, phi_rec, phi_sc, phi_ready = (sem("phi_" + n) for n in ("sq", "sum", "root", "clip", "rec", "sc", "ready"))
        xh_ready, xl_ready, wt_high, wt_ready = (sem(n) for n in ("xh_ready", "xl_ready", "wt_high", "wt_ready"))
        emb_done, emb_half, emb_used = sem("emb_done"), sem("emb_half"), sem("emb_used")
        stats1, mean1, var1, root1, rstd1, norm1 = (sem(n) for n in ("stats1", "mean1", "var1", "root1", "rstd1", "norm1"))
        stats2, mean2, var2, root2, len2, norm2 = (sem(n) for n in ("stats2", "mean2", "var2", "root2", "len2", "norm2"))
        xn_twice = sem("xn_twice")
        turned, xnt_high, xnt_ready, x2t_ready = sem("turned"), sem("xnt_high"), sem("xnt_ready"), sem("x2t_ready")
        w_done, w_used, a_ready, g_ready = sem("w_done"), sem("w_used"), sem("a_ready"), sem("g_ready")
        tap_done, conv_done, silu_done, ag_ready = sem("tap_done"), sem("conv_done"), sem("silu_done"), sem("ag_ready")
        bf_added, wf_done, wf_used = sem("bf_added"), sem("wf_done"), sem("wf_used")
        xb_done = [sem("xb_done0"), sem("xb_done1")]
        xb_used = [sem("xb_used0"), sem("xb_used1")]
        le_ready, max_ready, exp_done, pad_done, rec_done, d_ready = (sem(n) for n in ("le_ready", "max_ready", "exp_done", "pad_done", "rec_done", "d_ready"))
        rmax_done, dt_ready, cs_ready, ce_ready, rsum_done, xs_ready = (sem(n) for n in ("rmax_done", "dt_ready", "cs_ready", "ce_ready", "rsum_done", "xs_ready"))
        staged = [sem(f"staged{s}") for s in range(SLOTS)]
        held_pe, held_dve, held_pool = sem("held_pe"), sem("held_dve"), sem("held_pool")

        USES = (("logits", "rows", "combine", "inputs", "turn"), ("logits", "dispatch", "combine"))
        LAST_USES = (("logits", "inputs", "turn", "rows", "combine"), USES[1])

        def uses(s, j, stage):
            order = (LAST_USES if isinstance(s, int) and s == B else USES)[j]
            return s * len(order) + (order.index(stage) - len(order))

        def used(s, j, stage):
            return uses(s, j, stage) + 1

        def turns(b, norm):
            if norm == 1:
                return 4 * b if isinstance(b, int) and b < 2 else b * 8 - 4
            return b * 8 + (8 if not isinstance(b, int) or b < B - 1 else 4)

        def wait(eng, s, n):
            if not isinstance(n, int) or n > 0:
                eng.wait_ge(s, n)

        def hold(eng, held):
            eng.sem_inc(held, 1)

        def load_w1(sp, s, e0):
            dst = stage(s).rearrange("p (k h) -> p k h", k=3)
            sp.dma_start(dst[:, 0:2, :], ew1[bass.ds(e0, 2), 0:P, :].rearrange("e d h -> d e h")).then_inc(staged[s], 16)
            sp.dma_start(dst[0:64, 2, :], ew1[bass.ds(e0, 1), P:D, :].rearrange("e d h -> (e d) h")).then_inc(staged[s], 16)
            sp.dma_start(dst[64:P, 2, :], ew1[bass.ds(e0 + 1, 1), P:D, :].rearrange("e d h -> (e d) h")).then_inc(staged[s], 16)

        def load_w2(sp, s, e0):
            dst = stage(s).rearrange("p (c e n) -> p c e n", c=3, e=2)
            src = ew2[bass.ds(e0, 2), :, :].rearrange("e (p c j) d -> p c e (j d)", c=3, j=2)
            for c in range(3):
                sp.dma_start(dst[:, c, :, :], src[:, c, :, :]).then_inc(staged[s], 16)

        GATED = ((slice(0, NPATCH), slice(1, NIMG)), (slice(CLS, CLS + 1), slice(0, 1)), (slice(TXT0, TOK), slice(NIMG, SEQ)))

        def turned_columns(q):
            if q < 2:
                return ((slice(1 + q * 256, 257 + q * 256), slice(0, 256)),)
            if q == 2:
                return ((slice(513, NIMG), slice(0, P + LASTP)), (slice(0, 1), slice(P + LASTP, P + LASTP + 1)))
            return ((slice(NIMG, SEQ), slice(0, P)),)

        def load_unit(sp, k):
            if k < PAIRS:
                load_w1(sp, k, 2 * k)
            else:
                second, p = ORDER[k - PAIRS]
                if second:
                    load_w2(sp, k, 2 * p)
                else:
                    load_w1(sp, k, GROUP + 2 * p)

        hi_done, lo_done, w_spent = sem("hi_done"), sem("lo_done"), sem("w_spent")
        xpd_zero, xp_hi, xp_ready = sem("xpd_zero"), sem("xp_hi"), sem("xp_ready")
        hs_ready, t_done, hb_ready, hg_ready, hh_hi, hh_ready = (sem(n) for n in ("hs_ready", "t_done", "hb_ready", "hg_ready", "hh_hi", "hh_ready"))
        ys_ready, sel_ready = sem("ys_ready"), sem("sel_ready")
        ys_sent = [sem(f"ys_sent{p}") for p in range(PAIRS)]
        yb_ready, o_done, o_ready, stored = sem("yb_ready"), sem("o_done"), sem("o_ready"), sem("stored")

        def unit(g, second, p):
            if isinstance(g, int) and g in (0, NG):
                return p if g == 0 else NG * 8 - 4 + p
            return g * 8 + (ORDER.index((second, p)) - 4)

        def unit_slot(g, second, p):
            if isinstance(g, int) and g in (0, NG):
                return p if g == 0 else 4 + p
            return (ORDER.index((second, p)) + 4) % SLOTS

        def loads(g, second, p):
            if isinstance(g, int) and g in (0, NG):
                return 1 if g == 0 else NG
            return g + (1 if ORDER.index((second, p)) >= 4 else 0)

        last_sent = sem("last_sent")

        def send(eng, g, sent):
            for p in range(PAIRS):
                eng.wait_ge(ys_ready, g * PAIRS + (p + 1))
                for k in range(2):
                    e = 2 * p + k
                    n = g * GROUP + e
                    eng.dma_start(YB[n:n + EXP + 1:EXP, :, :], YS[16 * e:16 * e + 2 * B, p, k * D:(k + 1) * D]).then_inc(sent[p], 16)

        N_CONST = 14 * 16

        with nc.Block() as block:
            @block.sync
            def _(sp):
                def const(dst, src):
                    sp.dma_start(dst, src).then_inc(in_const, 16)

                def load_x(b):
                    if not (isinstance(b, int) and b == 0):
                        sp.wait_ge(emb_done, b * 6)
                    sp.dma_start(X[:, :, :], xp[bass.ds(b, 1), :, :, :].rearrange("o p c n -> (o p) c n")).then_inc(in_x, 16)

                sp.dma_start(Wt[:, :, :, :], wt).then_inc(in_wt, 16)
                load_x(0)
                sp.dma_start(PB[:, 0:5, :], pos[1:1 + 5 * P, :].rearrange("(t p) d -> p t d", p=P)).then_inc(in_pos, 16)
                sp.dma_start(PB[0:LASTP, 5, :], pos[1 + 5 * P:NIMG, :]).then_inc(in_pos, 16)
                sp.dma_start(PB[LASTP:LASTP + 1, 5, :], pos[0:1, :]).then_inc(in_pos, 16)
                sp.dma_start(TBb[:, :], tb.unsqueeze(0).broadcast_to([P, D])).then_inc(in_pos, 16)
                sp.dma_start(CB[0:LASTP, :], tb.unsqueeze(0).broadcast_to([LASTP, D])).then_inc(in_pos, 16)
                sp.dma_start(CB[LASTP:LASTP + 1, :], cls).then_inc(in_pos, 16)
                const(H[:, :, 6, :], txt.rearrange("b p d -> p b d"))
                for w, cols in ((w1, slice(0, HID)), (w2, slice(HID, 2 * HID))):
                    const(W12[:, 0, cols], w[0:P, :])
                    const(W12[0:D - P, 1, cols], w[P:D, :])
                    const(W12[P // 2:P, 1, cols], w[P:D, :])
                const(CHAN[:, :, :], chan)
                const(Wf[:, :, :], wf.rearrange("(c p) d -> p c d", p=P))
                const(BF[:, :], bf.unsqueeze(0).broadcast_to([P, D]))
                const(PHI[:, :, :], phi.rearrange("(s q) n o -> q s (n o)", s=2))
                const(SC[:, :], scale.unsqueeze(0).broadcast_to([HALF, 1]))
                const(b1T[:, :, :], eb1)
                const(b2e[:, :], eb2)
                sp.wait_ge(pos_ready, 2)
                sp.wait_ge(zeroed, 1)
                sp.dma_start(H[LASTP:LASTP + 1, :, 5, :], PB[LASTP:LASTP + 1, 5, :].unsqueeze(1).broadcast_to([1, B, D])).then_inc(in_cls, 16)
                with sp.Fori(1, B) as b:
                    load_x(b)
                sp.wait_ge(emb_used, B * 6)
                for k in range(SLOT_AFTER_EMBED):
                    load_unit(sp, k)
                sp.wait_ge(w_done, B * 12)
                for k in range(SLOT_AFTER_EMBED, SLOT_AFTER_MIXER):
                    load_unit(sp, k)
                sp.wait_ge(conv_done, B * CT)
                for k in range(SLOT_AFTER_MIXER, SLOT_AFTER_CONV):
                    load_unit(sp, k)
                sp.wait_ge(ag_ready, B * CT * 3)
                for k in range(SLOT_AFTER_CONV, SLOTS):
                    load_unit(sp, k)

                def load(g, second, p):
                    sp.wait_ge(w_spent, unit(g, second, p) * 3 - 21)
                    if second:
                        load_w2(sp, unit_slot(g, 1, p), g * GROUP + (2 * p - GROUP))
                    else:
                        load_w1(sp, unit_slot(g, 0, p), g * GROUP + 2 * p)

                for second, p in ORDER[SLOTS - PAIRS:]:
                    load(1, second, p)
                with sp.Fori(2, NG) as g:
                    for second, p in ORDER:
                        load(g, second, p)
                for p in range(PAIRS):
                    load(NG, 1, p)
                send(sp, NG - 1, [last_sent] * PAIRS)
                sp.wait_ge(last_sent, PAIRS * 32)
                for p in range(PAIRS):
                    sp.wait_ge(ys_sent[p], (NG - 1) * 32)
                for b in range(B):
                    sp.wait_ge(o_ready, b * TILES + 5)
                    sp.dma_start(out[b, 1:1 + 5 * P, :].rearrange("(t p) d -> p t d", p=P), H[:, b, 0:5, :]).then_inc(stored, 16)
                    sp.wait_ge(o_ready, b * TILES + TILES)
                    sp.dma_start(out[b, 1 + 5 * P:NIMG, :], H[0:LASTP, b, 5, :]).then_inc(stored, 16)
                    sp.dma_start(out[b, 0:1, :], H[LASTP:LASTP + 1, b, 5, :]).then_inc(stored, 16)
                    sp.dma_start(out[b, NIMG:SEQ, :], H[:, b, 6, :]).then_inc(stored, 16)
                sp.wait_ge(stored, B * 4 * 16)

            @block.gpsimd
            def _(pool):
                nc.gpsimd.memset(H[:, :, 5, :], 0.0).then_inc(zeroed, 1)
                nc.gpsimd.memset(ident[:, :], 0.0).then_inc(id_ready, 1)
                nc.gpsimd.memset(A[:, :, 0:TAPS - 1], 0.0).then_inc(a_pad, 1)
                nc.gpsimd.memset(AG[:, :, CLS + 1:TXT0], 0.0).then_inc(a_pad, 1)
                pool.wait_ge(id_ready, 1)
                nc.gpsimd.affine_select(out=ident[:, :], in_=ident[:, :], compare_op=ALU.not_equal, fill=1.0,
                                        base=0, pattern=[[-1, P]], channel_multiplier=1).then_inc(id_ready, 1)
                nc.gpsimd.memset(ones[:, :], 1.0).then_inc(id_ready, 1)
                pool.wait_ge(in_const, N_CONST)

                def twice(b):
                    for t in range(TILES):
                        pool.wait_ge(norm1, b * TILES + (t + 1))
                        hold(pool, held_pool)
                        nc.gpsimd.tensor_copy(XN[:, t, D:2 * P], XN[:, t, P:D]).then_inc(xn_twice, 1)

                def add_bf(b):
                    pool.wait_ge(norm1, b * TILES + TILES)
                    h = H[:, bass.ds(b, 1), :, :].rearrange("p o t d -> p (o t) d")
                    nc.gpsimd.tensor_tensor(h, h, BF[:, :].unsqueeze(1).broadcast_to([P, TILES, D]), ALU.add).then_inc(bf_added, 1)

                def gate(b, channels):
                    wait(pool, pad_done, b * 1)
                    for c in channels:
                        pool.wait_ge(silu_done, b * CT + c + 1)
                        pool.wait_ge(g_ready, b * CT + c + 1)
                        for dst, src in GATED:
                            nc.gpsimd.tensor_tensor(AG[:, c, dst], AG[:, c, dst], CV[:, c, src], ALU.mult).then_inc(ag_ready, 1)

                def x_low(b):
                    for c in range(CH):
                        pool.wait_ge(xh_ready, b * CH + (c + 1))
                        nc.gpsimd.tensor_tensor(XL[:, c, :], X[:, c, :], XH[:, c, :].bitcast(F32), ALU.subtract).then_inc(xl_ready, 1)

                def zero_pad(s):
                    pool.wait_ge(ag_ready, s * 9)
                    pool.wait_ge(xl_ready, B * CH if isinstance(s, int) and s >= B - 1 else s * CH + 2 * CH)
                    wait(pool, bf_added, B if isinstance(s, int) and s >= B - 1 else s + 1)
                    pool.wait_ge(le_ready, s * 2)
                    hold(pool, held_pool)
                    nc.gpsimd.memset(LE[EXP:P, CLS + 1:TXT0], 0.0).then_inc(pad_done, 1)

                twice(0)
                add_bf(0)
                x_low(1)
                gate(0, range(CT))
                twice(1)
                add_bf(1)
                with pool.Fori(1, B - 1) as b:
                    x_low(b + 1)
                    zero_pad(b)
                    gate(b, range(CT))
                    twice(b + 1)
                    add_bf(b + 1)
                zero_pad(B - 1)
                gate(B - 1, range(CT - 1))
                zero_pad(B)

                pool.wait_ge(pad_done, B)
                nc.gpsimd.memset(XPD[:, :].bitcast(F32), 0.0).then_inc(xpd_zero, 1)
                nc.gpsimd.memset(SEL[:, :], 0.0).then_inc(sel_ready, 1)
                pool.wait_ge(sel_ready, 1)
                for part in range(2):
                    sel = SEL[:, 0:EXP].rearrange("p (e b) -> p e b", e=GROUP)
                    nc.gpsimd.affine_select(out=sel, in_=sel, compare_op=ALU.not_equal, fill=1.0, base=-8 * part,
                                            pattern=[[-16, GROUP], [-1, B]], channel_multiplier=1).then_inc(sel_ready, 1)
                    pool.wait_ge(sel_ready, part + 2)

                for g in range(NG - 1):
                    send(pool, g, ys_sent)
                pool.wait_ge(yb_ready, 1)
                for b in range(1, B):
                    nc.gpsimd.tensor_tensor(YB[0:EXP, b, :], YB[0:EXP, b, :], b2e[:, :], ALU.add).then_inc(yb_ready, 1)

            @block.tensor
            def _(pe):
                def embed(b):
                    for t in range(6):
                        m = P if t < 5 else LASTP
                        out_ = bank(E_BANK + t % 2)
                        if t >= 2:
                            pe.wait_ge(emb_used, b * 6 + (t - 1))
                        for c in range(CH):
                            if t == 0:
                                pe.wait_ge(xl_ready, b * CH + (c + 1))
                            for r in range(2):
                                at = r * GRID + t * P
                                first, last = c + r == 0, c == CH - 1 and r == 1
                                parts = [(out_[0:m, 0:2 * D], XH[:, c, at:at + m], WtHL[:, c, r, :, :].rearrange("p k d -> p (k d)")),
                                         (out_[0:m, 0:D], XL[:, c, at:at + m], WtHL[:, c, r, 0, :])]
                                for k, (o, x, w) in enumerate(parts if not last else parts[::-1]):
                                    mm = nc.tensor.matmul(o, x, w, start=first and k == 0, stop=last and k == 1)
                        mm.then_inc(emb_done, 1)

                def transposes(src, width, normed, count, out_used, pairs=range(4)):
                    for q in pairs:
                        if q >= 2:
                            wait(pe, wf_used, out_used + (q - 1))
                        for t in range(2 * q, min(2 * q + 2, TILES)):
                            pe.wait_ge(normed, count + t + 1)
                            for s in range(2):
                                at = s * 256 + (t % 2) * P
                                mm = nc.tensor.transpose(bank(TURN[q])[0:width, at:at + P], src[:, t, s * width:(s + 1) * width], ident[:, :])
                        mm.then_inc(turned, 1)

                def mixer_in(b, first, last):
                    if first == 0:
                        pe.wait_ge(xnt_ready, b * 5 + 4)
                        wait(pe, wf_used, b * 4)
                    for i in range(first, last):
                        c, half = i // 2, i % 2
                        lo, hi = (0, SPLIT) if half == 0 else (SPLIT, SEQ)
                        if i == 1:
                            pe.wait_ge(xnt_ready, b * 5 + 5)
                        wait(pe, w_used, b * 12 + (i - 1))
                        passes = ((W12H, 0, XNH), (W12H, 0, XNL), (W12L, 0, XNH), (W12H, 1, XNR), (W12L, 1, XNR))
                        for k, (w, s, x) in enumerate(passes):
                            mm = nc.tensor.matmul(bank(W_BANK + i % 2)[:, 0:hi - lo], w[:, s, c * P:(c + 1) * P], x[:, lo:hi],
                                                  start=(k == 0), stop=(k == len(passes) - 1))
                        mm.then_inc(w_done, 1)

                def mixer_out(b, middle=None):
                    pe.wait_ge(ag_ready, b * 9 + 9)
                    pe.wait_ge(w_used, b * 12 + 12)
                    for t in range(TILES):
                        if t == 4 and middle:
                            middle()
                        for c in range(CT):
                            mm = nc.tensor.matmul(slot(OUT[t // 2 // 2 * 2], t), AG[:, c, t * P:(t + 1) * P], Wf[:, c, :],
                                                  start=(c == 0), stop=(c == CT - 1))
                        if t % 2 or t == TILES - 1:
                            mm.then_inc(wf_done, 1)

                def norm2_rows(s):
                    transposes(XN2, HALF, norm2, s * TILES - TILES, s * 4 - 2)

                def logits(s):
                    pe.wait_ge(x2t_ready, s * 4)
                    for j in range(2):
                        pe.wait_ge(xb_used[j], used(s, j, "logits"))
                        for h in range(2):
                            mm = nc.tensor.matmul(bank(X_BANK + j)[:, 0:LSPLIT], PHN[:, h, :], X2T[:, h, j * LSPLIT:(j + 1) * LSPLIT],
                                                  start=(h == 0), stop=(h == 1))
                        mm.then_inc(xb_done[j], 1)

                def logit_rows(s):
                    pe.wait_ge(le_ready, s * 2)
                    pe.wait_ge(xb_used[0], used(s, 0, "rows"))
                    hold(pe, held_pe)
                    for t in range(TILES):
                        mm = nc.tensor.transpose(bank(X_BANK)[:, t * EXP:(t + 1) * EXP], LE[0:EXP, t * P:(t + 1) * P], ident[0:EXP, 0:EXP])
                    mm.then_inc(xb_done[0], 1)

                def dispatch_turn(s):
                    pe.wait_ge(d_ready, s * 1)
                    pe.wait_ge(xb_used[1], used(s, 1, "dispatch"))
                    hold(pe, held_pe)
                    for t in range(TILES):
                        mm = nc.tensor.transpose(bank(X_BANK + 1)[:, t * EXP:(t + 1) * EXP], LE[EXP:P, t * P:(t + 1) * P], ident[EXP:P, EXP:P])
                    mm.then_inc(xb_done[1], 1)

                def combine_turn(s):
                    pe.wait_ge(ce_ready, s * 1)
                    for j, tiles in ((0, range(0, 4)), (1, range(4, TILES))):
                        pe.wait_ge(xb_used[j], used(s, j, "combine"))
                        for t in tiles:
                            mm = nc.tensor.transpose(bank(X_BANK + j)[:, (t % 4) * P:(t % 4 + 1) * P], CE[:, t, :], ident[:, :])
                        mm.then_inc(xb_done[j], 1)

                def inputs(s):
                    pe.wait_ge(dt_ready, s * 1)
                    pe.wait_ge(xb_used[0], used(s, 0, "inputs"))
                    for t in range(TILES):
                        mm = nc.tensor.matmul(bank(X_BANK)[0:EXP, 0:D], DT[:, t, :], XN2[:, t, :], start=(t == 0), stop=(t == TILES - 1))
                    mm.then_inc(xb_done[0], 1)

                def inputs_turn(s):
                    pe.wait_ge(xs_ready, s * 2)
                    pe.wait_ge(xb_used[0], used(s, 0, "turn"))
                    hold(pe, held_pe)
                    for h in range(2):
                        mm = nc.tensor.transpose(bank(X_BANK)[:, h * EXP:(h + 1) * EXP], XS[:, h * P:(h + 1) * P], ident[0:EXP, 0:EXP])
                    mm.then_inc(xb_done[0], 1)

                pe.wait_ge(wt_ready, 1)
                embed(0)
                pe.wait_ge(in_const, N_CONST)
                pe.wait_ge(id_ready, 3)
                pe.wait_ge(phi_sq, 1)
                for s in range(2):
                    mm = nc.tensor.matmul(bank(W_BANK)[0:HALF, 0:EXP], ones[:, :], PSQ[:, s, :], start=(s == 0), stop=(s == 1))
                mm.then_inc(phi_sum, 1)
                transposes(XN, P, xn_twice, 0, -2)
                pe.wait_ge(phi_root, 1)
                pe.wait_ge(phi_ready, 2)
                pe.wait_ge(w12_lo, 1)

                def step(b, before, after):
                    mixer_in(b, 0, 2)
                    if before:
                        norm2_rows(b)
                    mixer_in(b, 2, 4)
                    if before:
                        logits(b)
                    mixer_in(b, 4, 8)
                    if before and after:
                        logit_rows(b)
                    mixer_in(b, 8, 12)
                    if not after:
                        logit_rows(b)
                    if after:
                        embed(b + 1)
                        if before:
                            dispatch_turn(b)
                        mixer_out(b)
                    else:
                        mixer_out(b, lambda: dispatch_turn(b))
                    if before:
                        combine_turn(b)
                    if after:
                        transposes(XN, P, xn_twice, b * TILES + TILES, b * 4, range(3))
                    if before:
                        inputs(b)
                    if after:
                        transposes(XN, P, xn_twice, b * TILES + TILES, b * 4, range(3, 4))
                    if before:
                        inputs_turn(b)

                step(0, False, True)
                with pe.Fori(0, B // 2 - 1) as i:
                    step(i * 2 + 1, True, True)
                    step(i * 2 + 2, True, True)
                step(B - 1, True, False)
                norm2_rows(B)
                logits(B)
                dispatch_turn(B)
                inputs(B)
                inputs_turn(B)

                def first(g, p):
                    k, s = unit(g, 0, p), unit_slot(g, 0, p)
                    if p == 0:
                        pe.wait_ge(xp_ready, g * 4 + 4)
                        wait(pe, hs_ready, g * 2)
                    for c in range(3):
                        pe.wait_ge(lo_done, k * 3 + (c + 1))
                        x = XPD[:, (3 * p + c) * P:(3 * p + c + 1) * P]
                        ring = (3 * s + c) % HIS
                        for n in range(2):
                            cols = slice(n * HID, (n + 1) * HID)
                            for i, w in enumerate((WH[:, ring, cols], low(s)[:, c * CHUNK + n * HID:c * CHUNK + (n + 1) * HID])):
                                mm = nc.tensor.matmul(bank(H_BANK + n)[:, 0:HID], x, w,
                                                      start=(p == 0 and c == 0 and i == 0), stop=(p == PAIRS - 1 and c == 2 and i == 1))
                        mm.then_inc(w_spent, 1)

                def turn(g):
                    pe.wait_ge(hs_ready, g * 2 + 2)
                    wait(pe, hb_ready, g * 2)
                    hs = HS[:, :].rearrange("p (n j) -> p n j", j=KJ)
                    for j in range(KJ):
                        at = (j % 3) * 96
                        mm = nc.tensor.matmul(bank(T_BANK + j // 3)[:, at:at + 96], hs[:, :, j], SEL[:, :], start=True, stop=True)
                        if j % 3 == 2:
                            mm.then_inc(t_done, 1)

                def second(g, p):
                    k, s = unit(g, 1, p), unit_slot(g, 1, p)
                    if p == 0:
                        pe.wait_ge(hh_ready, g * 1)
                    wait(pe, ys_ready, g * PAIRS + (p - PAIRS - 1))
                    for c in range(3):
                        pe.wait_ge(lo_done, k * 3 + (c + 1))
                        ring = (3 * s + c) % HIS
                        for j in range(2):
                            x = HH[:, 2 * c + j, :, :, :].rearrange("p e r b -> p (e r b)")
                            for i, w in enumerate((WH[:, ring, :], low(s)[:, c * CHUNK:(c + 1) * CHUNK])):
                                w = w.rearrange("p (e j d) -> p e j d", e=2, j=2)[:, :, j, :]
                                mm = nc.tensor.matmul(bank(Y_BANK + p % 2)[:, 0:2 * D], x, w,
                                                      start=(c + j + i == 0), stop=(c == 2 and j == 1 and i == 1))
                        mm.then_inc(w_spent, 1)

                pe.wait_ge(sel_ready, 3)
                for p in range(PAIRS):
                    first(0, p)
                logit_rows(B)
                turn(0)

                def group(g):
                    for n, (s, p) in enumerate(ORDER):
                        (second if s else first)(g, p)
                        if isinstance(g, int) and n == 0:
                            combine_turn(B)
                        if n == 6:
                            turn(g)

                group(1)
                with pe.Fori(2, NG) as g:
                    group(g)
                for p in range(PAIRS):
                    second(NG, p)

                for b in range(B):
                    pe.wait_ge(yb_ready, b + 1)
                    for t in range(TILES):
                        n = b * TILES + t
                        wait(pe, o_ready, n - 7)
                        nc.tensor.matmul(bank(n % 8)[:, 0:D], CTt[:, b, t * P:(t + 1) * P], YB[:, b, :], start=True, stop=True).then_inc(o_done, 1)

            @block.scalar
            def _(act):
                def root1_(b):
                    act.wait_ge(var1, b + 1)
                    nc.scalar.activation(sd1[:, :], ve1[:, :], ACT.Sqrt).then_inc(root1, 1)

                def norm1_(b):
                    act.wait_ge(rstd1, b * 2 + 2)
                    for t in range(TILES):
                        nc.scalar.activation(XN[:, t, 0:D], H[:, bass.ds(b, 1), t, :].rearrange("p o d -> p (o d)"), ACT.Identity,
                                             bias=nm1[:, t:t + 1], scale=rs1[:, t:t + 1]).then_inc(norm1, 1)

                def keep_xnt(b, pairs=range(4)):
                    for q in pairs:
                        act.wait_ge(turned, turns(b, 1) + (q + 1))
                        for dst, src in turned_columns(q):
                            turn = bank(TURN[q]).rearrange("p (s n) -> p s n", s=2)
                            nc.scalar.activation(XNH[:, dst], turn[:, 0, src], ACT.Identity)
                            nc.scalar.activation(XNR[:, dst], turn[:, 1, src], ACT.Identity).then_inc(xnt_high, 1)

                def keep_a(b, first, last):
                    if first == 0:
                        act.wait_ge(a_pad, 2)
                        wait(act, conv_done, b * CT)
                    for i in range(first, last):
                        c, half = i // 2, i % 2
                        lo, hi = (0, SPLIT) if half == 0 else (SPLIT, SEQ)
                        act.wait_ge(w_done, b * 12 + (i + 1))
                        nc.scalar.activation(A[:, c, TAPS - 1 + lo:TAPS - 1 + hi], bank(W_BANK + i % 2)[:, 0:hi - lo], ACT.Identity,
                                             bias=CHAN[:, c, TAPS + 1:TAPS + 2]).then_inc(a_ready, 1)
                        act.wait_ge(a_ready, b * 6 + (i + 1))
                        act.sem_inc(w_used, 1)

                def combine_exp(s):
                    act.wait_ge(cs_ready, s * 1)
                    nc.scalar.activation(CE[:, :, :].rearrange("p t (r n) -> p t r n", r=2),
                                         CS[:, :, :].unsqueeze(2).broadcast_to([P, TILES, 2, EXP]), ACT.Exp).then_inc(ce_ready, 1)

                def silus(b):
                    for c in range(CT):
                        bias = CHAN[:, c, TAPS + 2:TAPS + 3]
                        act.wait_ge(w_done, b * 12 + (6 + 2 * c + 1))
                        src = bank(W_BANK)
                        nc.scalar.activation(AG[:, c, CLS:CLS + 1], src[:, 0:1], ACT.Silu, bias=bias)
                        nc.scalar.activation(AG[:, c, 0:SPLIT - 1], src[:, 1:SPLIT], ACT.Silu, bias=bias).then_inc(w_used, 1)
                        act.wait_ge(w_done, b * 12 + (6 + 2 * c + 2))
                        src = bank(W_BANK + 1)
                        nc.scalar.activation(AG[:, c, SPLIT - 1:NPATCH], src[:, 0:NIMG - SPLIT], ACT.Silu, bias=bias)
                        nc.scalar.activation(AG[:, c, TXT0:TOK], src[:, NIMG - SPLIT:SEQ - SPLIT], ACT.Silu, bias=bias).then_inc(w_used, 1)
                        act.wait_ge(w_used, b * 12 + (6 + 2 * c + 2))
                        act.sem_inc(g_ready, 1)
                        act.wait_ge(conv_done, b * CT + (c + 1))
                        nc.scalar.activation(CV[:, c, :], CV[:, c, :], ACT.Silu, bias=CHAN[:, c, TAPS:TAPS + 1]).then_inc(silu_done, 1)

                def keep_combine(s):
                    for j, lo, hi in ((0, 0, 4 * P), (1, 4 * P, TOK)):
                        act.wait_ge(xb_done[j], uses(s, j, "combine") + 1)
                        nc.scalar.activation(CTt[:, bass.ds(s - 1, 1), lo:hi].rearrange("p o n -> p (o n)"), bank(X_BANK + j)[:, 0:hi - lo],
                                             ACT.Identity).then_inc(xb_used[j], 1)

                def keep_inputs(s):
                    act.wait_ge(xb_done[0], uses(s, 0, "inputs") + 1)
                    nc.scalar.activation(XS[:, 0:D], bank(X_BANK)[0:EXP, 0:D], ACT.Identity).then_inc(xs_ready, 1)
                    nc.scalar.activation(XS[:, D:4 * EXP], bank(X_BANK)[0:EXP, P:D], ACT.Identity).then_inc(xs_ready, 1)
                    act.wait_ge(xs_ready, s * 2)
                    act.sem_inc(xb_used[0], 1)

                def root2_(b):
                    act.wait_ge(var2, b * 2 + 2)
                    nc.scalar.activation(sd2[:, :, :], ve2[:, :, :], ACT.Sqrt).then_inc(root2, 1)

                def keep_x2t(s):
                    for q in range(4):
                        cols = 256 if q < 3 else P
                        act.wait_ge(turned, turns(s - 1, 2) + (q + 1))
                        src = bank(TURN[q])[0:HALF, :].rearrange("p (s n) -> p s n", s=2)[:, :, 0:cols]
                        nc.scalar.activation(X2T[:, :, q * 256:q * 256 + cols], src, ACT.Identity).then_inc(x2t_ready, 1)

                def keep_logits(s):
                    for j in range(2):
                        act.wait_ge(xb_done[j], uses(s, j, "logits") + 1)
                        nc.scalar.activation(LE[:, j * LSPLIT:(j + 1) * LSPLIT], bank(X_BANK + j)[:, 0:LSPLIT], ACT.Identity).then_inc(le_ready, 1)
                        act.wait_ge(le_ready, s * 2 + (j - 1))
                        act.sem_inc(xb_used[j], 1)

                def dispatch_exp(s):
                    act.wait_ge(max_ready, s * 4)
                    for i, (lo, hi) in enumerate(SEG):
                        nc.scalar.activation(LE[EXP:P, lo:hi], LE[EXP:P, lo:hi], ACT.Exp, bias=nmx[EXP:P, :],
                                             accum_out=es[EXP:P, i:i + 1]).then_inc(exp_done, 1)

                def load_table(function):
                    nc.scalar.activation(unused[:, :], ident[:, 0:1], function)

                def x_high(b):
                    act.wait_ge(in_x, b * 16 + 16)
                    for c in range(CH):
                        nc.scalar.activation(XH[:, c, :], X[:, c, :], ACT.Identity).then_inc(xh_ready, 1)

                act.wait_ge(id_ready, 2)
                act.wait_ge(in_wt, 16)
                nc.scalar.activation(WtHL[:, :, :, 0, :], Wt, ACT.Identity).then_inc(wt_high, 1)
                x_high(0)
                act.wait_ge(in_const, N_CONST)
                nc.scalar.activation(W12H[:, :, :], W12[:, :, :], ACT.Identity).then_inc(w12_hi, 1)
                act.wait_ge(phi_sum, 1)
                nc.scalar.activation(pn[:, :], bank(W_BANK)[0:HALF, 0:EXP], ACT.Sqrt).then_inc(phi_root, 1)
                root1_(0)
                load_table(ACT.Silu)
                norm1_(0)
                keep_xnt(0)

                def step(b, before, after):
                    if after:
                        x_high(b + 1)
                    keep_a(b, 0, 2)
                    if before:
                        keep_x2t(b)
                    keep_a(b, 2, 4)
                    if before:
                        keep_logits(b)
                    keep_a(b, 4, 6)
                    silus(b)
                    if before:
                        dispatch_exp(b)
                        combine_exp(b)
                    if after:
                        root1_(b + 1)
                        norm1_(b + 1)
                    else:
                        load_table(ACT.Sqrt)
                    if before:
                        keep_combine(b)
                    if after:
                        keep_xnt(b + 1, range(3))
                    root2_(b)
                    if after:
                        load_table(ACT.Silu)
                    if before:
                        keep_inputs(b)
                    if after:
                        keep_xnt(b + 1, range(3, 4))

                step(0, False, True)
                with act.Fori(0, B // 2 - 1) as i:
                    step(i * 2 + 1, True, True)
                    step(i * 2 + 2, True, True)
                step(B - 1, True, False)
                keep_x2t(B)

                def high(g, second, p):
                    k, s = unit(g, second, p), unit_slot(g, second, p)
                    act.wait_ge(staged[s], loads(g, second, p) * 48)
                    for c in range(3):
                        wait(act, w_spent, k * 3 + (c - 5))
                        nc.scalar.activation(WH[:, (3 * s + c) % HIS, :], stage(s)[:, c * CHUNK:(c + 1) * CHUNK], ACT.Identity).then_inc(hi_done, 1)

                def keep_h(g):
                    act.wait_ge(w_spent, unit(g, 0, PAIRS - 1) * 3 + 3)
                    wait(act, t_done, g * 2)
                    for n in range(2):
                        nc.scalar.activation(HS[:, n * HID:(n + 1) * HID], bank(H_BANK + n)[:, 0:HID], ACT.Identity).then_inc(hs_ready, 1)

                def keep_y(g, p):
                    act.wait_ge(w_spent, unit(g, 1, p) * 3 + 3)
                    wait(act, ys_sent[p], g * 32 - 32 if not (isinstance(g, int)) or g > 1 else 0)
                    nc.scalar.activation(YS[:, p, :], bank(Y_BANK + p % 2)[:, 0:2 * D], ACT.Identity).then_inc(ys_ready, 1)

                def gelu(g):
                    act.wait_ge(hb_ready, g * 2 + 2)
                    nc.scalar.activation(HG[:, :], HB[:, :], ACT.Gelu).then_inc(hg_ready, 1)
                    act.wait_ge(hg_ready, g + 1)
                    hg = HG[:, :].rearrange("p (n b) -> p n b", b=B)
                    nc.scalar.activation(HH[:, :, :, 0, :].rearrange("p j e b -> p (j e) b"), hg, ACT.Identity).then_inc(hh_hi, 1)

                def group(g):
                    for n, (second, p) in enumerate(ORDER):
                        if not (isinstance(g, int) and g == 1 and n == 0):
                            high(g, second, p)
                        if n < 2:
                            if not (isinstance(g, int) and g == 1):
                                keep_y(g - 1, n + 2)
                            if n == 1:
                                gelu(g - 1)
                                if isinstance(g, int) and g == 1:
                                    keep_combine(B)
                        elif n in (4, 6):
                            keep_y(g, (n - 4) // 2)
                    keep_h(g)

                high(0, 0, 0)
                keep_logits(B)
                dispatch_exp(B)
                high(0, 0, 1)
                keep_inputs(B)
                high(0, 0, 2)
                high(0, 0, 3)
                high(1, 0, 0)
                keep_h(0)
                combine_exp(B)
                group(1)
                group(2)
                with act.Fori(3, NG) as g:
                    group(g)
                high(NG, 1, 0)
                keep_y(NG - 1, 2)
                keep_y(NG - 1, 3)
                gelu(NG - 1)
                high(NG, 1, 1)
                for p in range(2, PAIRS):
                    high(NG, 1, p)
                    keep_y(NG, p - 2)
                for p in range(2, PAIRS):
                    keep_y(NG, p)

            @block.vector
            def _(dve):
                def row(b, t):
                    return H[:, bass.ds(b, 1), t, :].rearrange("p o d -> p (o d)")

                def rows(b, q):
                    return H[:, bass.ds(b, 1), 2 * q:2 * q + 2, :].rearrange("p o t d -> p (o t) d")

                def norm_in(b, middle):
                    def stats(*tiles):
                        for t in tiles:
                            nc.vector.bn_stats(st1[:, t, :], row(b, t)).then_inc(stats1, 1)

                    for t in range(6):
                        m = P if t < 5 else LASTP
                        dve.wait_ge(emb_done, b * 6 + (t + 1))
                        out_ = bank(E_BANK + t % 2)[0:m]
                        nc.vector.tensor_tensor(row(b, t)[0:m], out_[:, 0:D], PB[0:m, t, :], ALU.add).then_inc(emb_half, 1)
                        if t > 1:
                            stats(t - 2)
                        dve.wait_ge(emb_half, b * 6 + (t + 1))
                        nc.vector.tensor_tensor(row(b, t)[0:m], out_[:, D:2 * D], row(b, t)[0:m], ALU.add).then_inc(emb_used, 1)
                        if t == 3:
                            if middle:
                                middle()
                            stats(6)
                    dve.wait_ge(emb_used, b * 6 + 6)
                    hold(dve, held_dve)
                    stats(4, 5)
                    dve.wait_ge(stats1, b * TILES + TILES)
                    hold(dve, held_dve)
                    for t in range(TILES):
                        nc.vector.bn_aggr(mv1[:, t, :], st1[:, t, :]).then_inc(mean1, 1)
                    dve.wait_ge(mean1, b * TILES + TILES)
                    nc.vector.tensor_scalar(ve1[:, :], mv1[:, :, 1], EPS_LN, None, ALU.add).then_inc(var1, 1)
                    dve.wait_ge(root1, b + 1)
                    nc.vector.reciprocal(rs1[:, :], sd1[:, :]).then_inc(rstd1, 1)
                    dve.wait_ge(rstd1, b * 2 + 1)
                    nc.vector.scalar_tensor_tensor(out=nm1[:, :], in0=mv1[:, :, 0], scalar=-1.0, in1=rs1[:, :], op0=ALU.mult, op1=ALU.mult).then_inc(rstd1, 1)

                def keep_xnt(b, pairs=range(4)):
                    done = 4 if pairs[0] == 3 else 0
                    for q in pairs:
                        done += len(turned_columns(q))
                        dve.wait_ge(xnt_high, b * 5 + done)
                        for dst, src in turned_columns(q):
                            turn = bank(TURN[q]).rearrange("p (s n) -> p s n", s=2)
                            nc.vector.tensor_tensor(XNL[:, dst], turn[:, 0, src], XNH[:, dst].bitcast(F32), ALU.subtract)
                            nc.vector.tensor_tensor(XNR[P // 2:P, dst], turn[P // 2:P, 1, src], XNR[P // 2:P, dst].bitcast(F32),
                                                    ALU.subtract).then_inc(xnt_ready, 1)

                def conv(b, channels):
                    for c in channels:
                        dve.wait_ge(a_ready, b * 6 + (2 * c + 2))
                        wait(dve, ag_ready, b * 9 + (3 * c - 6))
                        cv = CV[:, c, :]
                        nc.vector.tensor_scalar(cv, A[:, c, 0:SEQ], CHAN[:, c, 0:1], None, ALU.mult).then_inc(tap_done, 1)
                        for k in range(1, TAPS):
                            dve.wait_ge(tap_done, b * 9 + (3 * c + k))
                            mm = nc.vector.scalar_tensor_tensor(out=cv, in0=A[:, c, k:k + SEQ], scalar=CHAN[:, c, k:k + 1], in1=cv, op0=ALU.mult, op1=ALU.add)
                            mm.then_inc(tap_done if k < TAPS - 1 else conv_done, 1)

                def norm_mid(b, before, after):
                    dve.wait_ge(bf_added, b + 1)
                    def stats(*tiles):
                        for t in tiles:
                            nc.vector.bn_stats(st2[:, t, :], row(b, t)).then_inc(stats2, 1)

                    for q in range(4):
                        wait(dve, wf_used, b * 4 + q)
                        dve.wait_ge(wf_done, b * 4 + (q + 1))
                        if q < 3:
                            nc.vector.tensor_tensor(rows(b, q), both(OUT[q // 2 * 2], q), rows(b, q), ALU.add).then_inc(wf_used, 1)
                        else:
                            nc.vector.tensor_tensor(row(b, 6), slot(OUT[2], 6), row(b, 6), ALU.add).then_inc(wf_used, 1)
                        if q == 1 and not after:
                            keep_dispatch(b)
                        if q > 0:
                            stats(2 * q - 2, 2 * q - 1)
                    dve.wait_ge(wf_used, b * 4 + 4)
                    hold(dve, held_dve)
                    stats(6)
                    dve.wait_ge(stats2, b * TILES + TILES)
                    hold(dve, held_dve)
                    for t in range(TILES):
                        nc.vector.bn_aggr(mv2[:, t, :], st2[:, t, :]).then_inc(mean2, 1)
                    dve.wait_ge(mean2, b * TILES + TILES)
                    nc.vector.tensor_scalar(ve2[:, 0, :], mv2[:, :, 1], EPS_LN, None, ALU.add).then_inc(var2, 1)
                    nc.vector.tensor_scalar(ve2[:, 1, :], mv2[:, :, 1], float(D), None, ALU.mult).then_inc(var2, 1)
                    if after:
                        keep_xnt(b + 1, range(3))
                    dve.wait_ge(root2, b + 1)
                    nc.vector.reciprocal(rs2[:, :], sd2[:, 0, :]).then_inc(len2, 1)
                    dve.wait_ge(len2, b * 5 + 1)
                    nc.vector.tensor_tensor(nr2[:, :], sd2[:, 1, :], rs2[:, :], ALU.mult).then_inc(len2, 1)
                    dve.wait_ge(len2, b * 5 + 2)
                    nc.vector.tensor_scalar(nq2[:, :], nr2[:, :], EPS_L2, None, ALU.max).then_inc(len2, 1)
                    dve.wait_ge(len2, b * 5 + 3)
                    nc.vector.reciprocal(ri2[:, :], nq2[:, :]).then_inc(len2, 1)
                    dve.wait_ge(len2, b * 5 + 4)
                    nc.vector.tensor_tensor(sc2[:, :], rs2[:, :], ri2[:, :], ALU.mult).then_inc(len2, 1)
                    if before:
                        dve.wait_ge(xb_done[0], uses(b, 0, "inputs") + 1)
                    if after:
                        keep_xnt(b + 1, range(3, 4))
                    dve.wait_ge(len2, b * 5 + 5)
                    for t in range(TILES):
                        nc.vector.tensor_scalar(XN2[:, t, :], row(b, t), mv2[:, t, 0:1], sc2[:, t:t + 1], ALU.subtract, ALU.mult).then_inc(norm2, 1)

                def dispatch_max(s):
                    dve.wait_ge(le_ready, s * 2)
                    for i, (lo, hi) in enumerate(SEG):
                        nc.vector.reduce_max(mx2[EXP:P, i:i + 1], LE[EXP:P, lo:hi], AX.X).then_inc(max_ready, 1)
                    dve.wait_ge(max_ready, s * 4 - 2)
                    nc.vector.tensor_tensor(mxa[EXP:P, :], mx2[EXP:P, 0:1], mx2[EXP:P, 1:2], ALU.max).then_inc(max_ready, 1)
                    dve.wait_ge(max_ready, s * 4 - 1)
                    nc.vector.tensor_scalar(nmx[EXP:P, :], mxa[EXP:P, :], -1.0, None, ALU.mult).then_inc(max_ready, 1)

                def dispatch_scale(s):
                    dve.wait_ge(exp_done, s * 2)
                    nc.vector.tensor_tensor(esum[EXP:P, :], es[EXP:P, 0:1], es[EXP:P, 1:2], ALU.add).then_inc(rec_done, 1)
                    dve.wait_ge(rec_done, s * 2 - 1)
                    nc.vector.reciprocal(erec[EXP:P, :], esum[EXP:P, :]).then_inc(rec_done, 1)
                    dve.wait_ge(rec_done, s * 2)
                    dve.wait_ge(pad_done, s * 1)
                    nc.vector.tensor_scalar(LE[EXP:P, :], LE[EXP:P, :], erec[EXP:P, :], None, ALU.mult).then_inc(d_ready, 1)

                def combine_max(s):
                    dve.wait_ge(xb_done[0], uses(s, 0, "rows") + 1)
                    src = bank(X_BANK)[:, 0:TILES * EXP].rearrange("p (t n) -> p t n", n=EXP)
                    nc.vector.reduce_max(rmx[:, :], src, AX.X).then_inc(rmax_done, 1)
                    dve.wait_ge(rmax_done, s * 1)
                    nc.vector.tensor_tensor(CS[:, :, :], src, rmx[:, :].unsqueeze(2).broadcast_to([P, TILES, EXP]), ALU.subtract).then_inc(cs_ready, 1)
                    dve.wait_ge(cs_ready, s * 1)
                    dve.sem_inc(xb_used[0], 1)

                def combine_sum(s):
                    dve.wait_ge(ce_ready, s * 1)
                    nc.vector.reduce_sum(rsm[:, :], CE[:, :, 0:EXP], AX.X).then_inc(rsum_done, 1)
                    dve.wait_ge(rsum_done, s * 2 - 1)
                    nc.vector.reciprocal(RC[:, bass.ds(s - 1, 1), :].rearrange("p o t -> p (o t)"), rsm[:, :]).then_inc(rsum_done, 1)

                def keep_dispatch(s):
                    dve.wait_ge(xb_done[1], uses(s, 1, "dispatch") + 1)
                    nc.vector.tensor_copy(DT[:, :, :], bank(X_BANK + 1)[:, 0:TILES * EXP].rearrange("p (t n) -> p t n", n=EXP)).then_inc(dt_ready, 1)
                    dve.wait_ge(dt_ready, s * 1)
                    dve.sem_inc(xb_used[1], 1)

                def keep_xt(s):
                    dve.wait_ge(xb_done[0], uses(s, 0, "turn") + 1)
                    nc.vector.tensor_copy(XT[:, :, bass.ds(s - 1, 1), :].rearrange("p h o n -> p h (o n)"),
                                          bank(X_BANK)[:, 0:2 * EXP].rearrange("p (h n) -> p h n", h=2)).then_inc(xb_used[0], 1)

                for j in range(2):
                    dve.sem_inc(xb_used[j], 1)
                dve.wait_ge(wt_high, 1)
                nc.vector.tensor_tensor(WtHL[:, :, :, 1, :], Wt, WtHL[:, :, :, 0, :].bitcast(F32), ALU.subtract).then_inc(wt_ready, 1)
                for c in range(CH):
                    dve.wait_ge(xh_ready, c + 1)
                    nc.vector.tensor_tensor(XL[:, c, :], X[:, c, :], XH[:, c, :].bitcast(F32), ALU.subtract).then_inc(xl_ready, 1)
                dve.wait_ge(in_pos, 6 * 16)
                nc.vector.tensor_tensor(PB[:, 0:5, :], PB[:, 0:5, :], TBb[:, :].unsqueeze(1).broadcast_to([P, 5, D]), ALU.add).then_inc(pos_ready, 1)
                nc.vector.tensor_tensor(PB[0:LASTP + 1, 5, :], PB[0:LASTP + 1, 5, :], CB[0:LASTP + 1, :], ALU.add).then_inc(pos_ready, 1)

                def constants():
                    dve.wait_ge(in_const, N_CONST)
                    dve.wait_ge(in_cls, 16)
                    nc.vector.tensor_tensor(PSQ[:, :, :], PHI[:, :, :], PHI[:, :, :], ALU.mult).then_inc(phi_sq, 1)

                dve.wait_ge(pos_ready, 2)
                norm_in(0, constants)
                dve.wait_ge(phi_root, 1)
                nc.vector.tensor_scalar(pr[:, :], pn[:, :], EPS_L2, None, ALU.max).then_inc(phi_clip, 1)
                dve.wait_ge(phi_clip, 1)
                nc.vector.reciprocal(pn[:, :], pr[:, :]).then_inc(phi_rec, 1)
                dve.wait_ge(phi_rec, 1)
                nc.vector.tensor_scalar(pr[:, :], pn[:, :], SC[:, 0:1], None, ALU.mult).then_inc(phi_sc, 1)
                dve.wait_ge(phi_sc, 1)
                for s in range(2):
                    nc.vector.tensor_tensor(PHN[:, s, :].rearrange("p (r n) -> p r n", r=2), PHI[:, s, :].unsqueeze(1).broadcast_to([HALF, 2, EXP]),
                                            pr[:, :].unsqueeze(1).broadcast_to([HALF, 2, EXP]), ALU.mult).then_inc(phi_ready, 1)
                dve.wait_ge(w12_hi, 1)
                nc.vector.tensor_tensor(W12L[:, :, :], W12[:, :, :], W12H[:, :, :].bitcast(F32), ALU.subtract).then_inc(w12_lo, 1)
                keep_xnt(0)

                def step(b, before, after):
                    conv(b, (0, 1))
                    if not after:
                        conv(b, (2,))
                    if before:
                        dispatch_max(b)
                        combine_max(b)
                    if after:
                        conv(b, (2,))

                    def scales():
                        dispatch_scale(b)
                        combine_sum(b)

                    if after:
                        norm_in(b + 1, scales if before else None)
                    elif before:
                        dve.wait_ge(ag_ready, b * 9 + 6)
                        dve.wait_ge(silu_done, b * CT + CT)
                        dve.wait_ge(g_ready, b * CT + CT)
                        for dst, src in GATED:
                            nc.vector.tensor_tensor(AG[:, CT - 1, dst], AG[:, CT - 1, dst], CV[:, CT - 1, src], ALU.mult).then_inc(ag_ready, 1)
                        scales()
                    if before and after:
                        keep_dispatch(b)
                    norm_mid(b, before, after)
                    if before:
                        keep_xt(b)

                step(0, False, True)
                with dve.Fori(0, B // 2 - 1) as i:
                    step(i * 2 + 1, True, True)
                    step(i * 2 + 2, True, True)
                step(B - 1, True, False)

                def diagonal(g):
                    if not (isinstance(g, int) and g == 0):
                        dve.wait_ge(w_spent, unit(g - 1, 0, PAIRS - 1) * 3 + 3)
                    x = XT[:, :, :, bass.ds(g * GROUP, GROUP)]
                    for part in range(2):
                        for n, (r, s, k, at) in enumerate(((slice(0, P), 0, 0, 0), (slice(0, P), 0, 1, P + 16), (slice(0, 64), 1, 0, 2 * P), (slice(64, P), 1, 1, 2 * P + 16))):
                            src = x[r, s, :, :].rearrange("p b (q k) -> p q b k", k=2)[:, :, :, k]
                            hi = diag(r, at)
                            if part == 0:
                                nc.vector.tensor_copy(hi, src).then_inc(xp_hi, 1)
                            else:
                                dve.wait_ge(xp_hi, g * 4 + (n + 1))
                                nc.vector.tensor_tensor(diag(r, at + B), src, hi.bitcast(F32), ALU.subtract).then_inc(xp_ready, 1)

                def diag(r, at):
                    step = 3 * P + 32
                    return XPD[r, at:at + 4 * step].rearrange("p (q c) -> p q c", c=step)[:, :, 0:B]

                def low_part(g, second, p):
                    k, s = unit(g, second, p), unit_slot(g, second, p)
                    for c in range(3):
                        dve.wait_ge(hi_done, k * 3 + (c + 1))
                        cols = slice(c * CHUNK, (c + 1) * CHUNK)
                        nc.vector.tensor_tensor(low(s)[:, cols], stage(s)[:, cols], WH[:, (3 * s + c) % HIS, :].bitcast(F32), ALU.subtract).then_inc(lo_done, 1)

                def bias(g):
                    for i in range(2):
                        dve.wait_ge(t_done, g * 2 + (i + 1))
                        if i == 0:
                            wait(dve, hg_ready, g * 1)
                        src = bank(T_BANK + i)[:, 0:3 * 96].rearrange("p (j n) -> p j n", j=3)[:, :, 0:EXP]
                        for j in range(3):
                            jj = 3 * i + j
                            last = nc.vector.tensor_tensor(HB[:, jj * EXP:(jj + 1) * EXP].rearrange("p (e b) -> p e b", b=B),
                                                           src[:, j, :].rearrange("p (e b) -> p e b", b=B),
                                                           b1T[:, bass.ds(g * GROUP, GROUP), jj:jj + 1].broadcast_to([P, GROUP, B]), ALU.add)
                        last.then_inc(hb_ready, 1)

                def hidden_low(g):
                    dve.wait_ge(hh_hi, g + 1)
                    nc.vector.tensor_tensor(HH[:, :, :, 1, :].rearrange("p j e b -> p (j e) b"), HG[:, :].rearrange("p (n b) -> p n b", b=B),
                                            HH[:, :, :, 0, :].rearrange("p j e b -> p (j e) b").bitcast(F32), ALU.subtract).then_inc(hh_ready, 1)

                def group(g, after):
                    for n, (second, p) in enumerate(ORDER):
                        if isinstance(g, int) and g == 1 and n == 0:
                            combine_sum(B)
                        else:
                            low_part(g, second, p)
                        if n == 1:
                            hidden_low(g - 1)
                    if after:
                        diagonal(g + 1)
                    bias(g)

                low_part(0, 0, 0)
                dispatch_max(B)
                dispatch_scale(B)
                keep_dispatch(B)
                low_part(0, 0, 1)
                keep_xt(B)
                dve.wait_ge(xpd_zero, 1)
                dve.wait_ge(xb_used[0], used(B, 0, "turn") + 1)
                diagonal(0)
                low_part(0, 0, 2)
                low_part(0, 0, 3)
                low_part(1, 0, 0)
                combine_max(B)
                diagonal(1)
                bias(0)
                group(1, True)
                with dve.Fori(2, NG - 1) as g:
                    group(g, True)
                group(NG - 1, False)
                for p in range(PAIRS):
                    low_part(NG, 1, p)
                    if p == 0:
                        hidden_low(NG - 1)

                for p in range(PAIRS):
                    dve.wait_ge(ys_sent[p], (NG - 1) * 32)
                dve.wait_ge(last_sent, PAIRS * 32)
                nc.vector.tensor_tensor(YB[0:EXP, 0, :], YB[0:EXP, 0, :], b2e[:, :], ALU.add).then_inc(yb_ready, 1)
                for b in range(B):
                    for t in range(TILES):
                        n = b * TILES + t
                        dve.wait_ge(o_done, n + 1)
                        nc.vector.scalar_tensor_tensor(out=H[:, b, t, :], in0=bank(n % 8)[:, 0:D], scalar=RC[:, b, t:t + 1], in1=H[:, b, t, :],
                                                       op0=ALU.mult, op1=ALU.add).then_inc(o_ready, 1)


def kernel(**inputs):
    import numpy as np
    import concourse.bacc as bacc
    from concourse.bass_utils import run_bass_kernel_spmd

    def arr(name):
        return np.ascontiguousarray(inputs[name])

    x = arr("x").reshape(B, CH, GRID + 1, 8, 28, 8)
    left, right = x[..., :GRID, :], x[..., 1:, :]
    strips = np.concatenate([left, right], axis=-1)
    strips = np.ascontiguousarray(strips.transpose(0, 3, 5, 1, 2, 4)).reshape(B, P, CH, BLOCKS)
    filt = arr("L0_tok_w").reshape(D, CH, 2, 8, 16).transpose(3, 4, 1, 2, 0)
    filt = np.ascontiguousarray(filt).reshape(P, CH, 2, D)
    columns = [arr("L0_attn_conv_w").reshape(CT, P, TAPS)] + [arr(n).reshape(CT, P, 1) for n in ("L0_attn_conv_b", "L0_attn_b1", "L0_attn_b2")]
    chan = np.ascontiguousarray(np.concatenate(columns, axis=2).transpose(1, 0, 2))
    eb1 = np.ascontiguousarray(arr("L0_ffn_b1").reshape(EXP, P, KJ).transpose(1, 0, 2))
    arrays = {
        "xp": strips, "txt": arr("txt"), "wt": filt, "tb": arr("L0_tok_b"),
        "cls": arr("L0_tok_cls_token").reshape(1, D), "pos": arr("L0_tok_pos_embedding").reshape(NIMG, D),
        "w1": arr("L0_attn_W1"), "w2": arr("L0_attn_W2"), "chan": chan, "wf": arr("L0_attn_Wf"), "bf": arr("L0_attn_bf"),
        "phi": arr("L0_ffn_phi"), "scale": arr("L0_ffn_scale"), "ew1": arr("L0_ffn_w1"), "eb1": eb1,
        "ew2": arr("L0_ffn_w2"), "eb2": arr("L0_ffn_b2"),
    }
    nc = bacc.Bacc("TRN2", target_bir_lowering=False, num_devices=1)
    args = [nc.dram_tensor(f"in_{n}", a.shape, mybir.dt.from_np(a.dtype), kind="ExternalInput").ap() for n, a in arrays.items()]
    o = nc.dram_tensor("out_0", (B, SEQ, D), F32, kind="ExternalOutput").ap()
    build(nc, *args, o)
    r = run_bass_kernel_spmd(nc, [{f"in_{n}": a for n, a in arrays.items()}], core_ids=[0])
    return r.results[0]["out_0"]
```
